# Optimizing a Trainium2 kernel written in Bass

```python
import numpy as np
import jax
import jax.numpy as jnp

def _softmax(x, axis=-1):
    return jax.nn.softmax(x, axis=axis)

def _gelu(x):
    return jax.nn.gelu(x, approximate=True)

def _silu(x):
    return jax.nn.silu(x)

def _sigmoid(x):
    return jax.nn.sigmoid(x)

def _layernorm(x, axis=-1, eps=1e-05):
    m = jnp.mean(x, axis=axis, keepdims=True)
    v = jnp.var(x, axis=axis, keepdims=True)
    return (x - m) / jnp.sqrt(v + eps)

def _scatter_add(tgt, idx, src, axis=0):
    return tgt.at[idx].add(src)

def _segment_sum(src, seg, n):
    return jax.ops.segment_sum(src, seg, n)
kernel_name = 'mk_vit_tower_postln_d1_tok_img768_r4_54e686'

def setup_inputs(seed: int=0):
    np.random.seed(seed)
    _w = jnp.asarray

    def _rec_inputs():
        import jax
        import jax.numpy as jnp
        _rk = jax.random.key(seed)
        x = -0.00040386 + 0.999972 * jax.random.normal(jax.random.fold_in(_rk, 1), (8, 3, 128, 128), jnp.float32)
        return x
    x = _rec_inputs()

    def _L0_tok_setup():
        import jax, jax.numpy as jnp
        import numpy as np
        B, C, H, W = (16, 3, 128, 128)
        P = 16
        DIM = 192
        HEADS = 12
        DH = 64
        INNER = HEADS * DH
        MLP = 768
        EPS = 1e-05

        def layernorm(x, g, b):
            mu = jnp.mean(x, axis=-1, keepdims=True)
            var = jnp.var(x, axis=-1, keepdims=True)
            return (x - mu) * jax.lax.rsqrt(var + EPS) * g + b
        key = jax.random.key(seed)
        ks = jax.random.split(key, 8)
        patch_dim = C * P * P
        s = lambda d: 1.0 / np.sqrt(d)
        return {'x': jax.random.normal(ks[0], (B, C, H, W), jnp.float32), 'w_patch': jax.random.normal(ks[1], (patch_dim, DIM), jnp.float32) * s(patch_dim), 'b_patch': jnp.zeros((DIM,), jnp.float32), 'g1': jnp.ones((DIM,), jnp.float32), 'beta1': jnp.zeros((DIM,), jnp.float32), 'w_qkv': jax.random.normal(ks[2], (DIM, 3 * INNER), jnp.float32) * s(DIM), 'w_out': jax.random.normal(ks[3], (INNER, DIM), jnp.float32) * s(INNER), 'b_out': jnp.zeros((DIM,), jnp.float32), 'g2': jnp.ones((DIM,), jnp.float32), 'beta2': jnp.zeros((DIM,), jnp.float32), 'w_ff1': jax.random.normal(ks[4], (DIM, MLP), jnp.float32) * s(DIM), 'b_ff1': jnp.zeros((MLP,), jnp.float32), 'w_ff2': jax.random.normal(ks[5], (MLP, DIM), jnp.float32) * s(MLP), 'b_ff2': jnp.zeros((DIM,), jnp.float32)}
    _L0_tok_all = _L0_tok_setup()
    _L0_tok_in = {k: v for k, v in _L0_tok_all.items() if k in ('w_patch', 'b_patch', 'g1', 'beta1', 'w_qkv', 'w_out', 'b_out', 'g2', 'beta2', 'w_ff1', 'b_ff1', 'w_ff2', 'b_ff2')}
    del _L0_tok_all

    def _L0_attn_setup():
        import jax, jax.numpy as jnp
        import numpy as np
        NUM_HEADS = 12
        Q_BITS = 8

        def fake_quant(x, bits=Q_BITS):
            qmax = 2.0 ** (bits - 1) - 1.0
            scale = jnp.maximum(jnp.max(jnp.abs(x)) / qmax, 1e-08)
            q = jnp.clip(jnp.round(x / scale), -qmax - 1.0, qmax) * scale
            return x + jax.lax.stop_gradient(q - x)
        key = jax.random.key(seed)
        ks = jax.random.split(key, 5)
        B, N, C = (8, 256, 192)
        x = jax.random.normal(ks[0], (B, N, C), dtype=jnp.float32)
        w_qkv = jax.random.normal(ks[1], (C, 3 * C), dtype=jnp.float32) * 0.02
        b_qkv = jax.random.normal(ks[2], (3 * C,), dtype=jnp.float32) * 0.02
        w_proj = jax.random.normal(ks[3], (C, C), dtype=jnp.float32) * 0.02
        b_proj = jax.random.normal(ks[4], (C,), dtype=jnp.float32) * 0.02
        return {'x': x, 'w_qkv': w_qkv, 'b_qkv': b_qkv, 'w_proj': w_proj, 'b_proj': b_proj}
    _L0_attn_all = _L0_attn_setup()
    _L0_attn_in = {k: v for k, v in _L0_attn_all.items() if k in ('w_qkv', 'b_qkv', 'w_proj', 'b_proj')}
    del _L0_attn_all

    def _L0_ffn_setup():
        import jax, jax.numpy as jnp
        import numpy as np
        B, L, D, H, F = (4, 512, 192, 12, 768)
        ROUTE_FRAC = 0.15
        LN_EPS = 1e-05

        def _ln(x, g, b):
            m = jnp.mean(x, axis=-1, keepdims=True)
            v = jnp.mean((x - m) ** 2, axis=-1, keepdims=True)
            return (x - m) * jax.lax.rsqrt(v + LN_EPS) * g + b
        key = jax.random.key(seed)
        ks = jax.random.split(key, 20)
        s = 0.02
        return {'hidden_states': jax.random.normal(ks[0], (B, L, D), dtype=jnp.float32), 'g1': jnp.ones((D,), jnp.float32), 'b1': jnp.zeros((D,), jnp.float32), 'g2': jnp.ones((D,), jnp.float32), 'b2': jnp.zeros((D,), jnp.float32), 'Wr': jax.random.normal(ks[1], (D,), jnp.float32) * s, 'br': jnp.zeros((), jnp.float32), 'Wq': jax.random.normal(ks[2], (D, D), jnp.float32) * s, 'bq': jnp.zeros((D,), jnp.float32), 'Wk': jax.random.normal(ks[3], (D, D), jnp.float32) * s, 'bk': jnp.zeros((D,), jnp.float32), 'Wv': jax.random.normal(ks[4], (D, D), jnp.float32) * s, 'bv': jnp.zeros((D,), jnp.float32), 'Wo': jax.random.normal(ks[5], (D, D), jnp.float32) * s, 'bo': jnp.zeros((D,), jnp.float32), 'Wm': jax.random.normal(ks[6], (D, D), jnp.float32) * s, 'bm': jnp.zeros((D,), jnp.float32), 'W1': jax.random.normal(ks[7], (D, F), jnp.float32) * s, 'bf1': jnp.zeros((F,), jnp.float32), 'W2': jax.random.normal(ks[8], (F, D), jnp.float32) * s, 'bf2': jnp.zeros((D,), jnp.float32)}
    _L0_ffn_all = _L0_ffn_setup()
    _L0_ffn_in = {k: v for k, v in _L0_ffn_all.items() if k in ('g1', 'b1', 'g2', 'b2', 'Wr', 'br', 'Wq', 'bq', 'Wk', 'bk', 'Wv', 'bv', 'Wo', 'bo', 'Wm', 'bm', 'W1', 'bf1', 'W2', 'bf2')}
    del _L0_ffn_all
    return {'x': x, 'L0_tok_w_patch': _L0_tok_in['w_patch'], 'L0_tok_b_patch': _L0_tok_in['b_patch'], 'L0_tok_g1': _L0_tok_in['g1'], 'L0_tok_beta1': _L0_tok_in['beta1'], 'L0_tok_w_qkv': _L0_tok_in['w_qkv'], 'L0_tok_w_out': _L0_tok_in['w_out'], 'L0_tok_b_out': _L0_tok_in['b_out'], 'L0_tok_g2': _L0_tok_in['g2'], 'L0_tok_beta2': _L0_tok_in['beta2'], 'L0_tok_w_ff1': _L0_tok_in['w_ff1'], 'L0_tok_b_ff1': _L0_tok_in['b_ff1'], 'L0_tok_w_ff2': _L0_tok_in['w_ff2'], 'L0_tok_b_ff2': _L0_tok_in['b_ff2'], 'L0_attn_w_qkv': _L0_attn_in['w_qkv'], 'L0_attn_b_qkv': _L0_attn_in['b_qkv'], 'L0_attn_w_proj': _L0_attn_in['w_proj'], 'L0_attn_b_proj': _L0_attn_in['b_proj'], 'L0_ffn_g1': _L0_ffn_in['g1'], 'L0_ffn_b1': _L0_ffn_in['b1'], 'L0_ffn_g2': _L0_ffn_in['g2'], 'L0_ffn_b2': _L0_ffn_in['b2'], 'L0_ffn_Wr': _L0_ffn_in['Wr'], 'L0_ffn_br': _L0_ffn_in['br'], 'L0_ffn_Wq': _L0_ffn_in['Wq'], 'L0_ffn_bq': _L0_ffn_in['bq'], 'L0_ffn_Wk': _L0_ffn_in['Wk'], 'L0_ffn_bk': _L0_ffn_in['bk'], 'L0_ffn_Wv': _L0_ffn_in['Wv'], 'L0_ffn_bv': _L0_ffn_in['bv'], 'L0_ffn_Wo': _L0_ffn_in['Wo'], 'L0_ffn_bo': _L0_ffn_in['bo'], 'L0_ffn_Wm': _L0_ffn_in['Wm'], 'L0_ffn_bm': _L0_ffn_in['bm'], 'L0_ffn_W1': _L0_ffn_in['W1'], 'L0_ffn_bf1': _L0_ffn_in['bf1'], 'L0_ffn_W2': _L0_ffn_in['W2'], 'L0_ffn_bf2': _L0_ffn_in['bf2']}

def reference(x, L0_tok_w_patch, L0_tok_b_patch, L0_tok_g1, L0_tok_beta1, L0_tok_w_qkv, L0_tok_w_out, L0_tok_b_out, L0_tok_g2, L0_tok_beta2, L0_tok_w_ff1, L0_tok_b_ff1, L0_tok_w_ff2, L0_tok_b_ff2, L0_attn_w_qkv, L0_attn_b_qkv, L0_attn_w_proj, L0_attn_b_proj, L0_ffn_g1, L0_ffn_b1, L0_ffn_g2, L0_ffn_b2, L0_ffn_Wr, L0_ffn_br, L0_ffn_Wq, L0_ffn_bq, L0_ffn_Wk, L0_ffn_bk, L0_ffn_Wv, L0_ffn_bv, L0_ffn_Wo, L0_ffn_bo, L0_ffn_Wm, L0_ffn_bm, L0_ffn_W1, L0_ffn_bf1, L0_ffn_W2, L0_ffn_bf2):
    import jax
    import jax.numpy as jnp

    def _L0_tok_ref(x, w_patch, b_patch, g1, beta1, w_qkv, w_out, b_out, g2, beta2, w_ff1, b_ff1, w_ff2, b_ff2):
        import jax, jax.numpy as jnp
        import numpy as np
        B, C, H, W = (16, 3, 128, 128)
        P = 16
        DIM = 192
        HEADS = 12
        DH = 64
        INNER = HEADS * DH
        MLP = 768
        EPS = 1e-05

        def layernorm(x, g, b):
            mu = jnp.mean(x, axis=-1, keepdims=True)
            var = jnp.var(x, axis=-1, keepdims=True)
            return (x - mu) * jax.lax.rsqrt(var + EPS) * g + b
        b = x.shape[0]
        hp, wp = (H // P, W // P)
        xp = x.reshape(b, C, hp, P, wp, P)
        xp = xp.transpose(0, 2, 4, 3, 5, 1).reshape(b, hp * wp, P * P * C)
        t = xp @ w_patch + b_patch
        h = layernorm(t, g1, beta1)
        qkv = h @ w_qkv
        q, k, v = jnp.split(qkv, 3, axis=-1)
        split_heads = lambda z: z.reshape(b, -1, HEADS, DH).transpose(0, 2, 1, 3)
        q, k, v = map(split_heads, (q, k, v))
        scale = DH ** (-0.5)
        dots = jnp.einsum('bhid,bhjd->bhij', q, k) * scale
        attn = jax.nn.softmax(dots, axis=-1)
        o = jnp.einsum('bhij,bhjd->bhid', attn, v)
        o = o.transpose(0, 2, 1, 3).reshape(b, -1, INNER)
        t = o @ w_out + b_out + t
        h = layernorm(t, g2, beta2)
        h = jax.nn.gelu(h @ w_ff1 + b_ff1, approximate=False)
        t = h @ w_ff2 + b_ff2 + t
        return t

    def _L0_attn_ref(x, w_qkv, b_qkv, w_proj, b_proj):
        import jax, jax.numpy as jnp
        import numpy as np
        NUM_HEADS = 12
        Q_BITS = 8

        def fake_quant(x, bits=Q_BITS):
            qmax = 2.0 ** (bits - 1) - 1.0
            scale = jnp.maximum(jnp.max(jnp.abs(x)) / qmax, 1e-08)
            q = jnp.clip(jnp.round(x / scale), -qmax - 1.0, qmax) * scale
            return x + jax.lax.stop_gradient(q - x)
        B, N, C = x.shape
        H = NUM_HEADS
        hd = C // H
        scale = hd ** (-0.5)
        qkv = fake_quant(x) @ fake_quant(w_qkv) + b_qkv
        qkv = qkv.reshape(B, N, 3, H, hd).transpose(2, 0, 3, 1, 4)
        q, k, v = (qkv[0], qkv[1], qkv[2])
        attn = jnp.einsum('bhnd,bhmd->bhnm', fake_quant(q), fake_quant(k))
        attn = attn * scale
        attn = fake_quant(jax.nn.softmax(attn, axis=-1))
        out = jnp.einsum('bhnm,bhmd->bhnd', attn, fake_quant(v))
        out = out.transpose(0, 2, 1, 3).reshape(B, N, C)
        out = fake_quant(out) @ fake_quant(w_proj) + b_proj
        return out

    def _L0_ffn_ref(hidden_states, g1, b1, g2, b2, Wr, br, Wq, bq, Wk, bk, Wv, bv, Wo, bo, Wm, bm, W1, bf1, W2, bf2):
        import jax, jax.numpy as jnp
        import numpy as np
        B, L, D, H, F = (4, 512, 192, 12, 768)
        ROUTE_FRAC = 0.15
        LN_EPS = 1e-05

        def _ln(x, g, b):
            m = jnp.mean(x, axis=-1, keepdims=True)
            v = jnp.mean((x - m) ** 2, axis=-1, keepdims=True)
            return (x - m) * jax.lax.rsqrt(v + LN_EPS) * g + b
        b, l, d = hidden_states.shape
        dh = d // H
        normed = _ln(hidden_states, g1, b1)
        scores = jax.nn.sigmoid(jnp.einsum('bld,d->bl', normed, Wr) + br)
        k = max(1, int(round(ROUTE_FRAC * l)))
        _, idx = jax.lax.top_k(-scores, k)
        attn_mask = jnp.zeros((b, l), bool).at[jnp.arange(b)[:, None], idx].set(True)
        q = (normed @ Wq + bq).reshape(b, l, H, dh)
        kk = (normed @ Wk + bk).reshape(b, l, H, dh)
        v = (normed @ Wv + bv).reshape(b, l, H, dh)
        logits = jnp.einsum('blhd,bmhd->bhlm', q, kk) / jnp.sqrt(jnp.float32(dh))
        probs = jax.nn.softmax(logits, axis=-1)
        ctx = jnp.einsum('bhlm,bmhd->blhd', probs, v).reshape(b, l, d)
        attn_out = ctx @ Wo + bo
        w = scores / (jnp.sum(scores, axis=1, keepdims=True) + 1e-06)
        pooled = jnp.einsum('bl,bld->bd', w, normed)
        mix_out = (normed + scores[..., None] * pooled[:, None, :]) @ Wm + bm
        merged = jnp.where(attn_mask[..., None], attn_out, mix_out)
        h = hidden_states + merged
        n2 = _ln(h, g2, b2)
        ffn = jax.nn.gelu(n2 @ W1 + bf1, approximate=False) @ W2 + bf2
        return h + ffn
    h = _L0_tok_ref(x, L0_tok_w_patch, L0_tok_b_patch, L0_tok_g1, L0_tok_beta1, L0_tok_w_qkv, L0_tok_w_out, L0_tok_b_out, L0_tok_g2, L0_tok_beta2, L0_tok_w_ff1, L0_tok_b_ff1, L0_tok_w_ff2, L0_tok_b_ff2)
    h = _layernorm(h + _L0_attn_ref(h, L0_attn_w_qkv, L0_attn_b_qkv, L0_attn_w_proj, L0_attn_b_proj), axis=-1)
    h = _layernorm(h + _L0_ffn_ref(h, L0_ffn_g1, L0_ffn_b1, L0_ffn_g2, L0_ffn_b2, L0_ffn_Wr, L0_ffn_br, L0_ffn_Wq, L0_ffn_bq, L0_ffn_Wk, L0_ffn_bk, L0_ffn_Wv, L0_ffn_bv, L0_ffn_Wo, L0_ffn_bo, L0_ffn_Wm, L0_ffn_bm, L0_ffn_W1, L0_ffn_bf1, L0_ffn_W2, L0_ffn_bf2), axis=-1)
    return h

_drawn_inputs = setup_inputs


def setup_inputs(seed=0):
    import zlib

    import numpy as np

    out = dict(_drawn_inputs(seed))
    spreads = {'L0_tok_b_patch': (0.0, 0.1),
     'L0_tok_g1': (1.0, 0.2),
     'L0_tok_beta1': (0.0, 0.1),
     'L0_tok_b_out': (0.0, 0.1),
     'L0_tok_g2': (1.0, 0.2),
     'L0_tok_beta2': (0.0, 0.1),
     'L0_tok_b_ff1': (0.0, 0.1),
     'L0_tok_b_ff2': (0.0, 0.1),
     'L0_ffn_g1': (1.0, 0.2),
     'L0_ffn_b1': (0.0, 0.428),
     'L0_ffn_g2': (1.0, 0.6),
     'L0_ffn_b2': (0.0, 0.8),
     'L0_ffn_bq': (0.0, 0.8),
     'L0_ffn_bk': (0.0, 0.8),
     'L0_ffn_bv': (0.0, 0.8),
     'L0_ffn_bo': (0.0, 0.392),
     'L0_ffn_bm': (0.0, 0.1),
     'L0_ffn_bf1': (0.0, 0.518),
     'L0_ffn_bf2': (0.0, 0.1)}
    factors = {'L0_attn_b_qkv': 8.0,
     'L0_attn_b_proj': 3.672,
     'L0_ffn_Wq': 8.0,
     'L0_ffn_Wk': 8.0,
     'L0_ffn_Wv': 8.0,
     'L0_ffn_Wo': 7.203}
    for name, (base, spread) in spreads.items():
        noise = np.random.default_rng([zlib.crc32(name.encode()), seed]).standard_normal(out[name].shape)
        drawn = base * np.exp(spread * noise) if base else spread * noise
        out[name] = jnp.asarray(drawn.astype(out[name].dtype))
    for name, factor in factors.items():
        out[name] = (out[name] * factor).astype(out[name].dtype)
    return out
```

```python
import concourse.bass as bass
import numpy as np
from concourse import mybir
from contextlib import ExitStack

IMAGES, CHANNELS, SIDE, PATCH = 8, 3, 128, 16
GRID = SIDE // PATCH
TOKENS = GRID * GRID
ALL = IMAGES * TOKENS
TILE = 128
PER_TILE = TILE // TOKENS
TILES = ALL // TILE
DIM = 192
HALF = DIM // 2
PATCH_DIM = CHANNELS * PATCH * PATCH
PATCH_CHUNKS = PATCH_DIM // 128
HEADS = 12
HEAD1 = 64
INNER = HEADS * HEAD1
INNER_CHUNKS = INNER // 128
HEAD = DIM // HEADS
CHUNK_HEADS = HEADS // 2
PAD = 32
MLP = 768
MLP_CHUNKS = MLP // 128
PICKED = max(1, int(round(0.15 * TOKENS)))
ALL_PICKED = IMAGES * PICKED
HEAD_ROWS = 64
EPS = 1e-5
QMAX = 127.0
ROUND = 12582912.0

ROWS = ["b_patch", "b_out", "b_ff2", "bv2", "b_proj", "g1", "b1", "bo", "bm", "bf2"]
COLS = ["g1", "beta1", "g2", "beta2", "bq2", "bk2", "bq3", "bk3", "ffn_g1", "ffn_b1", "ffn_g2", "ffn_b2"]
CONSTS = {"same": 128, "before": 128, "pick": TILES * ALL_PICKED, "head": CHUNK_HEADS}


def const_at(name):
    at = 0
    for n, width in CONSTS.items():
        if n == name:
            return at, at + width
        at += width
    return 0, at


def vit_kernel(nc, A, out):
    f32, bf16 = mybir.dt.float32, mybir.dt.bfloat16
    ALU, ACT, X = mybir.AluOpType, mybir.ActivationFunctionType, mybir.AxisListType.X
    ctx = ExitStack()
    with ctx:
        (PATCHES, QKV, ATTEND, OUT, FF, QUANT, SCORES2, ATTEND2, PROJ, ROUTE, ATTEND3, FF3, END) = range(13)
        ALWAYS = (PATCHES, END)
        floor, ceiling = (nc.sbuf_base + 31) // 32 * 32, nc.sbuf_top
        placed = []

        def sb(name, shape, life, dtype=f32):
            width = int(np.prod(shape[1:])) * (2 if dtype == bf16 else 4)
            width = (width + 31) // 32 * 32
            at = floor
            for start, end, first, last in sorted(placed):
                if first <= life[1] and life[0] <= last and start < at + width and at < end:
                    at = end
            assert at + width <= ceiling, (name, at + width, ceiling)
            placed.append((at, at + width, *life))
            return nc.alloc_sbuf_tensor_at(name, shape, dtype, offset=at)

        def sem(name):
            return ctx.enter_context(nc.semaphore(name))

        stats = sb("stats", [128, TILES, 6], ALWAYS)
        mv = sb("mv", [128, TILES, 2], ALWAYS)
        var_eps = sb("var_eps", [128, TILES], ALWAYS)
        rstd = sb("rstd", [128, TILES], ALWAYS)
        power = sb("power", [128, TILES], ALWAYS)
        round_bias = sb("round_bias", [128, 1], ALWAYS)
        spread = sb("spread", [128, 3, 128], ALWAYS)
        gm = sb("gm", [128, 3], ALWAYS)
        mx1, sum1, inv1, mx2, sum2, inv2, f2 = (sb(n, [128, TILES, HEADS], ALWAYS) for n in
                                                ("mx1", "sum1", "inv1", "mx2", "sum2", "inv2", "f2"))
        mx3, sum3, inv3 = (sb(n, [128, IMAGES], ALWAYS) for n in ("mx3", "sum3", "inv3"))
        wmax, wscale, winv = (sb(n, [128, 2], ALWAYS) for n in ("wmax", "wscale", "winv"))
        hmax = sb("hmax", [128, TILES + 1], ALWAYS)
        hs = sb("hs", [128, 3], ALWAYS)
        qmax_parts = sb("qmax_parts", [128, 4], ALWAYS)
        qmax, qs, qinv = (sb(n, [128, 3], ALWAYS) for n in ("qmax", "qs", "qinv"))
        slog = sb("slog", [128, 1], ALWAYS)
        pmax = sb("pmax", [128, 1], ALWAYS)
        ps_ = sb("ps_", [128, 2], ALWAYS)
        omax_parts = sb("omax_parts", [128, 4], ALWAYS)
        omax = sb("omax", [128, 1], ALWAYS)
        os_ = sb("os_", [128, 5], ALWAYS)
        (eneg, eneg1, score, less, tie, total, total_e, total_i, rank, rest, weight) = (
            sb(n, [128, TILES], ALWAYS) for n in
            ("eneg", "eneg1", "score", "less", "tie", "total", "total_e", "total_i", "rank", "rest", "weight"))

        ident = sb("ident", [128, 128], ALWAYS)
        ident_b = sb("ident_b", [128, 128], (PATCHES, ATTEND2), bf16)
        consts = sb("consts", [128, const_at("")[1]], (PATCHES, ATTEND3))
        rows = sb("rows", [128, len(ROWS), DIM], ALWAYS)
        cols = sb("cols", [HALF, len(COLS), 2], ALWAYS)
        cols_ff = sb("cols_ff", [128, 2, MLP_CHUNKS], ALWAYS)
        row_v3 = sb("row_v3", [128, DIM + 2], (PATCHES, ROUTE))
        W1 = sb("W1", [HALF, 2, MLP], ALWAYS)
        W2 = sb("W2", [128, MLP_CHUNKS, DIM], ALWAYS)
        w_ffn = sb("w_ffn", [HALF, 4, 2, DIM], (PATCHES, ATTEND3))
        w_v3 = sb("w_v3", [HALF, 2, DIM + 2], (PATCHES, ROUTE))
        w_ff1 = sb("w_ff1", [HALF, 2, MLP], (PATCHES, FF))
        w_ff2 = sb("w_ff2", [128, MLP_CHUNKS, DIM], (PATCHES, FF))
        w_out = sb("w_out", [128, INNER_CHUNKS, DIM], (PATCHES, OUT))
        w_qkv2 = sb("w_qkv2", [HALF, 2, 3 * DIM], (PATCHES, OUT))
        w_proj = sb("w_proj", [128, 3, DIM], (PATCHES, OUT))
        w_qkv = sb("w_qkv", [HALF, 2, 3 * INNER], (PATCHES, ATTEND))
        xT = sb("xT", [128, TILES, PATCH_CHUNKS, TILE], (PATCHES, PATCHES))
        w_patch = sb("w_patch", [128, PATCH_CHUNKS, DIM], (PATCHES, PATCHES))

        def const(name):
            a, b = const_at(name)
            return consts[:, a:b]

        def row(name):
            return rows[:, ROWS.index(name), :]

        def col(name, chunk):
            return cols[:, COLS.index(name), chunk:chunk + 1]

        same, before = const("same"), const("before")
        pick_at = const("pick").rearrange("p (t n) -> p t n", t=TILES)
        head_mask = const("head")[0:HALF, :]

        xhat = sb("xhat", [128, TILES, DIM], ALWAYS)
        t1 = sb("t1", [128, TILES, DIM], (PATCHES, OUT))
        t1b = sb("t1b", [128, TILES, DIM], (QKV, OUT))
        hT = sb("hT", [HALF, 2, ALL], (QKV, ATTEND))
        qkT = sb("qkT", [128, 2 * INNER_CHUNKS, ALL], (QKV, ATTEND))
        v1 = sb("v1", [128, TILES, INNER], (QKV, OUT))
        p1 = sb("p1", [128, TILES, 2, 6, TOKENS], (QKV, OUT))
        pT1 = sb("pT1", [128, TILES, 2, 3, 128], (ATTEND, OUT))
        oT1 = sb("oT1", [128, INNER_CHUNKS, TILES, PER_TILE, TOKENS], (ATTEND, OUT))
        t2 = sb("t2", [128, TILES, DIM], (OUT, FF))
        t2b = sb("t2b", [128, TILES, DIM], (OUT, FF))
        h2T = sb("h2T", [HALF, 2, ALL], (OUT, FF))
        ff = sb("ff", [128, MLP_CHUNKS, ALL], (FF, FF))
        h1 = sb("h1", [128, TILES, DIM], (FF, PROJ))
        h1b = sb("h1b", [128, TILES, DIM], (QUANT, PROJ))

        wqkv_r = sb("wqkv_r", [HALF, 2, 3 * DIM], (QKV, FF))
        wqkv_q = sb("wqkv_q", [HALF, 2, 3 * DIM], (QKV, QUANT), bf16)
        wproj_r = sb("wproj_r", [128, 3, DIM], (QKV, FF))
        wproj_q = sb("wproj_q", [128, 3, DIM], (QKV, PROJ), bf16)
        hr = sb("hr", [128, TILES, DIM], (QUANT, QUANT))
        hq = sb("hq", [HALF, 2, ALL], (QUANT, QUANT), bf16)
        qk2 = sb("qk2", [HALF, 4, ALL], (QUANT, SCORES2))
        v2 = sb("v2", [128, TILES, DIM], (QUANT, ATTEND2))
        qk_r = sb("qk_r", [HALF, 4, ALL], (QUANT, SCORES2))
        q_q = sb("q_q", [HALF, 2, ALL], (QUANT, SCORES2), bf16)
        k_q = sb("k_q", [HALF, 2, ALL], (QUANT, SCORES2), bf16)
        k_heads = sb("k_heads", [HALF, CHUNK_HEADS, 2, ALL], (QUANT, SCORES2), bf16)
        v_r = sb("v_r", [128, TILES, DIM], (SCORES2, ATTEND2))
        v_q = sb("v_q", [128, TILES, HEADS, PAD], (QUANT, ATTEND2), bf16)
        q3h = sb("q3h", [HALF, 2, IMAGES, HEAD_ROWS], (QUANT, ATTEND3))
        e2 = sb("e2", [128, TILES, CHUNK_HEADS, PER_TILE, TOKENS], (SCORES2, ATTEND2))
        p2 = sb("p2", [128, TILES, CHUNK_HEADS, PER_TILE * TOKENS], (ATTEND2, ATTEND2))
        p2q = sb("p2q", [128, TILES, CHUNK_HEADS, PER_TILE * TOKENS], (ATTEND2, ATTEND2), bf16)
        pT2 = sb("pT2", [128, TILES, CHUNK_HEADS, 128], (ATTEND2, ATTEND2), bf16)
        o_r = sb("o_r", [128, 3, TILES, PER_TILE, TOKENS], (ATTEND2, PROJ))
        o_q = sb("o_q", [128, 3, TILES, PER_TILE, TOKENS], (ATTEND2, PROJ), bf16)

        zpre = sb("zpre", [128, TILES, DIM], (PROJ, PROJ))
        z = sb("z", [128, TILES, DIM], (PROJ, END))
        zb = sb("zb", [128, TILES, DIM], (PROJ, END))
        nh = sb("nh", [128, TILES, DIM], (PROJ, ROUTE))
        ng = sb("ng", [128, TILES, DIM], (PROJ, ROUTE))
        n3 = sb("n3", [128, TILES, DIM], (PROJ, ATTEND3))
        nT = sb("nT", [HALF, 2, ALL], (PROJ, ATTEND3))
        score_b = sb("score_b", [128, TILES, 128], (ROUTE, ROUTE))
        below = sb("below", [128, TILES, 128], (ROUTE, ROUTE))
        equal = sb("equal", [128, TILES, 128], (ROUTE, ROUTE))
        sTm = sb("sTm", [128, TILES, 128], (ROUTE, ROUTE))
        mixer = sb("mixer", [128, TILES, 128], (ROUTE, ATTEND3))
        picked = sb("picked", [128, TILES, ALL_PICKED], (ROUTE, ATTEND3))
        pickedT = sb("pickedT", [ALL_PICKED, ALL], (ROUTE, ATTEND3))
        mixT = sb("mixT", [HALF, 2, ALL], (ROUTE, ATTEND3))
        nselT = sb("nselT", [HALF, 2, ALL_PICKED], (ROUTE, ATTEND3))
        q3 = sb("q3", [HALF, 2, IMAGES, PICKED], (ROUTE, ATTEND3))
        k3 = sb("k3", [HALF, 2, ALL], (ROUTE, ATTEND3))
        v3 = sb("v3", [128, TILES, DIM + 2], (ROUTE, ATTEND3))
        p3 = sb("p3", [128, IMAGES, TOKENS], (ATTEND3, ATTEND3))
        pT3 = sb("pT3", [128, TILES, 128], (ATTEND3, ATTEND3))
        o3m = sb("o3m", [HALF, PER_TILE, 2 * TILES, CHUNK_HEADS * PICKED], (ATTEND3, ATTEND3))
        o3T = sb("o3T", [HALF, 2, PER_TILE, TILES, PICKED], (ATTEND3, ATTEND3))
        a3 = sb("a3", [ALL_PICKED, DIM], (ATTEND3, ATTEND3))
        mixb = sb("mixb", [128, TILES, DIM], (ATTEND3, ATTEND3))
        mixz = sb("mixz", [128, TILES, DIM], (ATTEND3, ATTEND3))
        h4 = sb("h4", [128, TILES, DIM], (ATTEND3, END))
        h4z = sb("h4z", [128, TILES, DIM], (ATTEND3, END))
        h5T = sb("h5T", [HALF, 2, ALL], (FF3, END))
        ff3 = sb("ff3", [128, MLP_CHUNKS, ALL], (FF3, END))
        ypre = sb("ypre", [128, TILES, DIM], (END, END))
        y = sb("y", [128, TILES, DIM], (END, END))

        pairs = [ctx.enter_context(nc.psum_tensor(f"pair{i}", [128, 2, 512], f32)) for i in range(4)]

        def bank(i):
            return pairs[i // 2][:, i % 2, :]

        def split_chunks(ap):
            return ap[0:HALF, 0:2 * TILE].rearrange("p (c n) -> p c n", c=2)

        def tokens(t):
            return slice(t * TILE, (t + 1) * TILE)

        def image(t, i):
            return slice((PER_TILE * t + i) * TOKENS, (PER_TILE * t + i + 1) * TOKENS)

        def place1(h):
            chunk, r = h // 2, h % 2
            return r, (chunk + r) % 2, chunk // 2

        ld_x = [sem(f"ld_x{t}") for t in range(TILES)]
        ld_x0 = [sem(f"ld_x0_{g}") for g in range(3)]
        ld_wp = [sem(f"ld_wp{g}") for g in range(3)]
        ld = {n: sem("ld_" + n) for n in ("ident", "const", "rows", "rows_tok", "row0", "cols", "cols_ff", "w_qk", "w_v", "w_out", "w_ff1", "w_ff2",
                                          "w_qkv2", "w_proj", "w_ffn", "W1", "W2")}
        pe = {n: sem("pe_" + n) for n in (
            "patch", "xhatT", "qk", "scores", "v", "pT", "o", "out", "x2T", "ff1", "ff2", "wide",
            "hT", "qk2", "v2", "scores2", "pT2", "o2", "proj", "scoreT", "nT", "k3", "v3", "mixT", "nsel",
            "pickT", "q3", "mix", "scores3", "pT3", "o3", "a3", "spread", "x4T", "W1", "W2")}
        mk = {n: sem("mk_" + n) for n in (
            "t1", "var", "rstd", "xhat", "hT", "qk", "sub", "exp", "p", "v", "pT", "oT", "t2", "h2T", "gelu", "h1",
            "spread", "scale", "wscale", "t1b", "t2b", "wq", "hr", "hq", "qk2", "v2", "qkr", "qq", "kq", "kd", "ka",
            "or", "vr", "vq", "sub2", "exp2", "p2", "pT2", "oq", "h1b", "zpre", "z", "nh", "n3", "eneg", "score_b", "mixer",
            "picked", "nT", "k3", "v3", "mixT", "nselT", "pickT", "q3h", "sub3", "exp3", "p3", "pT3", "o3T", "a3",
            "mixz", "h4", "zb", "h4z", "h5T", "gelu3", "ypre", "y", "zero", "identb", "cmp")}
        dve_step, act_step, pool_step = sem("dve_step"), sem("act_step"), sem("pool_step")
        stored = sem("stored")

        GROUPS = [[0], [1], [2], [3], [0, 1], [2, 3], [0, 1, 2, 3], [0, 1, 2, 3], [0, 1], [2, 3], [0], [1], [2], [3]]
        LN1, LN2, LNZ, LNN, LN4, LNY = 0, 4, 6, 7, 8, 10
        MAX_W, MAX_H, MAX_QKV, MAX_P, MAX_O = range(5)
        MAX_WIDTH = [2, 1, 3, 1, 1]
        V_PAIR = [0, 1, 1, 2]
        OUT_BANK = [6, 7, 4, 5]

        block = ctx.enter_context(nc.Block())

        @block.sync
        def _(sp):
            third = PATCH_CHUNKS // 3
            for g in range(3):
                cc = slice(g * third, (g + 1) * third)
                sp.dma_start(w_patch[:, cc], A["w_patch"][:, cc]).then_inc(ld_wp[g], 16)
                sp.dma_start(xT[:, 0, cc], A["xT"][:, 0, cc]).then_inc(ld_x0[g], 16)
            for t in range(1, TILES):
                sp.dma_start(xT[:, t], A["xT"][:, t]).then_inc(ld_x[t], 16)
                if t == 1:
                    sp.dma_start(ident[:], A["ident"]).then_inc(ld["ident"], 16)
            for m in range(2):
                half = slice(m * INNER, (m + 1) * INNER)
                sp.dma_start(w_qkv[:, :, half], A["w_qkv"][:, :, half]).then_inc(ld["w_qk"], 16)
            sp.dma_start(w_qkv[:, :, 2 * INNER:3 * INNER], A["w_qkv"][:, :, 2 * INNER:3 * INNER]).then_inc(ld["w_v"], 16)
            sp.dma_start(w_qkv2[:], A["w_qkv2"]).then_inc(ld["w_qkv2"], 16)
            sp.wait_ge(mk["zero"], 1)
            for r in range(4):
                sp.dma_start(w_proj[PAD * r:PAD * r + HEAD], A["w_proj"][r]).then_inc(ld["w_proj"], 16)
            sp.dma_start(consts[:], A["consts"]).then_inc(ld["const"], 16)
            sp.dma_start(cols_ff[:], A["cols_ff"]).then_inc(ld["cols_ff"], 16)
            sp.dma_start(rows[:, 1:3], A["rows"][1:3].rearrange("(a r) n -> a r n", a=1)
                         .to_broadcast([128, 2, DIM])).then_inc(ld["rows_tok"], 16)
            sp.dma_start(w_out[:], A["w_out"]).then_inc(ld["w_out"], 16)
            sp.dma_start(w_ff1[:], A["w_ff1"]).then_inc(ld["w_ff1"], 16)
            sp.dma_start(w_ff2[:], A["w_ff2"]).then_inc(ld["w_ff2"], 16)
            sp.dma_start(rows[:, 3:], A["rows"][3:].rearrange("(a r) n -> a r n", a=1)
                         .to_broadcast([128, len(ROWS) - 3, DIM])).then_inc(ld["rows"], 16)
            sp.dma_start(row_v3[:], A["row_v3"].to_broadcast([128, DIM + 2])).then_inc(ld["rows"], 16)
            sp.dma_start(w_v3[:], A["w_v3"]).then_inc(ld["w_ffn"], 16)
            sp.dma_start(w_ffn[:], A["w_ffn"]).then_inc(ld["w_ffn"], 16)
            sp.dma_start(W1[:], A["W1"]).then_inc(ld["W1"], 16)
            sp.dma_start(W2[:], A["W2"]).then_inc(ld["W2"], 16)
            for t in range(TILES):
                sp.wait_ge(mk["y"], t + 1)
                sp.dma_start(out[tokens(t), :], y[:, t]).then_inc(stored, 16)
            sp.wait_ge(stored, 16 * TILES)

        @block.tensor
        def _(te):
            mm = nc.tensor.matmul

            def turn(dst, src, parts):
                return nc.tensor.transpose(dst, src, ident[0:parts, 0:parts])

            def turn_tile(src, t, where):
                for c in range(2):
                    last = turn(bank(where)[0:HALF, c * TILE:(c + 1) * TILE],
                                src[:, t, c * HALF:(c + 1) * HALF], 128)
                return last

            def turn_spread(nth, where):
                te.wait_ge(mk["spread"], nth + 1)
                for k in range(MAX_WIDTH[nth]):
                    last = turn(bank(where)[:, k * 128:(k + 1) * 128], spread[:, k, :], 128)
                last.then_inc(pe["wide"], 1)

            for t in range(TILES):
                if t > 0:
                    te.wait_ge(ld_x[t], 16)
                for c in range(PATCH_CHUNKS):
                    if t == 0 and c % 2 == 0:
                        te.wait_ge(ld_wp[c // 2], 16)
                        te.wait_ge(ld_x0[c // 2], 16)
                    last = mm(bank(t)[:, 0:DIM], xT[:, t, c, :], w_patch[:, c, :],
                              start=(c == 0), stop=(c == PATCH_CHUNKS - 1))
                last.then_inc(pe["patch"], 1)
            te.wait_ge(ld["ident"], 16)
            for t in range(TILES):
                te.wait_ge(mk["xhat"], t + 1)
                turn_tile(xhat, t, 4 + t).then_inc(pe["xhatT"], 1)

            def project_qk(half):
                te.wait_ge(mk["hT"], 2 * half + 2)
                for m in range(2 * INNER_CHUNKS):
                    n = half * 2 * INNER_CHUNKS + m
                    if n >= 4:
                        te.wait_ge(mk["qk"], n - 3)
                    for c in range(2):
                        last = mm(bank(n % 4)[:, 0:256], w_qkv[:, c, m * 128:(m + 1) * 128],
                                  hT[:, c, half * 256:(half + 1) * 256], start=(c == 0), stop=(c == 1))
                    last.then_inc(pe["qk"], 1)

            def scores(t):
                te.wait_ge(mk["qk"], 2 * INNER_CHUNKS * (t // 2 + 1))
                if t >= 2:
                    te.wait_ge(mk["sub"], t - 1)
                for h2 in range(INNER_CHUNKS):
                    for i in range(PER_TILE):
                        for r in range(2):
                            where, half, slot = place1(2 * h2 + r)
                            rr = slice(64 * r, 64 * r + 64)
                            last = mm(pairs[2 + t % 2][64 * half:64 * half + 64, where,
                                                       slot * 128 + 64 * i:slot * 128 + 64 * i + 64],
                                      qkT[rr, h2, image(t, i)], qkT[rr, INNER_CHUNKS + h2, image(t, i)],
                                      start=True, stop=True)
                last.then_inc(pe["scores"], 1)

            def project_v(t):
                for g in range(2):
                    for c in range(2):
                        last = mm(pairs[V_PAIR[t]][:, g, 0:384], hT[:, c, tokens(t)],
                                  w_qkv[:, c, 2 * INNER + g * 384:2 * INNER + (g + 1) * 384],
                                  start=(c == 0), stop=(c == 1))
                last.then_inc(pe["v"], 1)

            te.wait_ge(ld["w_qk"], 32)
            te.wait_ge(mk["t1"], 4)
            project_qk(0)
            te.wait_ge(mk["hT"], 4)
            turn_spread(MAX_W, 7)
            te.wait_ge(ld["w_v"], 16)
            scores(0)
            project_v(0)
            te.wait_ge(mk["wscale"], 1)
            scores(1)
            project_v(1)
            te.wait_ge(mk["v"], 2)
            project_qk(1)
            scores(2)
            scores(3)

            def turn_p(t):
                te.wait_ge(mk["p"], t + 1)
                if t == 1:
                    te.wait_ge(mk["v"], 3)
                if t >= 2:
                    te.wait_ge(mk["oT"], t - 1)
                for r in range(2):
                    for m in range(3):
                        last = turn(pairs[t % 2][:, r, m * 128:(m + 1) * 128],
                                    p1[:, t, r, 2 * m:2 * m + 2, :].rearrange("p a j -> p (a j)"), 128)
                last.then_inc(pe["pT"], 1)

            def attend(t):
                te.wait_ge(mk["v"], t + 1)
                te.wait_ge(mk["pT"], t + 1)
                for h2 in range(INNER_CHUNKS):
                    for r in range(2):
                        where, half, slot = place1(2 * h2 + r)
                        for i in range(PER_TILE):
                            ii = slice(64 * i, 64 * i + 64)
                            h = 2 * h2 + r
                            last = mm(pairs[t % 2][64 * r:64 * r + 64, i, h2 * 64:(h2 + 1) * 64],
                                      v1[ii, t, h * 64:(h + 1) * 64],
                                      pT1[ii, t, where, slot, 64 * half:64 * half + 64], start=True, stop=True)
                last.then_inc(pe["o"], 1)

            def project_out(t):
                te.wait_ge(mk["oT"], t + 1)
                for c in range(INNER_CHUNKS):
                    last = mm(bank(OUT_BANK[t])[:, 0:DIM], oT1[:, c, t].rearrange("p i n -> p (i n)"), w_out[:, c, :],
                              start=(c == 0), stop=(c == INNER_CHUNKS - 1))
                last.then_inc(pe["out"], 1)

            te.wait_ge(mk["v"], 2)
            te.wait_ge(mk["qk"], 4 * INNER_CHUNKS)
            turn_p(0)
            project_v(2)
            attend(0)
            turn_p(1)
            te.wait_ge(mk["sub"], 3)
            project_v(3)
            attend(1)
            turn_p(2)
            te.wait_ge(ld["w_out"], 16)
            te.wait_ge(mk["sub"], 4)
            project_out(0)
            attend(2)
            turn_p(3)
            project_out(1)
            attend(3)
            te.wait_ge(mk["v"], 4)
            project_out(2)
            project_out(3)

            def up(half, w, src, first_ready, done, freed):
                for m in range(MLP_CHUNKS):
                    n = half * MLP_CHUNKS + m
                    if n >= 4:
                        te.wait_ge(freed, n - 3)
                    for c in range(2):
                        last = mm(bank(4 + n % 4)[:, 0:256], w[:, c, m * 128:(m + 1) * 128],
                                  src[:, c, half * 256:(half + 1) * 256], start=(c == 0), stop=(c == 1))
                    last.then_inc(done, 1)

            def down(t, w, src, done):
                for c in range(MLP_CHUNKS):
                    last = mm(bank(t)[:, 0:DIM], src[:, c, tokens(t)], w[:, c, :],
                              start=(c == 0), stop=(c == MLP_CHUNKS - 1))
                last.then_inc(done, 1)

            te.wait_ge(mk["oT"], 4)
            te.wait_ge(ld["w_ff1"], 16)
            te.wait_ge(ld["w_ff2"], 16)
            for half in range(2):
                for t in (2 * half, 2 * half + 1):
                    te.wait_ge(mk["xhat"], 4 + t + 1)
                    turn_tile(xhat, t, t).then_inc(pe["x2T"], 1)
                te.wait_ge(mk["h2T"], 2 * half + 2)
                if half == 0:
                    te.wait_ge(mk["t2"], 4)
                up(half, w_ff1, h2T, 4, pe["ff1"], mk["gelu"])
            for t in range(TILES):
                te.wait_ge(mk["gelu"], MLP_CHUNKS * (t // 2 + 1))
                down(t, w_ff2, ff, pe["ff2"])

            te.wait_ge(mk["gelu"], 2 * MLP_CHUNKS)
            turn_spread(MAX_H, 4)
            for t in range(TILES):
                te.wait_ge(mk["hr"], t + 1)
                turn_tile(hr, t, t).then_inc(pe["hT"], 1)
            te.wait_ge(mk["wq"], 2)
            te.wait_ge(mk["hq"], 4)
            te.wait_ge(mk["scale"], 2)
            for t in range(TILES):
                for c in range(2):
                    last = mm(bank(t)[:, 0:DIM], hq[:, c, tokens(t)], wqkv_q[:, c, 2 * DIM:3 * DIM],
                              start=(c == 0), stop=(c == 1))
                last.then_inc(pe["v2"], 1)
            for m in range(4):
                for c in range(2):
                    last = mm(bank(4 + m)[0:HALF, :], wqkv_q[:, c, m * HALF:(m + 1) * HALF], hq[:, c, :],
                              start=(c == 0), stop=(c == 1))
                last.then_inc(pe["qk2"], 1)
            te.wait_ge(mk["v2"], 4)
            turn_spread(MAX_QKV, 0)
            te.wait_ge(mk["scale"], 3)
            te.wait_ge(mk["qk2"], 4)
            te.wait_ge(mk["qq"], 1)
            te.wait_ge(mk["kd"], 4)
            te.wait_ge(mk["ka"], 2)
            for t in range(TILES):
                for i in range(PER_TILE):
                    for c in range(2):
                        last = mm(pairs[t][64 * c:64 * c + 64, i, 0:CHUNK_HEADS * TOKENS], q_q[:, c, image(t, i)],
                                  k_heads[:, :, c, image(t, i)], start=True, stop=True)
                last.then_inc(pe["scores2"], 1)
            te.wait_ge(mk["sub2"], 4)
            turn_spread(MAX_P, 0)
            te.wait_ge(mk["identb"], 1)
            te.wait_ge(mk["vq"], 1)

            def turn_p2(t):
                te.wait_ge(mk["p2"], t + 1)
                dst = bank(t).bitcast(bf16)
                for h in range(CHUNK_HEADS):
                    last = nc.tensor.transpose(dst[:, h * 128:(h + 1) * 128], p2q[:, t, h, :], ident_b[:, :])
                last.then_inc(pe["pT2"], 1)

            def attend2(t):
                te.wait_ge(mk["pT2"], t + 1)
                for h in range(HEADS):
                    for i in range(PER_TILE):
                        ii = slice(64 * i, 64 * i + 64)
                        half, slot = h // CHUNK_HEADS, h % CHUNK_HEADS
                        r = h % 4
                        at = (t % 2) * 192 + (h // 4) * 64
                        last = mm(pairs[2 + i][32 * r:32 * r + 32, t // 2, at:at + 64],
                                  v_q[ii, t, h, :], pT2[ii, t, slot, 64 * half:64 * half + 64],
                                  start=True, stop=True)
                last.then_inc(pe["o2"], 1)

            turn_p2(0)
            turn_p2(1)
            attend2(0)
            turn_p2(2)
            attend2(1)
            turn_p2(3)
            attend2(2)
            attend2(3)
            te.wait_ge(mk["pT2"], 4)
            turn_spread(MAX_O, 0)
            for t in range(TILES):
                te.wait_ge(mk["oq"], t // 2 + 1)
                for c in range(3):
                    last = mm(bank(t)[:, 0:DIM], o_q[:, c, t].rearrange("p i n -> p (i n)"), wproj_q[:, c, :],
                              start=(c == 0), stop=(c == 2))
                last.then_inc(pe["proj"], 1)

            WQ, WK, WO, WM = range(4)
            te.wait_ge(mk["zpre"], 4)
            for t in range(TILES):
                te.wait_ge(mk["nh"], t + 1)
                turn_tile(nh, t, t).then_inc(pe["nT"], 1)
            te.wait_ge(ld["w_ffn"], 32)
            te.wait_ge(mk["oq"], 2)
            for t in range(TILES):
                te.wait_ge(mk["nT"], t + 1)
                for c in range(2):
                    last = mm(bank(4 + t)[:, 0:DIM + 2], nT[:, c, tokens(t)], w_v3[:, c, :],
                              start=(c == 0), stop=(c == 1))
                last.then_inc(pe["v3"], 1)
            for m in range(2):
                for c in range(2):
                    last = mm(bank(m)[0:HALF, :], w_ffn[:, WK, c, m * HALF:(m + 1) * HALF], nT[:, c, :],
                              start=(c == 0), stop=(c == 1))
                last.then_inc(pe["k3"], 1)
            te.wait_ge(mk["score_b"], 1)
            for t in range(TILES):
                last = turn(bank(2)[:, tokens(t)], score_b[:, t, :], 128)
            last.then_inc(pe["scoreT"], 1)
            te.wait_ge(mk["n3"], 4)
            te.wait_ge(mk["picked"], 4)
            for c in range(2):
                for t in range(TILES):
                    last = mm(bank(3)[0:HALF, c * ALL_PICKED:(c + 1) * ALL_PICKED],
                              n3[:, t, c * HALF:(c + 1) * HALF], picked[:, t, :],
                              start=(t == 0), stop=(t == TILES - 1))
            last.then_inc(pe["nsel"], 1)
            te.wait_ge(mk["k3"], 2)
            for t in range(TILES):
                last = turn(bank(0)[0:ALL_PICKED, tokens(t)], picked[:, t, :], 128)
            last.then_inc(pe["pickT"], 1)
            te.wait_ge(mk["nselT"], 1)
            for m in range(2):
                for c in range(2):
                    last = mm(bank(1)[0:HALF, m * ALL_PICKED:(m + 1) * ALL_PICKED],
                              w_ffn[:, WQ, c, m * HALF:(m + 1) * HALF], nselT[:, c, :],
                              start=(c == 0), stop=(c == 1))
            last.then_inc(pe["q3"], 1)
            te.wait_ge(mk["v3"], 4)
            for t in range(TILES):
                te.wait_ge(mk["mixer"], t + 1)
                for c in range(2):
                    last = mm(bank(4 + t)[0:HALF, c * TILE:(c + 1) * TILE], n3[:, t, c * HALF:(c + 1) * HALF],
                              mixer[:, t, :], start=True, stop=True)
                last.then_inc(pe["mixT"], 1)
            te.wait_ge(mk["q3h"], 2)
            for n in range(IMAGES):
                t, i = n % TILES, n // TILES
                for c in range(2):
                    last = mm(bank(3)[64 * c:64 * c + 64, image(t, i)], q3h[:, c, n, :],
                              k3[:, c, image(t, i)], start=True, stop=True)
            last.then_inc(pe["scores3"], 1)
            for t in range(TILES):
                te.wait_ge(mk["mixT"], t + 1)
                for c in range(2):
                    last = mm(bank(4 + t)[:, 0:DIM], mixT[:, c, tokens(t)], w_ffn[:, WM, c, :],
                              start=(c == 0), stop=(c == 1))
                last.then_inc(pe["mix"], 1)
            te.wait_ge(mk["p3"], 1)
            for t in range(TILES):
                last = turn(bank(2)[:, tokens(t)], p3[:, 2 * t:2 * t + 2, :].rearrange("p i j -> p (i j)"), 128)
            last.then_inc(pe["pT3"], 1)
            te.wait_ge(mk["pickT"], 1)
            te.wait_ge(mk["pT3"], 1)
            for t in range(TILES):
                for c in range(2):
                    for i in range(PER_TILE):
                        ii = slice(64 * i, 64 * i + 64)
                        last = mm(bank(i)[0:HALF, (TILES * c + t) * 64:(TILES * c + t) * 64 + 60],
                                  v3[ii, t, c * HALF:(c + 1) * HALF], pT3[ii, t, 64 * c:64 * c + 60],
                                  start=True, stop=True)
            last.then_inc(pe["o3"], 1)
            te.wait_ge(mk["sub3"], 1)
            te.wait_ge(mk["o3T"], 2)
            for c in range(2):
                last = mm(bank(3)[0:ALL_PICKED, 0:DIM], o3T[:, c].rearrange("p i t q -> p (i t q)"),
                          w_ffn[:, WO, c, :], start=(c == 0), stop=(c == 1))
            last.then_inc(pe["a3"], 1)
            te.wait_ge(mk["a3"], 1)
            for t in range(TILES):
                te.wait_ge(mk["mixz"], t + 1)
                mm(bank(4 + t)[:, 0:DIM], pickedT[:, tokens(t)], a3[:, :], start=True, stop=True).then_inc(pe["spread"], 1)
            te.wait_ge(ld["W1"], 16)
            te.wait_ge(ld["W2"], 16)
            for half in range(2):
                for t in (2 * half, 2 * half + 1):
                    te.wait_ge(mk["xhat"], 8 + t + 1)
                    turn_tile(xhat, t, t).then_inc(pe["x4T"], 1)
                te.wait_ge(mk["h5T"], 2 * half + 2)
                if half == 0:
                    te.wait_ge(mk["h4"], 4)
                up(half, W1, h5T, 8, pe["W1"], mk["gelu3"])
            for t in range(TILES):
                te.wait_ge(mk["gelu3"], MLP_CHUNKS * (t // 2 + 1))
                down(t, W2, ff3, pe["W2"])

        @block.gpsimd
        def _(pool):
            steps = [0]

            def step(ins):
                steps[0] += 1
                ins.then_inc(pool_step, 1)
                pool.wait_ge(pool_step, steps[0])

            def inverse_deviation(group):
                tt = GROUPS[group]
                pool.wait_ge(mk["var"], group + 1)
                nc.gpsimd.tensor_tensor(rstd[:, tt[0]:tt[-1] + 1], var_eps[:, tt[0]:tt[-1] + 1],
                                        power[:, 0:len(tt)], ALU.pow).then_inc(mk["rstd"], 1)

            nc.gpsimd.memset(w_proj[:], 0.0).then_inc(mk["zero"], 1)
            nc.gpsimd.memset(wmax[:], 0.0).then_inc(mk["zero"], 1)
            nc.gpsimd.memset(qmax[:], 0.0).then_inc(mk["zero"], 1)
            nc.gpsimd.memset(round_bias[:], ROUND).then_inc(mk["zero"], 1)
            step(nc.gpsimd.memset(power[:], -0.5))
            pool.wait_ge(ld["ident"], 16)
            nc.gpsimd.tensor_copy(ident_b[:], ident[:]).then_inc(mk["identb"], 1)
            for t in range(TILES):
                inverse_deviation(LN1 + t)
            pool.wait_ge(ld["rows_tok"], 16)
            for t in range(TILES):
                nc.gpsimd.tensor_tensor(t1b[:, t], t1[:, t], row("b_out"), ALU.add).then_inc(mk["t1b"], 1)
            pool.wait_ge(mk["wscale"], 1)
            step(nc.gpsimd.tensor_scalar(wqkv_r[:], w_qkv2[:], winv[0:HALF, 0:1], ROUND, ALU.mult, ALU.add))
            nc.gpsimd.tensor_scalar(wqkv_q[:], wqkv_r[:], -ROUND, None, ALU.add).then_inc(mk["wq"], 1)
            step(nc.gpsimd.tensor_scalar(wproj_r[:], w_proj[:], winv[:, 1:2], ROUND, ALU.mult, ALU.add))
            nc.gpsimd.tensor_scalar(wproj_q[:], wproj_r[:], -ROUND, None, ALU.add).then_inc(mk["wq"], 1)
            pool.wait_ge(ld["rows"], 32)
            for g in range(2):
                inverse_deviation(LN2 + g)
                for t in (2 * g, 2 * g + 1):
                    nc.gpsimd.tensor_tensor(t2b[:, t], t2[:, t], row("b_ff2"), ALU.add).then_inc(mk["t2b"], 1)
            for t in range(TILES):
                pool.wait_ge(mk["h1"], t + 1)
                nc.gpsimd.tensor_tensor(h1b[:, t], h1[:, t], row("b_proj"), ALU.add).then_inc(mk["h1b"], 1)
            step(nc.gpsimd.memset(v_q[:], 0.0))
            step(nc.gpsimd.memset(q3h[:], 0.0))
            pool.wait_ge(mk["scale"], 3)
            step(nc.gpsimd.tensor_scalar(v_r[:], v2[:], qinv[:, 2:3], ROUND, ALU.mult, ALU.add))
            nc.gpsimd.tensor_scalar(v_q[:, :, :, 0:HEAD], v_r[:].rearrange("p t (h d) -> p t h d", d=HEAD), -ROUND, None,
                                    ALU.add).then_inc(mk["vq"], 1)
            inverse_deviation(LNZ)
            inverse_deviation(LNN)
            for t in range(TILES):
                pool.wait_ge(mk["nh"], t + 1)
                step(nc.gpsimd.tensor_tensor(ng[:, t], nh[:, t], row("g1"), ALU.mult))
                nc.gpsimd.tensor_tensor(n3[:, t], ng[:, t], row("b1"), ALU.add).then_inc(mk["n3"], 1)
            for t in range(TILES):
                nc.gpsimd.tensor_tensor(zb[:, t], z[:, t], row("bf2"), ALU.add).then_inc(mk["zb"], 1)
            for g in range(2):
                inverse_deviation(LN4 + g)
                for t in (2 * g, 2 * g + 1):
                    pool.wait_ge(mk["zb"], t + 1)
                    nc.gpsimd.tensor_tensor(h4z[:, t], h4[:, t], zb[:, t], ALU.add).then_inc(mk["h4z"], 1)
            for t in range(TILES):
                inverse_deviation(LNY + t)

        @block.scalar
        def _(act):
            act.dma_start(rows[:, 0:1], A["rows"][0:1].rearrange("(a r) n -> a r n", a=1)
                          .to_broadcast([128, 1, DIM])).then_inc(ld["row0"], 16)
            act.dma_start(cols[:], A["cols"]).then_inc(ld["cols"], 16)

            def from_chunks(t, where, dst, scale, bias, done):
                for c in range(2):
                    last = nc.scalar.activation(dst[:, c, tokens(t)], split_chunks(bank(where))[:, c, :], ACT.Identity,
                                                scale=col(scale, c), bias=col(bias, c))
                last.then_inc(done, 1)

            act.wait_ge(ld["cols"], 16)
            for t in range(TILES):
                act.wait_ge(pe["xhatT"], t + 1)
                from_chunks(t, 4 + t, hT, "g1", "beta1", mk["hT"])

            def keep_qk(half):
                for m in range(2 * INNER_CHUNKS):
                    n = half * 2 * INNER_CHUNKS + m
                    act.wait_ge(pe["qk"], n + 1)
                    nc.scalar.activation(qkT[:, m, half * 256:(half + 1) * 256], bank(n % 4)[:, 0:256],
                                         ACT.Copy).then_inc(mk["qk"], 1)

            def exp1(t):
                act.wait_ge(mk["sub"], t + 1)
                nc.scalar.activation(p1[:, t], p1[:, t], ACT.Exp, scale=HEAD1 ** -0.5).then_inc(mk["exp"], 1)

            def keep_pT(t):
                act.wait_ge(pe["pT"], t + 1)
                nc.scalar.activation(pT1[:, t].rearrange("p r m n -> p r (m n)"), pairs[t % 2][:, :, 0:384],
                                     ACT.Copy).then_inc(mk["pT"], 1)

            def keep_o(t):
                act.wait_ge(pe["o"], t + 1)
                nc.scalar.activation(oT1[:, :, t].rearrange("p c i n -> p i c n"),
                                     pairs[t % 2][:, :, 0:384].rearrange("p i (c n) -> p i c n", n=TOKENS),
                                     ACT.Copy).then_inc(mk["oT"], 1)

            keep_qk(0)
            exp1(0)
            exp1(1)
            keep_qk(1)
            exp1(2)
            keep_pT(0)
            exp1(3)
            for t in range(TILES):
                keep_o(t)
                if t + 1 < TILES:
                    keep_pT(t + 1)

            def gelus(half, src, dst, which, done):
                for m in range(MLP_CHUNKS):
                    n = half * MLP_CHUNKS + m
                    act.wait_ge(src, n + 1)
                    nc.scalar.activation(dst[:, m, half * 256:(half + 1) * 256], bank(4 + n % 4)[:, 0:256], ACT.Gelu,
                                         bias=cols_ff[:, which, m:m + 1]).then_inc(done, 1)

            act.wait_ge(ld["cols_ff"], 16)
            for half in range(2):
                for t in (2 * half, 2 * half + 1):
                    act.wait_ge(pe["x2T"], t + 1)
                    from_chunks(t, t, h2T, "g2", "beta2", mk["h2T"])
                gelus(half, pe["ff1"], ff, 0, mk["gelu"])

            for t in range(TILES):
                act.wait_ge(pe["hT"], t + 1)
                nc.scalar.activation(hq[:, :, tokens(t)], split_chunks(bank(t)), ACT.Copy,
                                     bias=-ROUND).then_inc(mk["hq"], 1)
            act.wait_ge(mk["scale"], 2)
            for m in range(4):
                act.wait_ge(pe["qk2"], m + 1)
                nc.scalar.activation(qk2[:, m, :], bank(4 + m)[0:HALF, :], ACT.Identity, scale=hs[0:HALF, 2:3],
                                     bias=col("bq2" if m < 2 else "bk2", m % 2)).then_inc(mk["qk2"], 1)
            act.wait_ge(mk["scale"], 3)
            nc.scalar.activation(qk_r[:, 0:2], qk2[:, 0:2], ACT.Identity, scale=qinv[0:HALF, 0:1],
                                 bias=round_bias[0:HALF, 0:1]).then_inc(mk["qkr"], 1)
            act.wait_ge(mk["kq"], 1)
            for h in range(4, CHUNK_HEADS):
                nc.scalar.activation(k_heads[:, h], k_q[:], ACT.Copy, scale=head_mask[:, h:h + 1]).then_inc(mk["ka"], 1)
            for t in range(TILES):
                act.wait_ge(mk["sub2"], t + 1)
                nc.scalar.activation(e2[:, t], e2[:, t], ACT.Exp, scale=slog[:, 0:1]).then_inc(mk["exp2"], 1)
            for t in range(TILES):
                act.wait_ge(pe["pT2"], t + 1)
                nc.scalar.activation(pT2[:, t].rearrange("p h n -> p (h n)"), bank(t).bitcast(bf16)[:, 0:768],
                                     ACT.Copy).then_inc(mk["pT2"], 1)
            act.wait_ge(mk["scale"], 4)
            for g in range(2):
                nc.scalar.activation(o_r[:, :, 2 * g:2 * g + 2, 1, :].rearrange("p c t n -> p t c n"),
                                     pairs[3][:, g, 0:384].rearrange("p (t c n) -> p t c n", t=2, c=3),
                                     ACT.Identity, scale=os_[:, 4:5], bias=round_bias[:, 0:1]).then_inc(mk["or"], 1)

            for t in range(TILES):
                act.wait_ge(pe["nT"], t + 1)
                from_chunks(t, t, nT, "ffn_g1", "ffn_b1", mk["nT"])
            act.wait_ge(mk["v3"], 4)
            nc.scalar.activation(eneg[:], v3[:, :, DIM], ACT.Exp, scale=-1.0).then_inc(mk["eneg"], 1)
            for m in range(2):
                act.wait_ge(pe["k3"], m + 1)
                nc.scalar.activation(k3[:, m, :], bank(m)[0:HALF, :], ACT.Identity, bias=col("bk3", m)).then_inc(mk["k3"], 1)
            act.wait_ge(pe["pickT"], 1)
            nc.scalar.activation(pickedT[:], bank(0)[0:ALL_PICKED, :], ACT.Copy).then_inc(mk["pickT"], 1)
            for t in range(TILES):
                act.wait_ge(pe["mixT"], t + 1)
                nc.scalar.activation(mixT[:, :, tokens(t)], split_chunks(bank(4 + t)), ACT.Copy).then_inc(mk["mixT"], 1)
            act.wait_ge(mk["sub3"], 1)
            nc.scalar.activation(p3[:], p3[:], ACT.Exp, scale=HEAD ** -0.5).then_inc(mk["exp3"], 1)
            act.wait_ge(pe["pT3"], 1)
            nc.scalar.activation(pT3[:].rearrange("p t n -> p (t n)"), bank(2), ACT.Copy).then_inc(mk["pT3"], 1)
            for half in range(2):
                for t in (2 * half, 2 * half + 1):
                    act.wait_ge(pe["x4T"], t + 1)
                    from_chunks(t, t, h5T, "ffn_g2", "ffn_b2", mk["h5T"])
                gelus(half, pe["W1"], ff3, 1, mk["gelu3"])

        @block.vector
        def _(dve):
            v = nc.vector
            steps = [0]

            def step(ins):
                steps[0] += 1
                ins.then_inc(dve_step, 1)
                dve.wait_ge(dve_step, steps[0])

            def wide(ap, n):
                return ap.unsqueeze(len(ap.shape)).to_broadcast(list(ap.shape) + [n])

            def statistics(group, src):
                tt = GROUPS[group]
                for t in tt:
                    last = v.bn_stats(stats[:, t], src[:, t])
                step(last)
                for t in tt:
                    last = v.bn_aggr(mv[:, t], stats[:, t])
                step(last)
                g = slice(tt[0], tt[-1] + 1)
                v.tensor_scalar(var_eps[:, g], mv[:, g, 1], EPS, None, ALU.add).then_inc(mk["var"], 1)

            def centre(group, t, src, dst):
                dve.wait_ge(mk["rstd"], group + 1)
                return v.tensor_scalar(dst[:, t], src[:, t], mv[:, t, 0:1], rstd[:, t:t + 1], ALU.subtract, ALU.mult)

            def layernorm(group, src, dst, done):
                statistics(group, src)
                for t in GROUPS[group]:
                    centre(group, t, src, dst).then_inc(done, 1)

            def global_max(nth, maxima, dst, where):
                width = MAX_WIDTH[nth]
                if nth > 0:
                    dve.wait_ge(pe["wide"], nth)
                v.tensor_copy(spread[:, 0:width, :], wide(maxima, 128)).then_inc(mk["spread"], 1)
                dve.wait_ge(pe["wide"], nth + 1)
                step(v.tensor_reduce(dst, bank(where)[:, 0:width * 128].rearrange("p (k n) -> p k n", k=width), X, ALU.max))

            def scale_of(dst, maxima):
                return v.tensor_scalar(dst, maxima, 1.0 / QMAX, 1e-8, ALU.mult, ALU.max)

            dve.wait_ge(ld["row0"], 16)
            for t in range(TILES):
                dve.wait_ge(pe["patch"], t + 1)
                v.tensor_tensor(t1[:, t], bank(t)[:, 0:DIM], row("b_patch"), ALU.add).then_inc(mk["t1"], 1)
                dve.wait_ge(mk["t1"], t + 1)
                layernorm(LN1 + t, t1, xhat, mk["xhat"])
            dve.wait_ge(mk["zero"], 4)
            dve.wait_ge(ld["w_qkv2"], 16)
            dve.wait_ge(ld["w_proj"], 64)
            dve.wait_ge(ld["const"], 16)
            step(v.tensor_reduce(wmax[0:HALF, 0:1], w_qkv2[:].rearrange("p c n -> p (c n)"), X, ALU.max, apply_absolute_value=True))
            step(v.tensor_reduce(wmax[:, 1:2], w_proj[:].rearrange("p c n -> p (c n)"), X, ALU.max, apply_absolute_value=True))
            global_max(MAX_W, wmax[:], gm[:, 0:2], 7)
            step(scale_of(wscale[:], gm[:, 0:2]))
            v.reciprocal(winv[:], wscale[:]).then_inc(mk["wscale"], 1)

            def soft_scores(t):
                src = pairs[2 + t % 2][:, :, 0:384].rearrange("p r (s j) -> p r s j", j=TOKENS)
                m = mx1[:, t].rearrange("p (r s) -> p r s", r=2)
                dve.wait_ge(pe["scores"], t + 1)
                step(v.tensor_reduce(m, src, X, ALU.max))
                v.tensor_tensor(p1[:, t], src, wide(m, TOKENS), ALU.subtract).then_inc(mk["sub"], 1)

            def keep_v(t):
                dve.wait_ge(pe["v"], t + 1)
                v.tensor_copy(v1[:, t].rearrange("p (g n) -> p g n", g=2), pairs[V_PAIR[t]][:, :, 0:384]).then_inc(mk["v"], 1)

            def normalise(t):
                e = p1[:, t].rearrange("p r s j -> p (r s) j")
                dve.wait_ge(mk["exp"], t + 1)
                step(v.tensor_reduce(sum1[:, t], e, X, ALU.add))
                step(v.reciprocal(inv1[:, t], sum1[:, t]))
                v.tensor_tensor(e, e, wide(inv1[:, t], TOKENS), ALU.mult).then_inc(mk["p"], 1)

            soft_scores(0)
            keep_v(0)
            soft_scores(1)
            keep_v(1)
            normalise(0)
            normalise(1)
            soft_scores(2)
            soft_scores(3)
            keep_v(2)
            normalise(2)
            keep_v(3)
            normalise(3)

            for g in range(2):
                for t in (2 * g, 2 * g + 1):
                    dve.wait_ge(pe["out"], t + 1)
                    dve.wait_ge(mk["t1b"], t + 1)
                    v.tensor_tensor(t2[:, t], bank(OUT_BANK[t])[:, 0:DIM], t1b[:, t], ALU.add).then_inc(mk["t2"], 1)
                dve.wait_ge(mk["t2"], 2 * g + 2)
                layernorm(LN2 + g, t2, xhat, mk["xhat"])
            for t in range(TILES):
                dve.wait_ge(pe["ff2"], t + 1)
                dve.wait_ge(mk["t2b"], t + 1)
                v.tensor_tensor(h1[:, t], bank(t)[:, 0:DIM], t2b[:, t], ALU.add).then_inc(mk["h1"], 1)
                dve.wait_ge(mk["h1"], t + 1)
                last = v.tensor_reduce(hmax[:, t:t + 1], h1[:, t], X, ALU.max, apply_absolute_value=True)
            step(last)
            step(v.tensor_reduce(hmax[:, TILES:TILES + 1], hmax[:, 0:TILES], X, ALU.max))

            dve.wait_ge(ld["rows"], 32)
            global_max(MAX_H, hmax[:, TILES:TILES + 1], gm[:, 0:1], 4)
            step(scale_of(hs[:, 0:1], gm[:, 0:1]))
            step(v.reciprocal(hs[:, 1:2], hs[:, 0:1]))
            for t in range(TILES):
                v.tensor_scalar(hr[:, t], h1[:, t], hs[:, 1:2], ROUND, ALU.mult, ALU.add).then_inc(mk["hr"], 1)
            v.tensor_tensor(hs[:, 2:3], hs[:, 0:1], wscale[:, 0:1], ALU.mult).then_inc(mk["scale"], 2)
            dve.wait_ge(mk["scale"], 2)
            for t in range(TILES):
                dve.wait_ge(pe["v2"], t + 1)
                v.scalar_tensor_tensor(out=v2[:, t], in0=bank(t)[:, 0:DIM], scalar=hs[:, 2:3], in1=row("bv2"),
                                       op0=ALU.mult, op1=ALU.add).then_inc(mk["v2"], 1)
            dve.wait_ge(mk["v2"], 4)
            v.tensor_reduce(qmax[:, 2:3], v2[:].rearrange("p t n -> p (t n)"), X, ALU.max, apply_absolute_value=True)
            for m in range(4):
                dve.wait_ge(mk["qk2"], m + 1)
                last = v.tensor_reduce(qmax_parts[0:HALF, m:m + 1], qk2[:, m, :], X, ALU.max, apply_absolute_value=True)
            step(last)
            step(v.tensor_reduce(qmax[0:HALF, 0:2], qmax_parts[0:HALF, :].rearrange("p (a b) -> p a b", a=2), X, ALU.max))
            global_max(MAX_QKV, qmax[:], gm[:, 0:3], 0)
            step(scale_of(qs[:], gm[:, 0:3]))
            v.reciprocal(qinv[:], qs[:]).then_inc(mk["scale"], 1)
            dve.wait_ge(mk["scale"], 3)
            step(v.tensor_scalar(qk_r[:, 2:4], qk2[:, 2:4], qinv[0:HALF, 1:2], ROUND, ALU.mult, ALU.add))
            v.tensor_scalar(k_q[:], qk_r[:, 2:4], -ROUND, None, ALU.add).then_inc(mk["kq"], 1)
            v.tensor_scalar(slog[:], qs[:, 0:1], qs[:, 1:2], HEAD ** -0.5, ALU.mult, ALU.mult)
            dve.wait_ge(mk["kq"], 1)
            for h in range(4):
                v.tensor_scalar(k_heads[:, h], k_q[:], head_mask[:, h:h + 1], None, ALU.mult).then_inc(mk["kd"], 1)
            dve.wait_ge(mk["qkr"], 1)
            v.tensor_scalar(q_q[:], qk_r[:, 0:2], -ROUND, None, ALU.add).then_inc(mk["qq"], 1)
            for t in range(TILES):
                src = pairs[t][:, :, 0:384].rearrange("p i (h j) -> p i h j", j=TOKENS)
                m = mx2[:, t].rearrange("p (h i) -> p i h", i=2)
                dve.wait_ge(pe["scores2"], t + 1)
                step(v.tensor_reduce(m, src, X, ALU.max))
                v.tensor_tensor(e2[:, t].rearrange("p h i j -> p i h j"), src, wide(m, TOKENS),
                                ALU.subtract).then_inc(mk["sub2"], 1)
            for t in range(TILES):
                dve.wait_ge(mk["exp2"], t + 1)
                last = v.tensor_reduce(sum2[:, t], e2[:, t].rearrange("p h i j -> p (h i) j"), X, ALU.add)
            step(last)
            step(v.reciprocal(inv2[:], sum2[:]))
            step(v.tensor_reduce(pmax[:], inv2[:].rearrange("p t n -> p (t n)"), X, ALU.max))
            global_max(MAX_P, pmax[:], gm[:, 0:1], 0)
            step(scale_of(ps_[:, 0:1], gm[:, 0:1]))
            step(v.reciprocal(ps_[:, 1:2], ps_[:, 0:1]))
            step(v.tensor_scalar(f2[:], inv2[:], ps_[:, 1:2], None, ALU.mult))
            for t in range(TILES):
                step(v.tensor_tensor(p2[:, t].rearrange("p h (i j) -> p (h i) j", j=TOKENS),
                                     e2[:, t].rearrange("p h i j -> p (h i) j"), wide(f2[:, t], TOKENS), ALU.mult))
                v.tensor_scalar(p2q[:, t], p2[:, t], ROUND, ROUND, ALU.add, ALU.subtract).then_inc(mk["p2"], 1)
            step(v.tensor_tensor(os_[:, 0:1], qs[:, 2:3], ps_[:, 0:1], ALU.mult))
            step(v.tensor_scalar(os_[:, 1:2], os_[:, 0:1], 1.0 / QMAX, None, ALU.mult))
            for g in range(2):
                for i in range(PER_TILE):
                    dve.wait_ge(pe["o2"], 2 * g + 2)
                    last = v.tensor_reduce(omax_parts[:, 2 * g + i:2 * g + i + 1], pairs[2 + i][:, g, 0:384],
                                           X, ALU.max, apply_absolute_value=True)
            step(last)
            step(v.tensor_reduce(omax[:], omax_parts[:], X, ALU.max))
            global_max(MAX_O, omax[:], gm[:, 0:1], 0)
            step(v.tensor_scalar(os_[:, 2:3], gm[:, 0:1], os_[:, 1:2], 1e-8, ALU.mult, ALU.max))
            step(v.reciprocal(os_[:, 3:4], os_[:, 2:3]))
            v.tensor_tensor(os_[:, 4:5], os_[:, 3:4], os_[:, 0:1], ALU.mult).then_inc(mk["scale"], 1)
            dve.wait_ge(mk["scale"], 4)
            for g in range(2):
                step(v.tensor_scalar(o_r[:, :, 2 * g:2 * g + 2, 0, :].rearrange("p c t n -> p t c n"),
                                     pairs[2][:, g, 0:384].rearrange("p (t c n) -> p t c n", t=2, c=3),
                                     os_[:, 4:5], ROUND, ALU.mult, ALU.add))
                dve.wait_ge(mk["or"], g + 1)
                v.tensor_scalar(o_q[:, :, 2 * g:2 * g + 2], o_r[:, :, 2 * g:2 * g + 2], -ROUND, None, ALU.add).then_inc(mk["oq"], 1)
            step(v.tensor_tensor(hs[:, 2:3], os_[:, 2:3], wscale[:, 1:2], ALU.mult))
            for t in range(TILES):
                dve.wait_ge(pe["proj"], t + 1)
                dve.wait_ge(mk["h1b"], t + 1)
                v.scalar_tensor_tensor(out=zpre[:, t], in0=bank(t)[:, 0:DIM], scalar=hs[:, 2:3], in1=h1b[:, t],
                                       op0=ALU.mult, op1=ALU.add).then_inc(mk["zpre"], 1)
            dve.wait_ge(mk["zpre"], 4)
            layernorm(LNZ, zpre, z, mk["z"])

            dve.wait_ge(mk["z"], 4)
            statistics(LNN, z)
            for t in range(TILES):
                centre(LNN, t, z, nh).then_inc(mk["nh"], 1)
            for t in range(TILES):
                dve.wait_ge(pe["v3"], t + 1)
                v.tensor_tensor(v3[:, t], bank(4 + t)[:, 0:DIM + 2], row_v3[:], ALU.add).then_inc(mk["v3"], 1)
            dve.wait_ge(mk["eneg"], 1)
            step(v.tensor_scalar(eneg1[:], eneg[:], 1.0, None, ALU.add))
            step(v.reciprocal(score[:], eneg1[:]))
            v.tensor_copy(score_b[:], wide(score[:], 128)).then_inc(mk["score_b"], 1)
            dve.wait_ge(pe["scoreT"], 1)
            for t in range(TILES):
                s = bank(2)[:, tokens(t)]
                v.scalar_tensor_tensor(out=below[:, t], in0=s, scalar=score[:, t:t + 1], in1=same,
                                       op0=ALU.is_lt, op1=ALU.mult, accum_out=less[:, t:t + 1])
                last = v.scalar_tensor_tensor(out=equal[:, t], in0=s, scalar=score[:, t:t + 1], in1=before,
                                              op0=ALU.is_equal, op1=ALU.mult, accum_out=tie[:, t:t + 1])
            step(last)
            step(v.tensor_tensor(rank[:], less[:], tie[:], ALU.add))
            for t in range(TILES):
                v.tensor_scalar(picked[:, t, :], pick_at[:, t, :], rank[:, t:t + 1], None,
                                ALU.is_equal).then_inc(mk["picked"], 1)
            for t in range(TILES):
                last = v.scalar_tensor_tensor(out=sTm[:, t], in0=bank(2)[:, tokens(t)], scalar=1.0, in1=same,
                                              op0=ALU.mult, op1=ALU.mult, accum_out=total[:, t:t + 1])
            step(last)
            v.tensor_scalar(rest[:], rank[:], float(PICKED), None, ALU.is_ge)
            step(v.tensor_scalar(total_e[:], total[:], 1e-6, None, ALU.add))
            step(v.reciprocal(total_i[:], total_e[:]))
            step(v.tensor_tensor(weight[:], score[:], total_i[:], ALU.mult))
            for t in range(TILES):
                v.scalar_tensor_tensor(out=mixer[:, t], in0=sTm[:, t], scalar=weight[:, t:t + 1], in1=ident[:],
                                       op0=ALU.mult, op1=ALU.add).then_inc(mk["mixer"], 1)
            dve.wait_ge(pe["nsel"], 1)
            v.tensor_copy(nselT[:].rearrange("p c n -> p (c n)"), bank(3)[0:HALF, 0:2 * ALL_PICKED]).then_inc(mk["nselT"], 1)
            dve.wait_ge(pe["q3"], 1)
            for c in range(2):
                last = v.tensor_scalar(q3[:, c].rearrange("p n q -> p (n q)"),
                                       bank(1)[0:HALF, c * ALL_PICKED:(c + 1) * ALL_PICKED],
                                       col("bq3", c), None, ALU.add)
            step(last)
            for c in range(2):
                v.tensor_tensor(q3h[:, c, :, 0:CHUNK_HEADS * PICKED].rearrange("p n (h q) -> p n h q", q=PICKED),
                                q3[:, c].unsqueeze(2).to_broadcast([HALF, IMAGES, CHUNK_HEADS, PICKED]),
                                head_mask.unsqueeze(1).unsqueeze(3).to_broadcast([HALF, IMAGES, CHUNK_HEADS, PICKED]),
                                ALU.mult).then_inc(mk["q3h"], 1)
            dve.wait_ge(pe["scores3"], 1)
            src = bank(3).rearrange("p (n j) -> p n j", j=TOKENS)
            step(v.tensor_reduce(mx3[:], src, X, ALU.max))
            v.tensor_tensor(p3[:], src, wide(mx3[:], TOKENS), ALU.subtract).then_inc(mk["sub3"], 1)
            dve.wait_ge(mk["exp3"], 1)
            step(v.tensor_reduce(sum3[:], p3[:], X, ALU.add))
            step(v.reciprocal(inv3[:], sum3[:]))
            v.tensor_tensor(p3[:], p3[:], wide(inv3[:], TOKENS), ALU.mult).then_inc(mk["p3"], 1)
            for t in range(TILES):
                dve.wait_ge(pe["mix"], t + 1)
                last = v.tensor_tensor(mixb[:, t], bank(4 + t)[:, 0:DIM], row("bm"), ALU.add)
            step(last)
            for t in range(TILES):
                v.scalar_tensor_tensor(out=mixz[:, t], in0=mixb[:, t], scalar=rest[:, t:t + 1], in1=z[:, t],
                                       op0=ALU.mult, op1=ALU.add).then_inc(mk["mixz"], 1)
            dve.wait_ge(pe["o3"], 1)
            for i in range(PER_TILE):
                src = bank(i)[0:HALF, :].rearrange("p (a b) -> p a b", b=64)[:, :, 0:60].rearrange("p a (h q) -> p a h q", q=PICKED)
                step(v.tensor_tensor(o3m[:, i].rearrange("p a (h q) -> p a h q", q=PICKED), src,
                                     head_mask.unsqueeze(1).unsqueeze(3).to_broadcast([HALF, 2 * TILES, CHUNK_HEADS, PICKED]),
                                     ALU.mult))
                v.tensor_reduce(o3T[:, :, i], o3m[:, i].rearrange("p (c t) (h q) -> p c t q h", c=2, q=PICKED),
                                X, ALU.add).then_inc(mk["o3T"], 1)
            dve.wait_ge(pe["a3"], 1)
            v.tensor_tensor(a3[:], bank(3)[0:ALL_PICKED, 0:DIM], row("bo")[0:ALL_PICKED, :], ALU.add).then_inc(mk["a3"], 1)
            for g in range(2):
                for t in (2 * g, 2 * g + 1):
                    dve.wait_ge(pe["spread"], t + 1)
                    v.tensor_tensor(h4[:, t], bank(4 + t)[:, 0:DIM], mixz[:, t], ALU.add).then_inc(mk["h4"], 1)
                dve.wait_ge(mk["h4"], 2 * g + 2)
                layernorm(LN4 + g, h4, xhat, mk["xhat"])
            for t in range(TILES):
                dve.wait_ge(pe["W2"], t + 1)
                dve.wait_ge(mk["h4z"], t + 1)
                v.tensor_tensor(ypre[:, t], bank(t)[:, 0:DIM], h4z[:, t], ALU.add).then_inc(mk["ypre"], 1)
                dve.wait_ge(mk["ypre"], t + 1)
                layernorm(LNY + t, ypre, y, mk["y"])


def kernel(**inputs):
    import concourse.bacc as bacc
    from concourse.bass_utils import run_bass_kernel_spmd

    a = {k: np.asarray(x) for k, x in inputs.items()}
    tok = lambda n: a["L0_tok_" + n]
    att = lambda n: a["L0_attn_" + n]
    ffn = lambda n: a["L0_ffn_" + n]

    def chunks(w, rows):
        return w.reshape(-1, rows, w.shape[1]).transpose(1, 0, 2)

    def column(x, rows):
        return x.reshape(-1, rows).T

    x = a["x"].reshape(IMAGES, CHANNELS, GRID, PATCH, GRID, PATCH).transpose(3, 5, 1, 0, 2, 4)
    x = x.reshape(PATCH_CHUNKS, 128, TILES, TILE).transpose(1, 2, 0, 3)

    token = np.arange(128)
    mine = token[:, None] // TOKENS == token[None, :] // TOKENS
    pick = np.full((128, TILES, PER_TILE, TILES, PICKED), -1.0)
    for t in range(TILES):
        for i in range(PER_TILE):
            pick[i * TOKENS:(i + 1) * TOKENS, t, i, t, :] = np.arange(PICKED)
    head = np.zeros((128, CHUNK_HEADS))
    head[np.arange(HALF), np.arange(HALF) // HEAD] = 1.0
    table = {"same": mine, "before": mine & (token[None, :] < token[:, None]),
             "pick": pick.reshape(128, -1), "head": head}

    qkv_b, qkv_w = att("b_qkv"), att("w_qkv")
    arrays = {
        "xT": x,
        "w_patch": chunks(tok("w_patch"), 128),
        "w_qkv": chunks(tok("w_qkv"), HALF),
        "w_out": chunks(tok("w_out"), 128),
        "w_ff1": chunks(tok("w_ff1"), HALF),
        "w_ff2": chunks(tok("w_ff2"), 128),
        "w_qkv2": chunks(qkv_w, HALF),
        "w_proj": att("w_proj").reshape(3, 4, HEAD, DIM).transpose(1, 2, 0, 3),
        "w_ffn": np.stack([chunks(ffn(n), HALF) for n in ("Wq", "Wk", "Wo", "Wm")], axis=1),
        "w_v3": chunks(np.concatenate([ffn("Wv")] + [ffn("Wr")[:, None]] * 2, axis=1), HALF),
        "row_v3": np.concatenate([ffn("bv")] + [ffn("br").reshape(1)] * 2).reshape(1, -1),
        "W1": chunks(ffn("W1"), HALF),
        "W2": chunks(ffn("W2"), 128),
        "rows": np.stack([tok("b_patch"), tok("b_out"), tok("b_ff2"), qkv_b[2 * DIM:], att("b_proj"), ffn("g1"),
                          ffn("b1"), ffn("bo"), ffn("bm"), ffn("bf2")]),
        "cols": np.stack([column(v, HALF) for v in (tok("g1"), tok("beta1"), tok("g2"), tok("beta2"), qkv_b[:DIM],
                                                    qkv_b[DIM:2 * DIM], ffn("bq"), ffn("bk"), ffn("g1"), ffn("b1"), ffn("g2"),
                                                    ffn("b2"))], axis=1),
        "cols_ff": np.stack([column(tok("b_ff1"), 128), column(ffn("bf1"), 128)], axis=1),
        "ident": np.eye(128, dtype=np.float32),
        "consts": np.concatenate([table[n] for n in CONSTS], axis=1).astype(np.float32),
    }
    arrays = {k: np.ascontiguousarray(v) for k, v in arrays.items()}

    nc = bacc.Bacc("TRN2", target_bir_lowering=False, num_devices=1)
    f32 = mybir.dt.float32
    A = {k: nc.dram_tensor("in_" + k, v.shape, f32, kind="ExternalInput").ap() for k, v in arrays.items()}
    out = nc.dram_tensor("out", (ALL, DIM), f32, kind="ExternalOutput").ap()
    vit_kernel(nc, A, out)
    r = run_bass_kernel_spmd(nc, [{"in_" + k: v for k, v in arrays.items()}], core_ids=[0])
    return r.results[0]["out"].reshape(IMAGES, TOKENS, DIM)
```

```python
import concourse.bass as bass
import numpy as np
from concourse import mybir
from contextlib import ExitStack

IMAGES, CHANNELS, SIDE, PATCH = 8, 3, 128, 16
GRID = SIDE // PATCH
TOKENS = GRID * GRID
ALL = IMAGES * TOKENS
TILE = 128
PER_TILE = TILE // TOKENS
TILES = ALL // TILE
DIM = 192
HALF = DIM // 2
PATCH_DIM = CHANNELS * PATCH * PATCH
PATCH_CHUNKS = PATCH_DIM // 128
HEADS = 12
HEAD1 = 64
INNER = HEADS * HEAD1
INNER_CHUNKS = INNER // 128
HEAD = DIM // HEADS
CHUNK_HEADS = HEADS // 2
PAD = 32
MLP = 768
MLP_CHUNKS = MLP // 128
PICKED = max(1, int(round(0.15 * TOKENS)))
ALL_PICKED = IMAGES * PICKED
HEAD_ROWS = 64
EPS = 1e-5
QMAX = 127.0
ROUND = 12582912.0

ROWS = ["b_patch", "b_out", "b_ff2", "bv2", "b_proj", "g1", "b1", "bo", "bm", "bf2", "bv3", "Wr"]
COLS = ["g1", "beta1", "g2", "beta2", "bq2", "bk2", "bq3", "bk3", "ffn_g1", "ffn_b1", "ffn_g2", "ffn_b2"]
CONSTS = {"same": 128, "before": 128, "pick": TILES * ALL_PICKED, "head": CHUNK_HEADS}


def const_at(name):
    at = 0
    for n, width in CONSTS.items():
        if n == name:
            return at, at + width
        at += width
    return 0, at


def vit_kernel(nc, A, out):
    f32, bf16 = mybir.dt.float32, mybir.dt.bfloat16
    ALU, ACT, X = mybir.AluOpType, mybir.ActivationFunctionType, mybir.AxisListType.X
    ctx = ExitStack()
    with ctx:
        (PATCHES, QKV, ATTEND, OUT, FF, QUANT, SCORES2, ATTEND2, PROJ, ROUTE, ATTEND3, FF3, END) = range(13)
        ALWAYS = (PATCHES, END)
        floor, ceiling = (nc.sbuf_base + 31) // 32 * 32, nc.sbuf_top
        placed = []

        def sb(name, shape, life, dtype=f32):
            width = int(np.prod(shape[1:])) * (2 if dtype == bf16 else 4)
            width = (width + 31) // 32 * 32
            at = floor
            for start, end, first, last in sorted(placed):
                if first <= life[1] and life[0] <= last and start < at + width and at < end:
                    at = end
            assert at + width <= ceiling, (name, at + width, ceiling)
            placed.append((at, at + width, *life))
            return nc.alloc_sbuf_tensor_at(name, shape, dtype, offset=at)

        def sem(name):
            return ctx.enter_context(nc.semaphore(name))

        stats = sb("stats", [128, TILES, 6], ALWAYS)
        mv = sb("mv", [128, TILES, 2], ALWAYS)
        var_eps = sb("var_eps", [128, TILES], ALWAYS)
        rstd = sb("rstd", [128, TILES], ALWAYS)
        var_n = sb("var_n", [128, TILES], ALWAYS)
        rstd_n = sb("rstd_n", [128, TILES], ALWAYS)
        power = sb("power", [128, TILES], ALWAYS)
        round_bias = sb("round_bias", [128, 1], ALWAYS)
        spread = sb("spread", [128, 3, 128], ALWAYS)
        gm = sb("gm", [128, 3], ALWAYS)
        mx1, sum1, inv1, mx2, sum2, inv2, f2 = (sb(n, [128, TILES, HEADS], ALWAYS) for n in
                                                ("mx1", "sum1", "inv1", "mx2", "sum2", "inv2", "f2"))
        mx3, sum3, inv3 = (sb(n, [128, IMAGES], ALWAYS) for n in ("mx3", "sum3", "inv3"))
        wmax, wscale, winv = (sb(n, [128, 2], ALWAYS) for n in ("wmax", "wscale", "winv"))
        hmax = sb("hmax", [128, TILES + 1], ALWAYS)
        hs = sb("hs", [128, 3], ALWAYS)
        qmax_parts = sb("qmax_parts", [128, 4], ALWAYS)
        qmax, qs, qinv = (sb(n, [128, 3], ALWAYS) for n in ("qmax", "qs", "qinv"))
        slog = sb("slog", [128, 1], ALWAYS)
        pmax = sb("pmax", [128, 1], ALWAYS)
        ps_ = sb("ps_", [128, 2], ALWAYS)
        omax_parts = sb("omax_parts", [128, 4], ALWAYS)
        omax = sb("omax", [128, 1], ALWAYS)
        os_ = sb("os_", [128, 5], ALWAYS)
        (eneg, eneg1, score, less, tie, total, total_e, total_i, rank, rest, weight) = (
            sb(n, [128, TILES], ALWAYS) for n in
            ("eneg", "eneg1", "score", "less", "tie", "total", "total_e", "total_i", "rank", "rest", "weight"))

        ident = sb("ident", [128, 128], ALWAYS)
        zeros = sb("zeros", [128, 128], ALWAYS)
        ident_b = sb("ident_b", [128, 128], (PATCHES, ATTEND2), bf16)
        consts = sb("consts", [128, const_at("")[1]], (PATCHES, ATTEND3))
        rows = sb("rows", [128, len(ROWS), DIM], ALWAYS)
        cols = sb("cols", [HALF, len(COLS), 2], ALWAYS)
        cols_ff = sb("cols_ff", [128, 2, MLP_CHUNKS], ALWAYS)
        br = sb("br", [128, 1], ALWAYS)
        router_g = sb("router_g", [128, DIM], (FF, PROJ))
        weighed_b = sb("weighed_b", [128, DIM], (FF, FF))
        router_c = sb("router_c", [128, 1], ALWAYS)
        router_bias = sb("router_bias", [128, 1], ALWAYS)
        logit = sb("logit", [128, TILES], ALWAYS)
        W1 = sb("W1", [HALF, 2, MLP], ALWAYS)
        W2 = sb("W2", [128, MLP_CHUNKS, DIM], ALWAYS)
        w_ffn = sb("w_ffn", [HALF, 5, 2, DIM], (PATCHES, ATTEND3))
        w_ff1 = sb("w_ff1", [HALF, 2, MLP], (PATCHES, FF))
        w_ff2 = sb("w_ff2", [128, MLP_CHUNKS, DIM], (PATCHES, FF))
        w_out = sb("w_out", [128, INNER_CHUNKS, DIM], (PATCHES, OUT))
        w_qkv2 = sb("w_qkv2", [HALF, 2, 3 * DIM], (PATCHES, OUT))
        w_proj = sb("w_proj", [128, 3, DIM], (PATCHES, OUT))
        w_qkv = sb("w_qkv", [HALF, 2, 3 * INNER], (PATCHES, ATTEND))
        xT = sb("xT", [128, TILES, PATCH_CHUNKS, TILE], (PATCHES, PATCHES))
        w_patch = sb("w_patch", [128, PATCH_CHUNKS, DIM], (PATCHES, PATCHES))

        def const(name):
            a, b = const_at(name)
            return consts[:, a:b]

        def row(name):
            return rows[:, ROWS.index(name), :]

        def col(name, chunk):
            return cols[:, COLS.index(name), chunk:chunk + 1]

        same, before = const("same"), const("before")
        pick_at = const("pick").rearrange("p (t n) -> p t n", t=TILES)
        head_mask = const("head")[0:HALF, :]

        xhat = sb("xhat", [128, TILES, DIM], ALWAYS)
        t1 = sb("t1", [128, TILES, DIM], (PATCHES, OUT))
        t1b = sb("t1b", [128, TILES, DIM], (QKV, OUT))
        hT = sb("hT", [HALF, 2, ALL], (QKV, ATTEND))
        qkT = sb("qkT", [128, 2 * INNER_CHUNKS, ALL], (QKV, ATTEND))
        v1 = sb("v1", [128, TILES, INNER], (QKV, OUT))
        p1 = sb("p1", [128, TILES, 2, 6, TOKENS], (QKV, OUT))
        pT1 = sb("pT1", [128, TILES, 2, 3, 128], (ATTEND, OUT))
        oT1 = sb("oT1", [128, INNER_CHUNKS, TILES, PER_TILE, TOKENS], (ATTEND, OUT))
        t2 = sb("t2", [128, TILES, DIM], (OUT, FF))
        t2b = sb("t2b", [128, TILES, DIM], (OUT, FF))
        h2T = sb("h2T", [HALF, 2, ALL], (OUT, FF))
        ff = sb("ff", [128, MLP_CHUNKS, ALL], (FF, FF))
        h1 = sb("h1", [128, TILES, DIM], (FF, PROJ))
        h1b = sb("h1b", [128, TILES, DIM], (QUANT, PROJ))

        wqkv_r = sb("wqkv_r", [HALF, 2, 3 * DIM], (QKV, FF))
        wqkv_q = sb("wqkv_q", [HALF, 2, 3 * DIM], (QKV, QUANT), bf16)
        wproj_r = sb("wproj_r", [128, 3, DIM], (QKV, FF))
        wproj_q = sb("wproj_q", [128, 3, DIM], (QKV, PROJ), bf16)
        hr = sb("hr", [128, TILES, DIM], (QUANT, QUANT))
        hq = sb("hq", [HALF, 2, ALL], (QUANT, QUANT), bf16)
        qk2 = sb("qk2", [HALF, 4, ALL], (QUANT, SCORES2))
        v2 = sb("v2", [128, TILES, DIM], (QUANT, ATTEND2))
        qk_r = sb("qk_r", [HALF, 4, ALL], (QUANT, SCORES2))
        q_q = sb("q_q", [HALF, 2, ALL], (QUANT, SCORES2), bf16)
        k_q = sb("k_q", [HALF, 2, ALL], (QUANT, SCORES2), bf16)
        k_heads = sb("k_heads", [HALF, CHUNK_HEADS, 2, ALL], (QUANT, SCORES2), bf16)
        v_r = sb("v_r", [128, TILES, DIM], (SCORES2, ATTEND2))
        v_q = sb("v_q", [128, TILES, HEADS, PAD], (QUANT, ATTEND2), bf16)
        q3h = sb("q3h", [HALF, 2, IMAGES, HEAD_ROWS], (QUANT, ATTEND3))
        e2 = sb("e2", [128, TILES, CHUNK_HEADS, PER_TILE, TOKENS], (SCORES2, ATTEND2))
        p2 = sb("p2", [128, TILES, CHUNK_HEADS, PER_TILE * TOKENS], (ATTEND2, ATTEND2))
        p2q = sb("p2q", [128, TILES, CHUNK_HEADS, PER_TILE * TOKENS], (ATTEND2, ATTEND2), bf16)
        pT2 = sb("pT2", [128, TILES, CHUNK_HEADS, 128], (ATTEND2, ATTEND2), bf16)
        o_r = sb("o_r", [128, 3, TILES, PER_TILE, TOKENS], (ATTEND2, PROJ))
        o_q = sb("o_q", [128, 3, TILES, PER_TILE, TOKENS], (ATTEND2, PROJ), bf16)

        zpre = sb("zpre", [128, TILES, DIM], (PROJ, ROUTE))
        z = sb("z", [128, TILES, DIM], (PROJ, END))
        zb = sb("zb", [128, TILES, DIM], (PROJ, END))
        nh = sb("nh", [128, TILES, DIM], (PROJ, ROUTE))
        ng = sb("ng", [128, TILES, DIM], (PROJ, ROUTE))
        n3 = sb("n3", [128, TILES, DIM], (PROJ, ATTEND3))
        nT = sb("nT", [HALF, 2, ALL], (PROJ, ATTEND3))
        weighed = sb("weighed", [128, TILES, DIM], (PROJ, PROJ))
        score_b = sb("score_b", [128, TILES, 128], (ROUTE, ROUTE))
        below = sb("below", [128, TILES, 128], (ROUTE, ROUTE))
        equal = sb("equal", [128, TILES, 128], (ROUTE, ROUTE))
        sTm = sb("sTm", [128, TILES, 128], (ROUTE, ROUTE))
        mixer = sb("mixer", [128, TILES, 128], (ROUTE, ATTEND3))
        picked = sb("picked", [128, TILES, ALL_PICKED], (ROUTE, ATTEND3))
        pickedT = sb("pickedT", [ALL_PICKED, ALL], (ROUTE, ATTEND3))
        mixT = sb("mixT", [HALF, 2, ALL], (ROUTE, ATTEND3))
        nselT = sb("nselT", [HALF, 2, ALL_PICKED], (ROUTE, ATTEND3))
        q3 = sb("q3", [HALF, 2, IMAGES, PICKED], (ROUTE, ATTEND3))
        k3 = sb("k3", [HALF, 2, ALL], (ROUTE, ATTEND3))
        v3 = sb("v3", [128, TILES, DIM], (ROUTE, ATTEND3))
        p3 = sb("p3", [128, IMAGES, TOKENS], (ATTEND3, ATTEND3))
        pT3 = sb("pT3", [128, TILES, 128], (ATTEND3, ATTEND3))
        o3m = sb("o3m", [HALF, PER_TILE, 2 * TILES, CHUNK_HEADS * PICKED], (ATTEND3, ATTEND3))
        o3T = sb("o3T", [HALF, 2, PER_TILE, TILES, PICKED], (ATTEND3, ATTEND3))
        a3 = sb("a3", [ALL_PICKED, DIM], (ATTEND3, ATTEND3))
        mixb = sb("mixb", [128, TILES, DIM], (ATTEND3, ATTEND3))
        mixz = sb("mixz", [128, TILES, DIM], (ATTEND3, ATTEND3))
        h4 = sb("h4", [128, TILES, DIM], (ATTEND3, END))
        h4z = sb("h4z", [128, TILES, DIM], (ATTEND3, END))
        h5T = sb("h5T", [HALF, 2, ALL], (FF3, END))
        ff3 = sb("ff3", [128, MLP_CHUNKS, ALL], (FF3, END))
        ypre = sb("ypre", [128, TILES, DIM], (END, END))
        y = sb("y", [128, TILES, DIM], (END, END))

        pairs = [ctx.enter_context(nc.psum_tensor(f"pair{i}", [128, 2, 512], f32)) for i in range(4)]

        def bank(i):
            return pairs[i // 2][:, i % 2, :]

        def split_chunks(ap):
            return ap[0:HALF, 0:2 * TILE].rearrange("p (c n) -> p c n", c=2)

        def tokens(t):
            return slice(t * TILE, (t + 1) * TILE)

        def image(t, i):
            return slice((PER_TILE * t + i) * TOKENS, (PER_TILE * t + i + 1) * TOKENS)

        def own_picks(ap, t):
            return ap.rearrange("p (i t q) -> p i t q", i=PER_TILE, t=TILES)[:, :, t, :]

        def place1(h):
            chunk, r = h // 2, h % 2
            return r, (chunk + r) % 2, chunk // 2

        ld_x = [sem(f"ld_x{t}") for t in range(TILES)]
        ld_x0 = [sem(f"ld_x0_{g}") for g in range(3)]
        ld_wp = [sem(f"ld_wp{g}") for g in range(3)]
        ld = {n: sem("ld_" + n) for n in ("ident", "const", "rows", "rows_tok", "row0", "cols", "cols_ff", "w_q", "w_k", "w_v", "w_out", "w_ff1", "w_ff2",
                                          "w_qkv2", "w_proj", "w_ffn", "W1", "W2")}
        pe = {n: sem("pe_" + n) for n in (
            "patch", "xhatT", "qk", "scores", "v", "pT", "o", "out", "x2T", "ff1", "ff2", "wide",
            "hT", "qk2", "v2", "scores2", "pT2", "o2", "proj", "scoreT", "nT", "k3", "v3", "mixT", "nsel",
            "pickT", "q3", "mix", "scores3", "pT3", "o3", "a3", "spread", "x4T", "W1", "W2")}
        mk = {n: sem("mk_" + n) for n in (
            "t1", "var", "rstd", "xhat", "hT", "qk", "sub", "exp", "p", "v", "pT", "oT", "t2", "h2T", "gelu", "h1",
            "spread", "scale", "wscale", "t1b", "t2b", "wq", "hr", "hq", "qk2", "v2", "qkr", "qq", "kq", "kd", "ka",
            "or", "vr", "vq", "sub2", "exp2", "f2", "p2_last", "p2", "pT2", "oq", "h1b", "zpre", "z", "nh", "rstd_n", "n3", "router", "logit", "eneg", "score_b", "mixer",
            "picked", "nT", "k3", "v3", "mixT", "nselT", "pickT", "q3", "q3h", "sub3", "exp3", "p3", "pT3", "o3T", "a3",
            "mixz", "h4", "zb", "h4z", "h5T", "gelu3", "ypre", "y", "zero", "zeros", "identb", "cmp")}
        dve_step, act_step, pool_step = sem("dve_step"), sem("act_step"), sem("pool_step")
        stored = sem("stored")

        GROUPS = [[0], [1], [2], [3], [0, 1], [2, 3], [0, 1], [2, 3], [0, 1], [2, 3], [0], [1], [2], [3]]
        LN1, LN2, LNZ, LN4, LNY = 0, 4, 6, 8, 10
        MAX_W, MAX_H, MAX_QKV, MAX_P, MAX_O = range(5)
        MAX_WIDTH = [2, 1, 3, 1, 1]
        V_PAIR = [0, 1, 0, 1]
        OUT_BANK = [6, 7, 4, 5]
        NT_BANK = [0, 1, 3, 4]
        WARM = [8, 8, 3, 8, 9, 5, 8]

        block = ctx.enter_context(nc.Block())

        @block.sync
        def _(sp):
            third = PATCH_CHUNKS // 3
            for g in range(3):
                cc = slice(g * third, (g + 1) * third)
                sp.dma_start(w_patch[:, cc], A["w_patch"][:, cc]).then_inc(ld_wp[g], 16)
                sp.dma_start(xT[:, 0, cc], A["xT"][:, 0, cc]).then_inc(ld_x0[g], 16)
            for t in range(1, TILES):
                sp.dma_start(xT[:, t], A["xT"][:, t]).then_inc(ld_x[t], 16)
                if t == 1:
                    sp.dma_start(ident[:], A["ident"]).then_inc(ld["ident"], 16)
            for m, name in enumerate(("w_q", "w_k", "w_v")):
                part = slice(m * INNER, (m + 1) * INNER)
                sp.dma_start(w_qkv[:, :, part], A["w_qkv"][:, :, part]).then_inc(ld[name], 16)
            sp.dma_start(w_qkv2[:], A["w_qkv2"]).then_inc(ld["w_qkv2"], 16)
            sp.wait_ge(mk["zero"], 1)
            for r in range(4):
                sp.dma_start(w_proj[PAD * r:PAD * r + HEAD], A["w_proj"][r]).then_inc(ld["w_proj"], 16)
            sp.dma_start(consts[:], A["consts"]).then_inc(ld["const"], 16)
            sp.dma_start(cols_ff[:], A["cols_ff"]).then_inc(ld["cols_ff"], 16)
            sp.dma_start(rows[:, 1:3], A["rows"][1:3].rearrange("(a r) n -> a r n", a=1)
                         .to_broadcast([128, 2, DIM])).then_inc(ld["rows_tok"], 16)
            sp.dma_start(w_out[:], A["w_out"]).then_inc(ld["w_out"], 16)
            sp.dma_start(w_ff1[:], A["w_ff1"]).then_inc(ld["w_ff1"], 16)
            sp.dma_start(w_ff2[:], A["w_ff2"]).then_inc(ld["w_ff2"], 16)
            sp.dma_start(rows[:, 3:], A["rows"][3:].rearrange("(a r) n -> a r n", a=1)
                         .to_broadcast([128, len(ROWS) - 3, DIM])).then_inc(ld["rows"], 16)
            sp.dma_start(br[:], A["br"].to_broadcast([128, 1])).then_inc(ld["rows"], 16)
            sp.dma_start(w_ffn[:], A["w_ffn"]).then_inc(ld["w_ffn"], 16)
            sp.dma_start(W1[:], A["W1"]).then_inc(ld["W1"], 16)
            sp.dma_start(W2[:], A["W2"]).then_inc(ld["W2"], 16)
            for t in range(TILES):
                sp.wait_ge(mk["y"], t + 1)
                sp.dma_start(out[tokens(t), :], y[:, t]).then_inc(stored, 16)
            sp.wait_ge(stored, 16 * TILES)

        @block.tensor
        def _(te):
            mm = nc.tensor.matmul

            def turn(dst, src, parts):
                return nc.tensor.transpose(dst, src, ident[0:parts, 0:parts])

            def turn_tile(src, t, where):
                for c in range(2):
                    last = turn(bank(where)[0:HALF, c * TILE:(c + 1) * TILE],
                                src[:, t, c * HALF:(c + 1) * HALF], 128)
                return last

            def keep_warm(products, where):
                for _ in range(products):
                    mm(bank(where)[:, 0:128], zeros[:], zeros[:], start=True, stop=True)

            def turn_spread(nth, where):
                te.wait_ge(mk["spread"], nth + 1)
                for k in range(MAX_WIDTH[nth]):
                    last = turn(bank(where)[:, k * 128:(k + 1) * 128], spread[:, k, :], 128)
                last.then_inc(pe["wide"], 1)

            def turn_h(t):
                if t == 0:
                    te.wait_ge(ld["ident"], 16)
                te.wait_ge(mk["xhat"], t + 1)
                turn_tile(xhat, t, 4 + t).then_inc(pe["xhatT"], 1)

            te.wait_ge(mk["zeros"], 1)
            keep_warm(WARM[6], 7)
            for t in range(TILES):
                if t >= 2:
                    turn_h(t - 2)
                if t > 0:
                    te.wait_ge(ld_x[t], 16)
                for c in range(PATCH_CHUNKS):
                    if t == 0 and c % 2 == 0:
                        te.wait_ge(ld_wp[c // 2], 16)
                        te.wait_ge(ld_x0[c // 2], 16)
                    last = mm(bank(t)[:, 0:DIM], xT[:, t, c, :], w_patch[:, c, :],
                              start=(c == 0), stop=(c == PATCH_CHUNKS - 1))
                last.then_inc(pe["patch"], 1)
            turn_h(2)

            def project_qk(half):
                te.wait_ge(mk["hT"], 2 * half + 2)
                for m in range(2 * INNER_CHUNKS):
                    n = half * 2 * INNER_CHUNKS + m
                    if n == INNER_CHUNKS:
                        turn_h(3)
                        te.wait_ge(ld["w_k"], 16)
                    if n >= 4:
                        te.wait_ge(mk["qk"], n - 3)
                    for c in range(2):
                        last = mm(bank(n % 4)[:, 0:256], w_qkv[:, c, m * 128:(m + 1) * 128],
                                  hT[:, c, half * 256:(half + 1) * 256], start=(c == 0), stop=(c == 1))
                    last.then_inc(pe["qk"], 1)

            def scores(t):
                te.wait_ge(mk["qk"], 2 * INNER_CHUNKS * (t // 2 + 1))
                if t >= 2:
                    te.wait_ge(mk["sub"], t - 1)
                for h2 in range(INNER_CHUNKS):
                    for i in range(PER_TILE):
                        for r in range(2):
                            where, half, slot = place1(2 * h2 + r)
                            rr = slice(64 * r, 64 * r + 64)
                            last = mm(pairs[2 + t % 2][64 * half:64 * half + 64, where,
                                                       slot * 128 + 64 * i:slot * 128 + 64 * i + 64],
                                      qkT[rr, h2, image(t, i)], qkT[rr, INNER_CHUNKS + h2, image(t, i)],
                                      start=True, stop=True)
                last.then_inc(pe["scores"], 1)

            def project_v(t):
                te.wait_ge(mk["qk"], 2 * INNER_CHUNKS * (t // 2 + 1) - 2 * (1 - t % 2))
                for g in range(2):
                    for c in range(2):
                        last = mm(pairs[V_PAIR[t]][:, g, 0:384], hT[:, c, tokens(t)],
                                  w_qkv[:, c, 2 * INNER + g * 384:2 * INNER + (g + 1) * 384],
                                  start=(c == 0), stop=(c == 1))
                last.then_inc(pe["v"], 1)

            te.wait_ge(ld["w_q"], 16)
            te.wait_ge(mk["t1"], 4)
            project_qk(0)
            te.wait_ge(mk["hT"], 4)
            turn_spread(MAX_W, 7)
            te.wait_ge(ld["w_v"], 16)
            project_v(0)
            project_v(1)
            scores(0)
            te.wait_ge(mk["wscale"], 1)
            scores(1)
            te.wait_ge(mk["v"], 2)
            project_qk(1)

            def turn_p(t):
                te.wait_ge(mk["p"], t + 1)
                if t < 2:
                    te.wait_ge(mk["v"], t + 3)
                if t >= 2:
                    te.wait_ge(mk["oT"], t - 1)
                for r in range(2):
                    for m in range(3):
                        last = turn(pairs[t % 2][:, r, m * 128:(m + 1) * 128],
                                    p1[:, t, r, 2 * m:2 * m + 2, :].rearrange("p a j -> p (a j)"), 128)
                last.then_inc(pe["pT"], 1)

            def attend(t):
                te.wait_ge(mk["v"], t + 1)
                te.wait_ge(mk["pT"], t + 1)
                for h2 in range(INNER_CHUNKS):
                    for r in range(2):
                        where, half, slot = place1(2 * h2 + r)
                        for i in range(PER_TILE):
                            ii = slice(64 * i, 64 * i + 64)
                            h = 2 * h2 + r
                            last = mm(pairs[t % 2][64 * r:64 * r + 64, i, h2 * 64:(h2 + 1) * 64],
                                      v1[ii, t, h * 64:(h + 1) * 64],
                                      pT1[ii, t, where, slot, 64 * half:64 * half + 64], start=True, stop=True)
                last.then_inc(pe["o"], 1)

            def turn_half(half, normed, turned):
                for t in (2 * half, 2 * half + 1):
                    te.wait_ge(mk["xhat"], normed + t + 1)
                    turn_tile(xhat, t, t).then_inc(turned, 1)

            def project_out(t):
                te.wait_ge(mk["oT"], t + 1)
                for c in range(INNER_CHUNKS):
                    last = mm(bank(OUT_BANK[t])[:, 0:DIM], oT1[:, c, t].rearrange("p i n -> p (i n)"), w_out[:, c, :],
                              start=(c == 0), stop=(c == INNER_CHUNKS - 1))
                last.then_inc(pe["out"], 1)

            project_v(2)
            project_v(3)
            scores(2)
            turn_p(0)
            scores(3)
            turn_p(1)
            attend(0)
            attend(1)
            te.wait_ge(ld["w_out"], 16)
            te.wait_ge(mk["sub"], 4)
            turn_p(2)
            project_out(0)
            turn_p(3)
            attend(2)
            project_out(1)
            attend(3)
            project_out(2)
            te.wait_ge(mk["oT"], 4)
            turn_half(0, 4, pe["x2T"])
            project_out(3)

            def up(half, w, src, done, freed, normed, turned):
                for m in range(MLP_CHUNKS):
                    n = half * MLP_CHUNKS + m
                    if half == 0 and m == MLP_CHUNKS // 2:
                        turn_half(1, normed, turned)
                    if n >= 4:
                        te.wait_ge(freed, n - 3)
                    for c in range(2):
                        last = mm(bank(4 + n % 4)[:, 0:256], w[:, c, m * 128:(m + 1) * 128],
                                  src[:, c, half * 256:(half + 1) * 256], start=(c == 0), stop=(c == 1))
                    last.then_inc(done, 1)

            def down(t, w, src, done):
                for c in range(MLP_CHUNKS):
                    last = mm(bank(t)[:, 0:DIM], src[:, c, tokens(t)], w[:, c, :],
                              start=(c == 0), stop=(c == MLP_CHUNKS - 1))
                last.then_inc(done, 1)

            te.wait_ge(ld["w_ff1"], 16)
            te.wait_ge(ld["w_ff2"], 16)
            te.wait_ge(mk["t2"], 4)
            for half in range(2):
                te.wait_ge(mk["h2T"], 2 * half + 2)
                up(half, w_ff1, h2T, pe["ff1"], mk["gelu"], 4, pe["x2T"])
            for t in range(TILES):
                te.wait_ge(mk["gelu"], MLP_CHUNKS * (t // 2 + 1))
                down(t, w_ff2, ff, pe["ff2"])

            te.wait_ge(mk["gelu"], 2 * MLP_CHUNKS)
            turn_spread(MAX_H, 4)
            for t in range(TILES):
                te.wait_ge(mk["hr"], t + 1)
                turn_tile(hr, t, t).then_inc(pe["hT"], 1)
            te.wait_ge(mk["wq"], 2)
            te.wait_ge(mk["hq"], 4)
            te.wait_ge(mk["scale"], 2)
            for t in range(TILES):
                for c in range(2):
                    last = mm(bank(t)[:, 0:DIM], hq[:, c, tokens(t)], wqkv_q[:, c, 2 * DIM:3 * DIM],
                              start=(c == 0), stop=(c == 1))
                last.then_inc(pe["v2"], 1)
            for m in range(4):
                for c in range(2):
                    last = mm(bank(4 + m)[0:HALF, :], wqkv_q[:, c, m * HALF:(m + 1) * HALF], hq[:, c, :],
                              start=(c == 0), stop=(c == 1))
                last.then_inc(pe["qk2"], 1)
            te.wait_ge(mk["v2"], 4)
            turn_spread(MAX_QKV, 0)
            te.wait_ge(mk["scale"], 3)
            te.wait_ge(mk["qk2"], 4)
            te.wait_ge(mk["qq"], 1)
            te.wait_ge(mk["kd"], 4)
            te.wait_ge(mk["ka"], 2)
            for t in range(TILES):
                for i in range(PER_TILE):
                    for c in range(2):
                        last = mm(pairs[t][64 * c:64 * c + 64, i, 0:CHUNK_HEADS * TOKENS], q_q[:, c, image(t, i)],
                                  k_heads[:, :, c, image(t, i)], start=True, stop=True)
                last.then_inc(pe["scores2"], 1)
            te.wait_ge(mk["sub2"], 4)
            turn_spread(MAX_P, 0)
            te.wait_ge(mk["identb"], 1)
            te.wait_ge(mk["vq"], 1)

            def turn_p2(t):
                te.wait_ge(mk["p2"], t + 1)
                dst = bank(t).bitcast(bf16)
                for h in range(CHUNK_HEADS):
                    last = nc.tensor.transpose(dst[:, h * 128:(h + 1) * 128], p2q[:, t, h, :], ident_b[:, :])
                last.then_inc(pe["pT2"], 1)

            def attend2(t):
                te.wait_ge(mk["pT2"], t + 1)
                for h in range(HEADS):
                    for i in range(PER_TILE):
                        ii = slice(64 * i, 64 * i + 64)
                        half, slot = h // CHUNK_HEADS, h % CHUNK_HEADS
                        r = h % 4
                        at = (t % 2) * 192 + (h // 4) * 64
                        last = mm(pairs[2 + i][32 * r:32 * r + 32, t // 2, at:at + 64],
                                  v_q[ii, t, h, :], pT2[ii, t, slot, 64 * half:64 * half + 64],
                                  start=True, stop=True)
                last.then_inc(pe["o2"], 1)

            turn_p2(0)
            turn_p2(1)
            attend2(0)
            turn_p2(2)
            attend2(1)
            turn_p2(3)
            attend2(2)
            attend2(3)
            te.wait_ge(mk["pT2"], 4)
            turn_spread(MAX_O, 0)
            for t in range(TILES):
                te.wait_ge(mk["oq"], t // 2 + 1)
                for c in range(3):
                    last = mm(bank(t)[:, 0:DIM], o_q[:, c, t].rearrange("p i n -> p (i n)"), wproj_q[:, c, :],
                              start=(c == 0), stop=(c == 2))
                last.then_inc(pe["proj"], 1)

            WQ, WK, WV, WO, WM = range(5)
            te.wait_ge(mk["oq"], 2)
            keep_warm(WARM[0], 7)
            for t in range(TILES):
                te.wait_ge(mk["nh"], t + 1)
                turn_tile(nh, t, NT_BANK[t]).then_inc(pe["nT"], 1)
            keep_warm(WARM[1], 7)
            te.wait_ge(mk["score_b"], 1)
            for t in range(TILES):
                last = turn(bank(2)[:, tokens(t)], score_b[:, t, :], 128)
            last.then_inc(pe["scoreT"], 1)
            keep_warm(WARM[2], 7)
            te.wait_ge(ld["w_ffn"], 16)
            te.wait_ge(mk["nT"], 4)
            for m in range(2):
                for c in range(2):
                    last = mm(bank(m)[0:HALF, :], w_ffn[:, WK, c, m * HALF:(m + 1) * HALF], nT[:, c, :],
                              start=(c == 0), stop=(c == 1))
                last.then_inc(pe["k3"], 1)

            def project_v3(t):
                for c in range(2):
                    last = mm(bank(4 + t)[:, 0:DIM], nT[:, c, tokens(t)], w_ffn[:, WV, c, :],
                              start=(c == 0), stop=(c == 1))
                last.then_inc(pe["v3"], 1)

            project_v3(0)
            te.wait_ge(mk["n3"], 4)
            for t in range(TILES):
                te.wait_ge(mk["picked"], t + 1)
                for c in range(2):
                    last = mm(own_picks(bank(3)[0:HALF, c * ALL_PICKED:(c + 1) * ALL_PICKED], t),
                              n3[:, t, c * HALF:(c + 1) * HALF], own_picks(picked[:, t, :], t), start=True, stop=True)
            last.then_inc(pe["nsel"], 1)
            te.wait_ge(mk["k3"], 2)
            for t in range(TILES):
                last = turn(bank(0)[0:ALL_PICKED, tokens(t)], picked[:, t, :], 128)
            last.then_inc(pe["pickT"], 1)
            te.wait_ge(mk["nselT"], 1)
            for m in range(2):
                for c in range(2):
                    last = mm(bank(1)[0:HALF, m * ALL_PICKED:(m + 1) * ALL_PICKED],
                              w_ffn[:, WQ, c, m * HALF:(m + 1) * HALF], nselT[:, c, :],
                              start=(c == 0), stop=(c == 1))
            last.then_inc(pe["q3"], 1)
            project_v3(1)
            project_v3(2)

            def mix(t):
                te.wait_ge(mk["v3"], t + 1)
                te.wait_ge(mk["mixer"], t + 1)
                for c in range(2):
                    last = mm(bank(4 + t)[0:HALF, c * TILE:(c + 1) * TILE], n3[:, t, c * HALF:(c + 1) * HALF],
                              mixer[:, t, :], start=True, stop=True)
                last.then_inc(pe["mixT"], 1)

            te.wait_ge(mk["q3h"], 2)
            for n in range(IMAGES):
                t, i = n % TILES, n // TILES
                for c in range(2):
                    last = mm(bank(3)[64 * c:64 * c + 64, image(t, i)], q3h[:, c, n, :],
                              k3[:, c, image(t, i)], start=True, stop=True)
            last.then_inc(pe["scores3"], 1)
            project_v3(3)
            for t in range(TILES):
                mix(t)
            for t in range(TILES):
                te.wait_ge(mk["mixT"], t + 1)
                for c in range(2):
                    last = mm(bank(4 + t)[:, 0:DIM], mixT[:, c, tokens(t)], w_ffn[:, WM, c, :],
                              start=(c == 0), stop=(c == 1))
                last.then_inc(pe["mix"], 1)
            te.wait_ge(mk["p3"], 1)
            for t in range(TILES):
                last = turn(bank(2)[:, tokens(t)], p3[:, 2 * t:2 * t + 2, :].rearrange("p i j -> p (i j)"), 128)
            last.then_inc(pe["pT3"], 1)
            te.wait_ge(mk["pickT"], 1)
            te.wait_ge(mk["pT3"], 1)
            for t in range(TILES):
                for c in range(2):
                    for i in range(PER_TILE):
                        ii = slice(64 * i, 64 * i + 64)
                        last = mm(bank(i)[0:HALF, (TILES * c + t) * 64:(TILES * c + t) * 64 + 60],
                                  v3[ii, t, c * HALF:(c + 1) * HALF], pT3[ii, t, 64 * c:64 * c + 60],
                                  start=True, stop=True)
            last.then_inc(pe["o3"], 1)
            te.wait_ge(mk["sub3"], 1)
            keep_warm(WARM[3], 3)
            te.wait_ge(mk["o3T"], 2)
            for c in range(2):
                last = mm(bank(3)[0:ALL_PICKED, 0:DIM], o3T[:, c].rearrange("p i t q -> p (i t q)"),
                          w_ffn[:, WO, c, :], start=(c == 0), stop=(c == 1))
            last.then_inc(pe["a3"], 1)
            te.wait_ge(mk["a3"], 1)
            for t in range(TILES):
                te.wait_ge(mk["mixz"], t + 1)
                mm(bank(4 + t)[:, 0:DIM], pickedT[:, tokens(t)], a3[:, :], start=True, stop=True).then_inc(pe["spread"], 1)
            te.wait_ge(ld["W1"], 16)
            te.wait_ge(ld["W2"], 16)
            keep_warm(WARM[4], 3)
            turn_half(0, 8, pe["x4T"])
            te.wait_ge(mk["h4"], 4)
            keep_warm(WARM[5], 7)
            for half in range(2):
                te.wait_ge(mk["h5T"], 2 * half + 2)
                up(half, W1, h5T, pe["W1"], mk["gelu3"], 8, pe["x4T"])
            for t in range(TILES):
                te.wait_ge(mk["gelu3"], MLP_CHUNKS * (t // 2 + 1))
                down(t, W2, ff3, pe["W2"])

        @block.gpsimd
        def _(pool):
            steps = [0]

            def step(ins):
                steps[0] += 1
                ins.then_inc(pool_step, 1)
                pool.wait_ge(pool_step, steps[0])

            def inverse_deviation(group):
                tt = GROUPS[group]
                pool.wait_ge(mk["var"], group + 1)
                nc.gpsimd.tensor_tensor(rstd[:, tt[0]:tt[-1] + 1], var_eps[:, tt[0]:tt[-1] + 1],
                                        power[:, 0:len(tt)], ALU.pow).then_inc(mk["rstd"], 1)

            nc.gpsimd.memset(w_proj[:], 0.0).then_inc(mk["zero"], 1)
            nc.gpsimd.memset(wmax[:], 0.0).then_inc(mk["zero"], 1)
            nc.gpsimd.memset(qmax[:], 0.0).then_inc(mk["zero"], 1)
            nc.gpsimd.memset(round_bias[:], ROUND).then_inc(mk["zero"], 1)
            step(nc.gpsimd.memset(power[:], -0.5))
            pool.wait_ge(ld["ident"], 16)
            nc.gpsimd.tensor_copy(ident_b[:], ident[:]).then_inc(mk["identb"], 1)
            for t in range(TILES):
                inverse_deviation(LN1 + t)
            pool.wait_ge(ld["rows_tok"], 16)
            for t in range(TILES):
                nc.gpsimd.tensor_tensor(t1b[:, t], t1[:, t], row("b_out"), ALU.add).then_inc(mk["t1b"], 1)
            pool.wait_ge(mk["wscale"], 1)
            step(nc.gpsimd.tensor_scalar(wqkv_r[:], w_qkv2[:], winv[0:HALF, 0:1], ROUND, ALU.mult, ALU.add))
            nc.gpsimd.tensor_scalar(wqkv_q[:], wqkv_r[:], -ROUND, None, ALU.add).then_inc(mk["wq"], 1)
            step(nc.gpsimd.tensor_scalar(wproj_r[:], w_proj[:], winv[:, 1:2], ROUND, ALU.mult, ALU.add))
            nc.gpsimd.tensor_scalar(wproj_q[:], wproj_r[:], -ROUND, None, ALU.add).then_inc(mk["wq"], 1)
            pool.wait_ge(ld["rows"], 32)
            for g in range(2):
                inverse_deviation(LN2 + g)
                for t in (2 * g, 2 * g + 1):
                    nc.gpsimd.tensor_tensor(t2b[:, t], t2[:, t], row("b_ff2"), ALU.add).then_inc(mk["t2b"], 1)
            for t in range(TILES):
                pool.wait_ge(mk["h1"], t + 1)
                nc.gpsimd.tensor_tensor(h1b[:, t], h1[:, t], row("b_proj"), ALU.add).then_inc(mk["h1b"], 1)
            step(nc.gpsimd.memset(v_q[:], 0.0))
            step(nc.gpsimd.memset(q3h[:], 0.0))
            pool.wait_ge(mk["scale"], 3)
            step(nc.gpsimd.tensor_scalar(v_r[:], v2[:], qinv[:, 2:3], ROUND, ALU.mult, ALU.add))
            nc.gpsimd.tensor_scalar(v_q[:, :, :, 0:HEAD], v_r[:].rearrange("p t (h d) -> p t h d", d=HEAD), -ROUND, None,
                                    ALU.add).then_inc(mk["vq"], 1)
            pool.wait_ge(mk["f2"], 1)
            nc.gpsimd.tensor_tensor(p2[:, TILES - 1].rearrange("p h (i j) -> p (h i) j", j=TOKENS),
                                    e2[:, TILES - 1].rearrange("p h i j -> p (h i) j"),
                                    f2[:, TILES - 1].unsqueeze(2).to_broadcast([128, HEADS, TOKENS]),
                                    ALU.mult).then_inc(mk["p2_last"], 1)
            for g in range(2):
                pool.wait_ge(mk["var"], LNZ + g + 1)
                nc.gpsimd.tensor_tensor(rstd_n[:, 2 * g:2 * g + 2], var_n[:, 2 * g:2 * g + 2], power[:, 0:2],
                                        ALU.pow).then_inc(mk["rstd_n"], 1)
                inverse_deviation(LNZ + g)
            for t in range(TILES):
                pool.wait_ge(mk["nh"], t + 1)
                step(nc.gpsimd.tensor_tensor(ng[:, t], nh[:, t], row("g1"), ALU.mult))
                nc.gpsimd.tensor_tensor(n3[:, t], ng[:, t], row("b1"), ALU.add).then_inc(mk["n3"], 1)
            for t in range(TILES):
                pool.wait_ge(mk["z"], t + 1)
                nc.gpsimd.tensor_tensor(zb[:, t], z[:, t], row("bf2"), ALU.add).then_inc(mk["zb"], 1)
            for g in range(2):
                inverse_deviation(LN4 + g)
                for t in (2 * g, 2 * g + 1):
                    pool.wait_ge(mk["zb"], t + 1)
                    nc.gpsimd.tensor_tensor(h4z[:, t], h4[:, t], zb[:, t], ALU.add).then_inc(mk["h4z"], 1)
            for t in range(TILES):
                inverse_deviation(LNY + t)

        @block.scalar
        def _(act):
            act.dma_start(rows[:, 0:1], A["rows"][0:1].rearrange("(a r) n -> a r n", a=1)
                          .to_broadcast([128, 1, DIM])).then_inc(ld["row0"], 16)
            act.dma_start(cols[:], A["cols"]).then_inc(ld["cols"], 16)

            def from_chunks(t, where, dst, scale, bias, done):
                for c in range(2):
                    last = nc.scalar.activation(dst[:, c, tokens(t)], split_chunks(bank(where))[:, c, :], ACT.Identity,
                                                scale=col(scale, c), bias=col(bias, c))
                last.then_inc(done, 1)

            def keep_h(t):
                act.wait_ge(pe["xhatT"], t + 1)
                from_chunks(t, 4 + t, hT, "g1", "beta1", mk["hT"])

            act.wait_ge(ld["cols"], 16)
            for t in range(TILES - 1):
                keep_h(t)

            def keep_qk(half):
                for m in range(2 * INNER_CHUNKS):
                    n = half * 2 * INNER_CHUNKS + m
                    if n == INNER_CHUNKS:
                        keep_h(TILES - 1)
                    act.wait_ge(pe["qk"], n + 1)
                    nc.scalar.activation(qkT[:, m, half * 256:(half + 1) * 256], bank(n % 4)[:, 0:256],
                                         ACT.Copy).then_inc(mk["qk"], 1)

            def exp1(t):
                act.wait_ge(mk["sub"], t + 1)
                nc.scalar.activation(p1[:, t], p1[:, t], ACT.Exp, scale=HEAD1 ** -0.5).then_inc(mk["exp"], 1)

            def keep_pT(t):
                act.wait_ge(pe["pT"], t + 1)
                nc.scalar.activation(pT1[:, t].rearrange("p r m n -> p r (m n)"), pairs[t % 2][:, :, 0:384],
                                     ACT.Copy).then_inc(mk["pT"], 1)

            def keep_o(t):
                act.wait_ge(pe["o"], t + 1)
                nc.scalar.activation(oT1[:, :, t].rearrange("p c i n -> p i c n"),
                                     pairs[t % 2][:, :, 0:384].rearrange("p i (c n) -> p i c n", n=TOKENS),
                                     ACT.Copy).then_inc(mk["oT"], 1)

            keep_qk(0)
            exp1(0)
            exp1(1)
            keep_qk(1)
            keep_pT(0)
            exp1(2)
            keep_pT(1)
            exp1(3)
            keep_o(0)
            keep_o(1)
            keep_pT(2)
            keep_pT(3)
            keep_o(2)
            keep_o(3)

            def keep_half(half, turned, dst, scale, bias, done):
                for t in (2 * half, 2 * half + 1):
                    act.wait_ge(turned, t + 1)
                    from_chunks(t, t, dst, scale, bias, done)

            def gelus(half, src, dst, which, done, *second_half):
                for m in range(MLP_CHUNKS):
                    n = half * MLP_CHUNKS + m
                    if half == 0 and m == MLP_CHUNKS // 2:
                        keep_half(1, *second_half)
                    act.wait_ge(src, n + 1)
                    nc.scalar.activation(dst[:, m, half * 256:(half + 1) * 256], bank(4 + n % 4)[:, 0:256], ACT.Gelu,
                                         bias=cols_ff[:, which, m:m + 1]).then_inc(done, 1)

            act.wait_ge(ld["cols_ff"], 16)
            turned = (pe["x2T"], h2T, "g2", "beta2", mk["h2T"])
            keep_half(0, *turned)
            for half in range(2):
                gelus(half, pe["ff1"], ff, 0, mk["gelu"], *turned)

            for t in range(TILES):
                act.wait_ge(pe["hT"], t + 1)
                nc.scalar.activation(hq[:, :, tokens(t)], split_chunks(bank(t)), ACT.Copy,
                                     bias=-ROUND).then_inc(mk["hq"], 1)
            act.wait_ge(mk["scale"], 2)
            for m in range(4):
                act.wait_ge(pe["qk2"], m + 1)
                nc.scalar.activation(qk2[:, m, :], bank(4 + m)[0:HALF, :], ACT.Identity, scale=hs[0:HALF, 2:3],
                                     bias=col("bq2" if m < 2 else "bk2", m % 2)).then_inc(mk["qk2"], 1)
            act.wait_ge(mk["scale"], 3)
            nc.scalar.activation(qk_r[:, 0:2], qk2[:, 0:2], ACT.Identity, scale=qinv[0:HALF, 0:1],
                                 bias=round_bias[0:HALF, 0:1]).then_inc(mk["qkr"], 1)
            act.wait_ge(mk["kq"], 1)
            for h in range(4, CHUNK_HEADS):
                nc.scalar.activation(k_heads[:, h], k_q[:], ACT.Copy, scale=head_mask[:, h:h + 1]).then_inc(mk["ka"], 1)
            for t in range(TILES):
                act.wait_ge(mk["sub2"], t + 1)
                nc.scalar.activation(e2[:, t], e2[:, t], ACT.Exp, scale=slog[:, 0:1]).then_inc(mk["exp2"], 1)
            for t in range(TILES):
                act.wait_ge(pe["pT2"], t + 1)
                nc.scalar.activation(pT2[:, t].rearrange("p h n -> p (h n)"), bank(t).bitcast(bf16)[:, 0:768],
                                     ACT.Copy).then_inc(mk["pT2"], 1)
            act.wait_ge(mk["scale"], 4)
            for g in range(2):
                nc.scalar.activation(o_r[:, :, 2 * g:2 * g + 2, 1, :].rearrange("p c t n -> p t c n"),
                                     pairs[3][:, g, 0:384].rearrange("p (t c n) -> p t c n", t=2, c=3),
                                     ACT.Identity, scale=os_[:, 4:5], bias=round_bias[:, 0:1]).then_inc(mk["or"], 1)

            for t in range(TILES):
                if t == 2:
                    act.wait_ge(mk["router"], 2)
                    act.wait_ge(mk["logit"], TILES)
                    nc.scalar.activation(eneg[:], logit[:], ACT.Exp, scale=-1.0,
                                         bias=router_bias[:]).then_inc(mk["eneg"], 1)
                act.wait_ge(pe["nT"], t + 1)
                from_chunks(t, NT_BANK[t], nT, "ffn_g1", "ffn_b1", mk["nT"])
            for m in range(2):
                act.wait_ge(pe["k3"], m + 1)
                nc.scalar.activation(k3[:, m, :], bank(m)[0:HALF, :], ACT.Identity, bias=col("bk3", m)).then_inc(mk["k3"], 1)
            act.wait_ge(pe["nsel"], 1)
            nc.scalar.activation(nselT[:].rearrange("p c n -> p (c n)"), bank(3)[0:HALF, 0:2 * ALL_PICKED],
                                 ACT.Copy).then_inc(mk["nselT"], 1)
            act.wait_ge(pe["pickT"], 1)
            nc.scalar.activation(pickedT[:], bank(0)[0:ALL_PICKED, :], ACT.Copy).then_inc(mk["pickT"], 1)
            act.wait_ge(pe["q3"], 1)
            for c in range(2):
                nc.scalar.activation(q3[:, c].rearrange("p n q -> p (n q)"),
                                     bank(1)[0:HALF, c * ALL_PICKED:(c + 1) * ALL_PICKED], ACT.Identity,
                                     bias=col("bq3", c)).then_inc(mk["q3"], 1)
            for t in range(TILES):
                act.wait_ge(pe["mixT"], t + 1)
                nc.scalar.activation(mixT[:, :, tokens(t)], split_chunks(bank(4 + t)), ACT.Copy).then_inc(mk["mixT"], 1)
            act.wait_ge(mk["sub3"], 1)
            nc.scalar.activation(p3[:], p3[:], ACT.Exp, scale=HEAD ** -0.5).then_inc(mk["exp3"], 1)
            act.wait_ge(pe["pT3"], 1)
            nc.scalar.activation(pT3[:].rearrange("p t n -> p (t n)"), bank(2), ACT.Copy).then_inc(mk["pT3"], 1)
            turned = (pe["x4T"], h5T, "ffn_g2", "ffn_b2", mk["h5T"])
            keep_half(0, *turned)
            for half in range(2):
                gelus(half, pe["W1"], ff3, 1, mk["gelu3"], *turned)

        @block.vector
        def _(dve):
            v = nc.vector
            steps = [0]

            def step(ins):
                steps[0] += 1
                ins.then_inc(dve_step, 1)
                dve.wait_ge(dve_step, steps[0])

            def wide(ap, n):
                return ap.unsqueeze(len(ap.shape)).to_broadcast(list(ap.shape) + [n])

            def statistics(group, src):
                tt = GROUPS[group]
                for t in tt:
                    last = v.bn_stats(stats[:, t], src[:, t])
                step(last)
                for t in tt:
                    last = v.bn_aggr(mv[:, t], stats[:, t])
                step(last)
                g = slice(tt[0], tt[-1] + 1)
                return v.tensor_scalar(var_eps[:, g], mv[:, g, 1], EPS, None, ALU.add)

            def centre(t, src, dst, factor):
                return v.tensor_scalar(dst[:, t], src[:, t], mv[:, t, 0:1], factor[:, t:t + 1], ALU.subtract, ALU.mult)

            def layernorm(group, src, dst, done):
                statistics(group, src).then_inc(mk["var"], 1)
                dve.wait_ge(mk["rstd"], group + 1)
                for t in GROUPS[group]:
                    centre(t, src, dst, rstd).then_inc(done, 1)

            def global_max(nth, maxima, dst, where):
                width = MAX_WIDTH[nth]
                if nth > 0:
                    dve.wait_ge(pe["wide"], nth)
                v.tensor_copy(spread[:, 0:width, :], wide(maxima, 128)).then_inc(mk["spread"], 1)
                dve.wait_ge(pe["wide"], nth + 1)
                step(v.tensor_reduce(dst, bank(where)[:, 0:width * 128].rearrange("p (k n) -> p k n", k=width), X, ALU.max))

            def scale_of(dst, maxima):
                return v.tensor_scalar(dst, maxima, 1.0 / QMAX, 1e-8, ALU.mult, ALU.max)

            v.memset(zeros[:], 0.0).then_inc(mk["zeros"], 1)
            dve.wait_ge(ld["row0"], 16)
            for t in range(TILES):
                dve.wait_ge(pe["patch"], t + 1)
                v.tensor_tensor(t1[:, t], bank(t)[:, 0:DIM], row("b_patch"), ALU.add).then_inc(mk["t1"], 1)
                dve.wait_ge(mk["t1"], t + 1)
                layernorm(LN1 + t, t1, xhat, mk["xhat"])
            dve.wait_ge(mk["zero"], 4)
            dve.wait_ge(ld["w_qkv2"], 16)
            dve.wait_ge(ld["w_proj"], 64)
            dve.wait_ge(ld["const"], 16)
            step(v.tensor_reduce(wmax[0:HALF, 0:1], w_qkv2[:].rearrange("p c n -> p (c n)"), X, ALU.max, apply_absolute_value=True))
            step(v.tensor_reduce(wmax[:, 1:2], w_proj[:].rearrange("p c n -> p (c n)"), X, ALU.max, apply_absolute_value=True))
            global_max(MAX_W, wmax[:], gm[:, 0:2], 7)
            step(scale_of(wscale[:], gm[:, 0:2]))
            v.reciprocal(winv[:], wscale[:]).then_inc(mk["wscale"], 1)

            def soft_scores(t):
                src = pairs[2 + t % 2][:, :, 0:384].rearrange("p r (s j) -> p r s j", j=TOKENS)
                m = mx1[:, t].rearrange("p (r s) -> p r s", r=2)
                dve.wait_ge(pe["scores"], t + 1)
                step(v.tensor_reduce(m, src, X, ALU.max))
                v.tensor_tensor(p1[:, t], src, wide(m, TOKENS), ALU.subtract).then_inc(mk["sub"], 1)

            def keep_v(t):
                dve.wait_ge(pe["v"], t + 1)
                v.tensor_copy(v1[:, t].rearrange("p (g n) -> p g n", g=2), pairs[V_PAIR[t]][:, :, 0:384]).then_inc(mk["v"], 1)

            def normalise(t):
                e = p1[:, t].rearrange("p r s j -> p (r s) j")
                dve.wait_ge(mk["exp"], t + 1)
                step(v.tensor_reduce(sum1[:, t], e, X, ALU.add))
                step(v.reciprocal(inv1[:, t], sum1[:, t]))
                v.tensor_tensor(e, e, wide(inv1[:, t], TOKENS), ALU.mult).then_inc(mk["p"], 1)

            keep_v(0)
            keep_v(1)
            soft_scores(0)
            soft_scores(1)
            normalise(0)
            normalise(1)
            keep_v(2)
            keep_v(3)
            soft_scores(2)
            soft_scores(3)
            normalise(2)
            normalise(3)

            for g in range(2):
                for t in (2 * g, 2 * g + 1):
                    dve.wait_ge(pe["out"], t + 1)
                    dve.wait_ge(mk["t1b"], t + 1)
                    v.tensor_tensor(t2[:, t], bank(OUT_BANK[t])[:, 0:DIM], t1b[:, t], ALU.add).then_inc(mk["t2"], 1)
                dve.wait_ge(mk["t2"], 2 * g + 2)
                layernorm(LN2 + g, t2, xhat, mk["xhat"])
            dve.wait_ge(ld["rows"], 32)
            v.tensor_tensor(router_g[:], row("g1"), row("Wr"), ALU.mult).then_inc(mk["router"], 1)
            step(v.scalar_tensor_tensor(out=weighed_b[:], in0=row("b1"), scalar=1.0, in1=row("Wr"),
                                        op0=ALU.mult, op1=ALU.mult, accum_out=router_c[:]))
            v.tensor_scalar(router_bias[:], router_c[:], br[:, 0:1], -1.0, ALU.add, ALU.mult).then_inc(mk["router"], 1)
            for t in range(TILES):
                dve.wait_ge(pe["ff2"], t + 1)
                dve.wait_ge(mk["t2b"], t + 1)
                v.tensor_tensor(h1[:, t], bank(t)[:, 0:DIM], t2b[:, t], ALU.add).then_inc(mk["h1"], 1)
                dve.wait_ge(mk["h1"], t + 1)
                last = v.tensor_reduce(hmax[:, t:t + 1], h1[:, t], X, ALU.max, apply_absolute_value=True)
            step(last)
            step(v.tensor_reduce(hmax[:, TILES:TILES + 1], hmax[:, 0:TILES], X, ALU.max))

            global_max(MAX_H, hmax[:, TILES:TILES + 1], gm[:, 0:1], 4)
            step(scale_of(hs[:, 0:1], gm[:, 0:1]))
            step(v.reciprocal(hs[:, 1:2], hs[:, 0:1]))
            for t in range(TILES):
                v.tensor_scalar(hr[:, t], h1[:, t], hs[:, 1:2], ROUND, ALU.mult, ALU.add).then_inc(mk["hr"], 1)
            v.tensor_tensor(hs[:, 2:3], hs[:, 0:1], wscale[:, 0:1], ALU.mult).then_inc(mk["scale"], 2)
            dve.wait_ge(mk["scale"], 2)
            for t in range(TILES):
                dve.wait_ge(pe["v2"], t + 1)
                v.scalar_tensor_tensor(out=v2[:, t], in0=bank(t)[:, 0:DIM], scalar=hs[:, 2:3], in1=row("bv2"),
                                       op0=ALU.mult, op1=ALU.add).then_inc(mk["v2"], 1)
            dve.wait_ge(mk["v2"], 4)
            v.tensor_reduce(qmax[:, 2:3], v2[:].rearrange("p t n -> p (t n)"), X, ALU.max, apply_absolute_value=True)
            for m in range(4):
                dve.wait_ge(mk["qk2"], m + 1)
                last = v.tensor_reduce(qmax_parts[0:HALF, m:m + 1], qk2[:, m, :], X, ALU.max, apply_absolute_value=True)
            step(last)
            step(v.tensor_reduce(qmax[0:HALF, 0:2], qmax_parts[0:HALF, :].rearrange("p (a b) -> p a b", a=2), X, ALU.max))
            global_max(MAX_QKV, qmax[:], gm[:, 0:3], 0)
            step(scale_of(qs[:], gm[:, 0:3]))
            v.reciprocal(qinv[:], qs[:]).then_inc(mk["scale"], 1)
            dve.wait_ge(mk["scale"], 3)
            step(v.tensor_scalar(qk_r[:, 2:4], qk2[:, 2:4], qinv[0:HALF, 1:2], ROUND, ALU.mult, ALU.add))
            v.tensor_scalar(k_q[:], qk_r[:, 2:4], -ROUND, None, ALU.add).then_inc(mk["kq"], 1)
            v.tensor_scalar(slog[:], qs[:, 0:1], qs[:, 1:2], HEAD ** -0.5, ALU.mult, ALU.mult)
            dve.wait_ge(mk["kq"], 1)
            for h in range(4):
                v.tensor_scalar(k_heads[:, h], k_q[:], head_mask[:, h:h + 1], None, ALU.mult).then_inc(mk["kd"], 1)
            dve.wait_ge(mk["qkr"], 1)
            v.tensor_scalar(q_q[:], qk_r[:, 0:2], -ROUND, None, ALU.add).then_inc(mk["qq"], 1)
            for t in range(TILES):
                src = pairs[t][:, :, 0:384].rearrange("p i (h j) -> p i h j", j=TOKENS)
                m = mx2[:, t].rearrange("p (h i) -> p i h", i=2)
                dve.wait_ge(pe["scores2"], t + 1)
                step(v.tensor_reduce(m, src, X, ALU.max))
                v.tensor_tensor(e2[:, t].rearrange("p h i j -> p i h j"), src, wide(m, TOKENS),
                                ALU.subtract).then_inc(mk["sub2"], 1)
            for t in range(TILES):
                dve.wait_ge(mk["exp2"], t + 1)
                last = v.tensor_reduce(sum2[:, t], e2[:, t].rearrange("p h i j -> p (h i) j"), X, ALU.add)
            step(last)
            step(v.reciprocal(inv2[:], sum2[:]))
            step(v.tensor_reduce(pmax[:], inv2[:].rearrange("p t n -> p (t n)"), X, ALU.max))
            global_max(MAX_P, pmax[:], gm[:, 0:1], 0)
            step(scale_of(ps_[:, 0:1], gm[:, 0:1]))
            step(v.reciprocal(ps_[:, 1:2], ps_[:, 0:1]))
            v.tensor_scalar(f2[:], inv2[:], ps_[:, 1:2], None, ALU.mult).then_inc(mk["f2"], 1)
            dve.wait_ge(mk["f2"], 1)
            for t in range(TILES):
                if t < TILES - 1:
                    step(v.tensor_tensor(p2[:, t].rearrange("p h (i j) -> p (h i) j", j=TOKENS),
                                         e2[:, t].rearrange("p h i j -> p (h i) j"), wide(f2[:, t], TOKENS), ALU.mult))
                else:
                    dve.wait_ge(mk["p2_last"], 1)
                v.tensor_scalar(p2q[:, t], p2[:, t], ROUND, ROUND, ALU.add, ALU.subtract).then_inc(mk["p2"], 1)
            step(v.tensor_tensor(os_[:, 0:1], qs[:, 2:3], ps_[:, 0:1], ALU.mult))
            step(v.tensor_scalar(os_[:, 1:2], os_[:, 0:1], 1.0 / QMAX, None, ALU.mult))
            for g in range(2):
                for i in range(PER_TILE):
                    dve.wait_ge(pe["o2"], 2 * g + 2)
                    last = v.tensor_reduce(omax_parts[:, 2 * g + i:2 * g + i + 1], pairs[2 + i][:, g, 0:384],
                                           X, ALU.max, apply_absolute_value=True)
            step(last)
            step(v.tensor_reduce(omax[:], omax_parts[:], X, ALU.max))
            global_max(MAX_O, omax[:], gm[:, 0:1], 0)
            step(v.tensor_scalar(os_[:, 2:3], gm[:, 0:1], os_[:, 1:2], 1e-8, ALU.mult, ALU.max))
            step(v.reciprocal(os_[:, 3:4], os_[:, 2:3]))
            v.tensor_tensor(os_[:, 4:5], os_[:, 3:4], os_[:, 0:1], ALU.mult).then_inc(mk["scale"], 1)
            dve.wait_ge(mk["scale"], 4)
            for g in range(2):
                step(v.tensor_scalar(o_r[:, :, 2 * g:2 * g + 2, 0, :].rearrange("p c t n -> p t c n"),
                                     pairs[2][:, g, 0:384].rearrange("p (t c n) -> p t c n", t=2, c=3),
                                     os_[:, 4:5], ROUND, ALU.mult, ALU.add))
                dve.wait_ge(mk["or"], g + 1)
                v.tensor_scalar(o_q[:, :, 2 * g:2 * g + 2], o_r[:, :, 2 * g:2 * g + 2], -ROUND, None, ALU.add).then_inc(mk["oq"], 1)
            step(v.tensor_tensor(hs[:, 2:3], os_[:, 2:3], wscale[:, 1:2], ALU.mult))
            for g in range(2):
                gg = slice(2 * g, 2 * g + 2)
                for t in (2 * g, 2 * g + 1):
                    dve.wait_ge(pe["proj"], t + 1)
                    dve.wait_ge(mk["h1b"], t + 1)
                    v.scalar_tensor_tensor(out=zpre[:, t], in0=bank(t)[:, 0:DIM], scalar=hs[:, 2:3], in1=h1b[:, t],
                                           op0=ALU.mult, op1=ALU.add).then_inc(mk["zpre"], 1)
                dve.wait_ge(mk["zpre"], 2 * g + 2)
                step(statistics(LNZ + g, zpre))
                v.scalar_tensor_tensor(out=var_n[:, gg], in0=var_eps[:, gg], scalar=EPS, in1=mv[:, gg, 1],
                                       op0=ALU.mult, op1=ALU.add).then_inc(mk["var"], 1)
            for g in range(2):
                dve.wait_ge(mk["rstd_n"], g + 1)
                for t in (2 * g, 2 * g + 1):
                    centre(t, zpre, nh, rstd_n).then_inc(mk["nh"], 1)
            dve.wait_ge(mk["router"], 2)
            for t in range(TILES):
                dve.wait_ge(mk["nh"], t + 1)
                v.scalar_tensor_tensor(out=weighed[:, t], in0=nh[:, t], scalar=1.0, in1=router_g[:],
                                       op0=ALU.mult, op1=ALU.mult, accum_out=logit[:, t:t + 1]).then_inc(mk["logit"], 1)
            dve.wait_ge(mk["rstd"], LNZ + 2)
            for t in range(2):
                centre(t, zpre, z, rstd).then_inc(mk["z"], 1)
            dve.wait_ge(mk["eneg"], 1)
            step(v.tensor_scalar(eneg1[:], eneg[:], 1.0, None, ALU.add))
            step(v.reciprocal(score[:], eneg1[:]))
            v.tensor_copy(score_b[:], wide(score[:], 128)).then_inc(mk["score_b"], 1)
            for t in range(2, TILES):
                centre(t, zpre, z, rstd).then_inc(mk["z"], 1)
            dve.wait_ge(pe["scoreT"], 1)
            for t in range(TILES):
                s = bank(2)[:, tokens(t)]
                v.scalar_tensor_tensor(out=below[:, t], in0=s, scalar=score[:, t:t + 1], in1=same,
                                       op0=ALU.is_lt, op1=ALU.mult, accum_out=less[:, t:t + 1])
                last = v.scalar_tensor_tensor(out=equal[:, t], in0=s, scalar=score[:, t:t + 1], in1=before,
                                              op0=ALU.is_equal, op1=ALU.mult, accum_out=tie[:, t:t + 1])
            step(last)
            step(v.tensor_tensor(rank[:], less[:], tie[:], ALU.add))
            for t in range(TILES):
                v.tensor_scalar(picked[:, t, :], pick_at[:, t, :], rank[:, t:t + 1], None,
                                ALU.is_equal).then_inc(mk["picked"], 1)

            def keep_v3(t):
                dve.wait_ge(pe["v3"], t + 1)
                v.tensor_tensor(v3[:, t], bank(4 + t)[:, 0:DIM], row("bv3"), ALU.add).then_inc(mk["v3"], 1)

            for t in range(TILES):
                last = v.scalar_tensor_tensor(out=sTm[:, t], in0=bank(2)[:, tokens(t)], scalar=1.0, in1=same,
                                              op0=ALU.mult, op1=ALU.mult, accum_out=total[:, t:t + 1])
            step(last)
            v.tensor_scalar(rest[:], rank[:], float(PICKED), None, ALU.is_ge)
            step(v.tensor_scalar(total_e[:], total[:], 1e-6, None, ALU.add))
            step(v.reciprocal(total_i[:], total_e[:]))
            step(v.tensor_tensor(weight[:], score[:], total_i[:], ALU.mult))
            for t in range(TILES):
                v.scalar_tensor_tensor(out=mixer[:, t], in0=sTm[:, t], scalar=weight[:, t:t + 1], in1=ident[:],
                                       op0=ALU.mult, op1=ALU.add).then_inc(mk["mixer"], 1)
            keep_v3(0)
            for c in range(2):
                dve.wait_ge(mk["q3"], c + 1)
                v.tensor_tensor(q3h[:, c, :, 0:CHUNK_HEADS * PICKED].rearrange("p n (h q) -> p n h q", q=PICKED),
                                q3[:, c].unsqueeze(2).to_broadcast([HALF, IMAGES, CHUNK_HEADS, PICKED]),
                                head_mask.unsqueeze(1).unsqueeze(3).to_broadcast([HALF, IMAGES, CHUNK_HEADS, PICKED]),
                                ALU.mult).then_inc(mk["q3h"], 1)
            for t in range(1, TILES):
                keep_v3(t)
            dve.wait_ge(pe["scores3"], 1)
            src = bank(3).rearrange("p (n j) -> p n j", j=TOKENS)
            step(v.tensor_reduce(mx3[:], src, X, ALU.max))
            v.tensor_tensor(p3[:], src, wide(mx3[:], TOKENS), ALU.subtract).then_inc(mk["sub3"], 1)
            dve.wait_ge(mk["exp3"], 1)
            step(v.tensor_reduce(sum3[:], p3[:], X, ALU.add))
            step(v.reciprocal(inv3[:], sum3[:]))
            v.tensor_tensor(p3[:], p3[:], wide(inv3[:], TOKENS), ALU.mult).then_inc(mk["p3"], 1)
            for t in range(TILES):
                dve.wait_ge(pe["mix"], t + 1)
                last = v.tensor_tensor(mixb[:, t], bank(4 + t)[:, 0:DIM], row("bm"), ALU.add)
            step(last)
            dve.wait_ge(mk["z"], 4)
            for t in range(TILES):
                v.scalar_tensor_tensor(out=mixz[:, t], in0=mixb[:, t], scalar=rest[:, t:t + 1], in1=z[:, t],
                                       op0=ALU.mult, op1=ALU.add).then_inc(mk["mixz"], 1)
            dve.wait_ge(pe["o3"], 1)
            for i in range(PER_TILE):
                src = bank(i)[0:HALF, :].rearrange("p (a b) -> p a b", b=64)[:, :, 0:60].rearrange("p a (h q) -> p a h q", q=PICKED)
                step(v.tensor_tensor(o3m[:, i].rearrange("p a (h q) -> p a h q", q=PICKED), src,
                                     head_mask.unsqueeze(1).unsqueeze(3).to_broadcast([HALF, 2 * TILES, CHUNK_HEADS, PICKED]),
                                     ALU.mult))
                v.tensor_reduce(o3T[:, :, i], o3m[:, i].rearrange("p (c t) (h q) -> p c t q h", c=2, q=PICKED),
                                X, ALU.add).then_inc(mk["o3T"], 1)
            dve.wait_ge(pe["a3"], 1)
            v.tensor_tensor(a3[:], bank(3)[0:ALL_PICKED, 0:DIM], row("bo")[0:ALL_PICKED, :], ALU.add).then_inc(mk["a3"], 1)
            for g in range(2):
                for t in (2 * g, 2 * g + 1):
                    dve.wait_ge(pe["spread"], t + 1)
                    v.tensor_tensor(h4[:, t], bank(4 + t)[:, 0:DIM], mixz[:, t], ALU.add).then_inc(mk["h4"], 1)
                dve.wait_ge(mk["h4"], 2 * g + 2)
                layernorm(LN4 + g, h4, xhat, mk["xhat"])
            for t in range(TILES):
                dve.wait_ge(pe["W2"], t + 1)
                dve.wait_ge(mk["h4z"], t + 1)
                v.tensor_tensor(ypre[:, t], bank(t)[:, 0:DIM], h4z[:, t], ALU.add).then_inc(mk["ypre"], 1)
                dve.wait_ge(mk["ypre"], t + 1)
                layernorm(LNY + t, ypre, y, mk["y"])


def kernel(**inputs):
    import concourse.bacc as bacc
    from concourse.bass_utils import run_bass_kernel_spmd

    a = {k: np.asarray(x) for k, x in inputs.items()}
    tok = lambda n: a["L0_tok_" + n]
    att = lambda n: a["L0_attn_" + n]
    ffn = lambda n: a["L0_ffn_" + n]

    def chunks(w, rows):
        return w.reshape(-1, rows, w.shape[1]).transpose(1, 0, 2)

    def column(x, rows):
        return x.reshape(-1, rows).T

    x = a["x"].reshape(IMAGES, CHANNELS, GRID, PATCH, GRID, PATCH).transpose(3, 5, 1, 0, 2, 4)
    x = x.reshape(PATCH_CHUNKS, 128, TILES, TILE).transpose(1, 2, 0, 3)

    token = np.arange(128)
    mine = token[:, None] // TOKENS == token[None, :] // TOKENS
    pick = np.full((128, TILES, PER_TILE, TILES, PICKED), -1.0)
    for t in range(TILES):
        for i in range(PER_TILE):
            pick[i * TOKENS:(i + 1) * TOKENS, t, i, t, :] = np.arange(PICKED)
    head = np.zeros((128, CHUNK_HEADS))
    head[np.arange(HALF), np.arange(HALF) // HEAD] = 1.0
    table = {"same": mine, "before": mine & (token[None, :] < token[:, None]),
             "pick": pick.reshape(128, -1), "head": head}

    qkv_b, qkv_w = att("b_qkv"), att("w_qkv")
    arrays = {
        "xT": x,
        "w_patch": chunks(tok("w_patch"), 128),
        "w_qkv": chunks(tok("w_qkv"), HALF),
        "w_out": chunks(tok("w_out"), 128),
        "w_ff1": chunks(tok("w_ff1"), HALF),
        "w_ff2": chunks(tok("w_ff2"), 128),
        "w_qkv2": chunks(qkv_w, HALF),
        "w_proj": att("w_proj").reshape(3, 4, HEAD, DIM).transpose(1, 2, 0, 3),
        "w_ffn": np.stack([chunks(ffn(n), HALF) for n in ("Wq", "Wk", "Wv", "Wo", "Wm")], axis=1),
        "br": ffn("br").reshape(1, 1),
        "W1": chunks(ffn("W1"), HALF),
        "W2": chunks(ffn("W2"), 128),
        "rows": np.stack([tok("b_patch"), tok("b_out"), tok("b_ff2"), qkv_b[2 * DIM:], att("b_proj"), ffn("g1"),
                          ffn("b1"), ffn("bo"), ffn("bm"), ffn("bf2"), ffn("bv"), ffn("Wr")]),
        "cols": np.stack([column(v, HALF) for v in (tok("g1"), tok("beta1"), tok("g2"), tok("beta2"), qkv_b[:DIM],
                                                    qkv_b[DIM:2 * DIM], ffn("bq"), ffn("bk"), ffn("g1"), ffn("b1"), ffn("g2"),
                                                    ffn("b2"))], axis=1),
        "cols_ff": np.stack([column(tok("b_ff1"), 128), column(ffn("bf1"), 128)], axis=1),
        "ident": np.eye(128, dtype=np.float32),
        "consts": np.concatenate([table[n] for n in CONSTS], axis=1).astype(np.float32),
    }
    arrays = {k: np.ascontiguousarray(v) for k, v in arrays.items()}

    nc = bacc.Bacc("TRN2", target_bir_lowering=False, num_devices=1)
    f32 = mybir.dt.float32
    A = {k: nc.dram_tensor("in_" + k, v.shape, f32, kind="ExternalInput").ap() for k, v in arrays.items()}
    out = nc.dram_tensor("out", (ALL, DIM), f32, kind="ExternalOutput").ap()
    vit_kernel(nc, A, out)
    r = run_bass_kernel_spmd(nc, [{"in_" + k: v for k, v in arrays.items()}], core_ids=[0])
    return r.results[0]["out"].reshape(IMAGES, TOKENS, DIM)
```

```python
import concourse.bass as bass
import numpy as np
from concourse import mybir
from contextlib import ExitStack

IMAGES, CHANNELS, SIDE, PATCH = 8, 3, 128, 16
GRID = SIDE // PATCH
TOKENS = GRID * GRID
ALL = IMAGES * TOKENS
TILE = 128
PER_TILE = TILE // TOKENS
TILES = ALL // TILE
DIM = 192
HALF = DIM // 2
PATCH_DIM = CHANNELS * PATCH * PATCH
PATCH_CHUNKS = PATCH_DIM // 128
HEADS = 12
HEAD1 = 64
INNER = HEADS * HEAD1
INNER_CHUNKS = INNER // 128
HEAD = DIM // HEADS
CHUNK_HEADS = HEADS // 2
PAD = 32
MLP = 768
MLP_CHUNKS = MLP // 128
PICKED = max(1, int(round(0.15 * TOKENS)))
ALL_PICKED = IMAGES * PICKED
HEAD_ROWS = 64
EPS = 1e-5
QMAX = 127.0
ROUND = 12582912.0

ROWS = ["b_patch", "b_out", "b_ff2", "bv2", "b_proj", "g1", "b1", "bo", "bm", "bf2", "bv3", "Wr"]
COLS = ["g1", "beta1", "g2", "beta2", "bq2", "bk2", "bq3", "bk3", "ffn_g1", "ffn_b1", "ffn_g2", "ffn_b2"]
CONSTS = {"same": 128, "before": 128, "pick": TILES * ALL_PICKED, "head": CHUNK_HEADS}


def const_at(name):
    at = 0
    for n, width in CONSTS.items():
        if n == name:
            return at, at + width
        at += width
    return 0, at


def vit_kernel(nc, A, out):
    f32, f32r, bf16 = mybir.dt.float32, mybir.dt.float32r, mybir.dt.bfloat16
    ALU, ACT, X = mybir.AluOpType, mybir.ActivationFunctionType, mybir.AxisListType.X
    ctx = ExitStack()
    with ctx:
        (PATCHES, QKV, ATTEND, OUT, FF, QUANT, SCORES2, ATTEND2, PROJ, ROUTE, ATTEND3, FF3, END) = range(13)
        ALWAYS = (PATCHES, END)
        floor, ceiling = (nc.sbuf_base + 31) // 32 * 32, nc.sbuf_top
        placed = []

        def sb(name, shape, life, dtype=f32):
            width = int(np.prod(shape[1:])) * (2 if dtype == bf16 else 4)
            width = (width + 31) // 32 * 32
            at = floor
            for start, end, first, last in sorted(placed):
                if first <= life[1] and life[0] <= last and start < at + width and at < end:
                    at = end
            assert at + width <= ceiling, (name, at + width, ceiling)
            placed.append((at, at + width, *life))
            return nc.alloc_sbuf_tensor_at(name, shape, dtype, offset=at)

        def sem(name):
            return ctx.enter_context(nc.semaphore(name))

        stats = sb("stats", [128, TILES, 6], ALWAYS)
        mv = sb("mv", [128, TILES, 2], ALWAYS)
        var_eps = sb("var_eps", [128, TILES], ALWAYS)
        rstd = sb("rstd", [128, TILES], ALWAYS)
        var_n = sb("var_n", [128, TILES], ALWAYS)
        rstd_n = sb("rstd_n", [128, TILES], ALWAYS)
        power = sb("power", [128, TILES], ALWAYS)
        round_bias = sb("round_bias", [128, 1], ALWAYS)
        spread = sb("spread", [128, 3, 128], ALWAYS)
        gm = sb("gm", [128, 3], ALWAYS)
        one = sb("one", [128, 1], ALWAYS)
        mx1, sum1, inv1, mx2, sum2, inv2, f2 = (sb(n, [128, TILES, HEADS], ALWAYS) for n in
                                                ("mx1", "sum1", "inv1", "mx2", "sum2", "inv2", "f2"))
        mx3, sum3, inv3 = (sb(n, [128, IMAGES], ALWAYS) for n in ("mx3", "sum3", "inv3"))
        wmax, wscale, winv = (sb(n, [128, 2], ALWAYS) for n in ("wmax", "wscale", "winv"))
        hmax = sb("hmax", [128, TILES + 1], ALWAYS)
        hs = sb("hs", [128, 3], ALWAYS)
        qmax_parts = sb("qmax_parts", [128, 4], ALWAYS)
        qmax, qs, qinv = (sb(n, [128, 3], ALWAYS) for n in ("qmax", "qs", "qinv"))
        slog = sb("slog", [128, 1], ALWAYS)
        pmax = sb("pmax", [128, 1], ALWAYS)
        ps_ = sb("ps_", [128, 2], ALWAYS)
        omax_parts = sb("omax_parts", [128, 4], ALWAYS)
        omax = sb("omax", [128, 1], ALWAYS)
        os_ = sb("os_", [128, 5], ALWAYS)
        (eneg, eneg1, score, less, tie, total, total_e, total_i, rank, rest, weight) = (
            sb(n, [128, TILES], ALWAYS) for n in
            ("eneg", "eneg1", "score", "less", "tie", "total", "total_e", "total_i", "rank", "rest", "weight"))

        ident = sb("ident", [128, 128], ALWAYS)
        zeros = sb("zeros", [128, 128], ALWAYS)
        ident_b = sb("ident_b", [128, 128], (PATCHES, ATTEND2), bf16)
        consts = sb("consts", [128, const_at("")[1]], (PATCHES, ATTEND3))
        rows = sb("rows", [128, len(ROWS), DIM], ALWAYS)
        cols = sb("cols", [HALF, len(COLS), 2], ALWAYS)
        cols_ff = sb("cols_ff", [128, 2, MLP_CHUNKS], ALWAYS)
        br = sb("br", [128, 1], ALWAYS)
        router_g = sb("router_g", [128, DIM], (FF, PROJ))
        weighed_b = sb("weighed_b", [128, DIM], (FF, FF))
        router_c = sb("router_c", [128, 1], ALWAYS)
        router_bias = sb("router_bias", [128, 1], ALWAYS)
        logit = sb("logit", [128, TILES], ALWAYS)
        W1 = sb("W1", [HALF, 2, MLP], (PATCHES, FF))
        W2 = sb("W2", [128, MLP_CHUNKS, DIM], ALWAYS)
        w_ffn = sb("w_ffn", [HALF, 5, 2, DIM], (PATCHES, ATTEND3))
        w_ff1 = sb("w_ff1", [HALF, 2, MLP], (PATCHES, OUT))
        w_ff2 = sb("w_ff2", [128, MLP_CHUNKS, DIM], (PATCHES, FF))
        w_out = sb("w_out", [128, INNER_CHUNKS, DIM], (PATCHES, OUT))
        w_qkv2 = sb("w_qkv2", [HALF, 2, 3 * DIM], (PATCHES, OUT))
        w_proj = sb("w_proj", [128, 3, DIM], (PATCHES, OUT))
        w_qkv = sb("w_qkv", [HALF, 2, 3 * INNER], (PATCHES, QKV))
        xT = sb("xT", [128, TILES, PATCH_CHUNKS, TILE], (PATCHES, PATCHES))
        w_patch = sb("w_patch", [128, PATCH_CHUNKS, DIM], (PATCHES, PATCHES))

        def const(name):
            a, b = const_at(name)
            return consts[:, a:b]

        def row(name):
            return rows[:, ROWS.index(name), :]

        def col(name, chunk):
            return cols[:, COLS.index(name), chunk:chunk + 1]

        same, before = const("same"), const("before")
        pick_at = const("pick").rearrange("p (t n) -> p t n", t=TILES)
        head_mask = const("head")[0:HALF, :]

        xhat = sb("xhat", [128, TILES, DIM], ALWAYS)
        t1 = sb("t1", [128, TILES, DIM], (PATCHES, OUT))
        t1b = sb("t1b", [128, TILES, DIM], (QKV, OUT))
        hT = sb("hT", [HALF, 2, ALL], (QKV, QKV))
        hT_parts = [sb("hT_" + n, [HALF, 2, ALL], (QKV, ATTEND), f32r) for n in ("high", "rest")]
        w_qkv_parts = [sb("w_qkv_" + n, [HALF, 2, 3 * INNER], (QKV, ATTEND), f32r) for n in ("high", "rest")]
        qkT = sb("qkT", [128, 2 * INNER_CHUNKS, ALL], (QKV, ATTEND))
        v1 = sb("v1", [128, TILES, INNER], (QKV, OUT))
        p1 = sb("p1", [128, TILES, 2, 6, TOKENS], (QKV, OUT))
        pT1 = sb("pT1", [128, TILES, 2, 3, 128], (ATTEND, OUT))
        oT1 = sb("oT1", [128, INNER_CHUNKS, TILES, PER_TILE, TOKENS], (ATTEND, OUT))
        t2 = sb("t2", [128, TILES, DIM], (OUT, FF))
        t2b = sb("t2b", [128, TILES, DIM], (OUT, FF))
        h2T = sb("h2T", [HALF, 2, ALL], (OUT, FF))
        h2T_parts = [sb("h2T_" + n, [HALF, 2, ALL], (OUT, FF), f32r) for n in ("high", "rest")]
        w_ff1_parts = [sb("w_ff1_" + n, [HALF, 2, MLP], (OUT, FF), f32r) for n in ("high", "rest")]
        W1_parts = [sb("W1_" + n, [HALF, 2, MLP], (FF, END), f32r) for n in ("high", "rest")]
        ff = sb("ff", [128, MLP_CHUNKS, ALL], (FF, FF))
        h1 = sb("h1", [128, TILES, DIM], (FF, PROJ))
        h1b = sb("h1b", [128, TILES, DIM], (QUANT, PROJ))

        wqkv_r = sb("wqkv_r", [HALF, 2, 3 * DIM], (QKV, FF))
        wqkv_q = sb("wqkv_q", [HALF, 2, 3 * DIM], (QKV, QUANT), bf16)
        wproj_r = sb("wproj_r", [128, 3, DIM], (QKV, FF))
        wproj_q = sb("wproj_q", [128, 3, DIM], (QKV, PROJ), bf16)
        hr = sb("hr", [128, TILES, DIM], (QUANT, QUANT))
        hq = sb("hq", [HALF, 2, ALL], (QUANT, QUANT), bf16)
        qk2 = sb("qk2", [HALF, 4, ALL], (QUANT, SCORES2))
        v2 = sb("v2", [128, TILES, DIM], (QUANT, ATTEND2))
        qk_r = sb("qk_r", [HALF, 4, ALL], (QUANT, SCORES2))
        q_q = sb("q_q", [HALF, 2, ALL], (QUANT, SCORES2), bf16)
        k_q = sb("k_q", [HALF, 2, ALL], (QUANT, SCORES2), bf16)
        k_heads = sb("k_heads", [HALF, CHUNK_HEADS, 2, ALL], (QUANT, SCORES2), bf16)
        v_r = sb("v_r", [128, TILES, DIM], (SCORES2, ATTEND2))
        v_q = sb("v_q", [128, TILES, HEADS, PAD], (QUANT, ATTEND2), bf16)
        q3h = sb("q3h", [HALF, 2, IMAGES, HEAD_ROWS], (QUANT, ATTEND3))
        e2 = sb("e2", [128, TILES, CHUNK_HEADS, PER_TILE, TOKENS], (SCORES2, ATTEND2))
        folded = sb("folded", [128, TILES - 1, HEADS, TOKENS // 2], (SCORES2, ATTEND2))
        p2 = sb("p2", [128, TILES, CHUNK_HEADS, PER_TILE * TOKENS], (ATTEND2, ATTEND2))
        p2q = sb("p2q", [128, TILES, CHUNK_HEADS, PER_TILE * TOKENS], (ATTEND2, ATTEND2), bf16)
        pT2 = sb("pT2", [128, TILES, CHUNK_HEADS, 128], (ATTEND2, ATTEND2), bf16)
        o_r = sb("o_r", [128, 3, TILES, PER_TILE, TOKENS], (ATTEND2, PROJ))
        o_q = sb("o_q", [128, 3, TILES, PER_TILE, TOKENS], (ATTEND2, PROJ), bf16)

        zpre = sb("zpre", [128, TILES, DIM], (PROJ, ROUTE))
        z = sb("z", [128, TILES, DIM], (PROJ, END))
        zb = sb("zb", [128, TILES, DIM], (PROJ, END))
        nh = sb("nh", [128, TILES, DIM], (PROJ, ROUTE))
        ng = sb("ng", [128, TILES, DIM], (PROJ, ROUTE))
        n3 = sb("n3", [128, TILES, DIM], (PROJ, ATTEND3))
        nT = sb("nT", [HALF, 2, ALL], (PROJ, ATTEND3))
        weighed = sb("weighed", [128, TILES, DIM], (PROJ, PROJ))
        score_b = sb("score_b", [128, TILES, 128], (ROUTE, ROUTE))
        below = sb("below", [128, TILES, 128], (ROUTE, ROUTE))
        equal = sb("equal", [128, TILES, 128], (ROUTE, ROUTE))
        sTm = sb("sTm", [128, TILES, 128], (ROUTE, ROUTE))
        mixer = sb("mixer", [128, TILES, 128], (ROUTE, ATTEND3))
        picked = sb("picked", [128, TILES, ALL_PICKED], (ROUTE, ATTEND3))
        pickedT = sb("pickedT", [ALL_PICKED, ALL], (ROUTE, ATTEND3))
        mixT = sb("mixT", [HALF, 2, ALL], (ROUTE, ATTEND3))
        nselT = sb("nselT", [HALF, 2, ALL_PICKED], (ROUTE, ATTEND3))
        q3 = sb("q3", [HALF, 2, IMAGES, PICKED], (ROUTE, ATTEND3))
        k3 = sb("k3", [HALF, 2, ALL], (ROUTE, ATTEND3))
        v3 = sb("v3", [128, TILES, DIM], (ROUTE, ATTEND3))
        p3 = sb("p3", [128, IMAGES, TOKENS], (ATTEND3, ATTEND3))
        pT3 = sb("pT3", [128, TILES, 128], (ATTEND3, ATTEND3))
        o3m = sb("o3m", [HALF, 2, PER_TILE, 4, CHUNK_HEADS * PICKED], (ATTEND3, ATTEND3))
        o3T = sb("o3T", [HALF, 2, PER_TILE, TILES, PICKED], (ATTEND3, ATTEND3))
        a3 = sb("a3", [ALL_PICKED, DIM], (ATTEND3, ATTEND3))
        zm = sb("zm", [128, TILES, DIM], (ROUTE, ATTEND3))
        mixz = sb("mixz", [128, TILES, DIM], (ATTEND3, ATTEND3))
        h4 = sb("h4", [128, TILES, DIM], (ATTEND3, END))
        h4z = sb("h4z", [128, TILES, DIM], (ATTEND3, END))
        h5T = sb("h5T", [HALF, 2, ALL], (FF3, END))
        h5T_parts = [sb("h5T_" + n, [HALF, 2, ALL], (FF3, END), f32r) for n in ("high", "rest")]
        ff3 = sb("ff3", [128, MLP_CHUNKS, ALL], (FF3, END))
        ypre = sb("ypre", [128, TILES, DIM], (END, END))
        y = sb("y", [128, TILES, DIM], (END, END))

        pairs = [ctx.enter_context(nc.psum_tensor(f"pair{i}", [128, 2, 512], f32)) for i in range(4)]

        def bank(i):
            return pairs[i // 2][:, i % 2, :]

        def split_chunks(ap):
            return ap[0:HALF, 0:2 * TILE].rearrange("p (c n) -> p c n", c=2)

        def tokens(t):
            return slice(t * TILE, (t + 1) * TILE)

        def image(t, i):
            return slice((PER_TILE * t + i) * TOKENS, (PER_TILE * t + i + 1) * TOKENS)

        def own_picks(ap, t):
            return ap.rearrange("p (i t q) -> p i t q", i=PER_TILE, t=TILES)[:, :, t, :]

        def place1(h):
            chunk, r = h // 2, h % 2
            return r, (chunk + r) % 2, chunk // 2

        ld_x = [sem(f"ld_x{t}") for t in range(TILES)]
        ld_x0 = [sem(f"ld_x0_{g}") for g in range(3)]
        ld_wp = [sem(f"ld_wp{g}") for g in range(3)]
        ld = {n: sem("ld_" + n) for n in (
            "ident", "const", "rows", "rows_tok", "row0", "cols", "cols_ff", "w_q", "w_k", "w_v", "w_out", "w_ff1",
            "w_ff2", "w_qkv2", "w_proj", "w_ffn", "W1", "W2")}
        pe = {n: sem("pe_" + n) for n in (
            "patch", "xhatT", "qk", "scores", "v", "pT", "o", "out", "x2T", "ff1", "ff2", "wide", "hT", "qk2", "v2",
            "scores2", "pT2", "o2", "proj", "scoreT", "nT", "k3", "v3", "mixT", "nsel", "pickT", "q3", "mix",
            "scores3", "pT3", "o3", "a3", "spread", "x4T", "W1", "W2")}
        mk = {n: sem("mk_" + n) for n in (
            "t1", "var", "rstd", "xhat", "hT", "qk", "sub", "exp", "p", "v", "pT", "oT", "t2", "h2T", "gelu",
            "h1", "spread", "scale", "wscale", "t1b", "t2b", "wq", "hr", "hq", "qk2", "v2", "qkr", "qq", "kq",
            "kd", "ka", "or", "vq", "sub2", "max2", "copied2", "pool_sub2", "exp2", "folded", "f2", "p2_last",
            "p2", "pT2", "oq", "h1b", "zpre", "z", "nh", "rstd_n", "n3", "router", "logit", "eneg", "score_b",
            "mixer", "picked", "nT", "k3", "v3", "mixT", "nselT", "pickT", "q3", "q3h", "sub3", "exp3", "p3",
            "pT3", "o3T", "a3", "zm", "mixz", "h4", "zb", "h4z", "h5T", "gelu3", "ypre", "y", "zero", "zeros",
            "w_parts", "h_parts", "w_ff1_parts", "W1_parts", "h2T_parts", "h5T_parts", "identb")}
        dve_step, pool_step = sem("dve_step"), sem("pool_step")
        stored = sem("stored")

        GROUPS = [[0], [1], [2], [3], [0, 1], [2, 3], [0, 1], [2, 3], [0, 1], [2, 3], [0], [1], [2], [3]]
        LN1, LN2, LNZ, LN4, LNY = 0, 4, 6, 8, 10
        COPIED = 1
        MAX_W, MAX_H, MAX_QKV, MAX_P, MAX_O = range(5)
        MAX_WIDTH = [2, 1, 3, 1, 1]
        V_PAIR = [0, 1, 0, 1]
        OUT_BANK = [6, 7, 4, 5]
        NT_BANK = [0, 1, 3, 4]
        AHEAD1, AHEAD3 = 3, 2
        PT3_BANK = [2, 1]
        O3_BANK = [[0, 3], [1, 2]]

        block = ctx.enter_context(nc.Block())

        @block.sync
        def _(sp):
            third = PATCH_CHUNKS // 3
            for g in range(3):
                cc = slice(g * third, (g + 1) * third)
                sp.dma_start(w_patch[:, cc], A["w_patch"][:, cc]).then_inc(ld_wp[g], 16)
                sp.dma_start(xT[:, 0, cc], A["xT"][:, 0, cc]).then_inc(ld_x0[g], 16)
            for t in range(1, TILES):
                sp.dma_start(xT[:, t], A["xT"][:, t]).then_inc(ld_x[t], 16)
                if t == 1:
                    sp.dma_start(ident[:], A["ident"]).then_inc(ld["ident"], 16)
            for m, name in enumerate(("w_q", "w_k", "w_v")):
                part = slice(m * INNER, (m + 1) * INNER)
                sp.dma_start(w_qkv[:, :, part], A["w_qkv"][:, :, part]).then_inc(ld[name], 16)
            sp.dma_start(w_qkv2[:], A["w_qkv2"]).then_inc(ld["w_qkv2"], 16)
            sp.wait_ge(mk["zero"], 1)
            for r in range(4):
                sp.dma_start(w_proj[PAD * r:PAD * r + HEAD], A["w_proj"][r]).then_inc(ld["w_proj"], 16)
            sp.dma_start(consts[:], A["consts"]).then_inc(ld["const"], 16)
            sp.dma_start(cols_ff[:], A["cols_ff"]).then_inc(ld["cols_ff"], 16)
            sp.dma_start(rows[:, 1:3], A["rows"][1:3].rearrange("(a r) n -> a r n", a=1)
                         .to_broadcast([128, 2, DIM])).then_inc(ld["rows_tok"], 16)
            sp.dma_start(w_out[:], A["w_out"]).then_inc(ld["w_out"], 16)
            sp.dma_start(w_ff1[:], A["w_ff1"]).then_inc(ld["w_ff1"], 16)
            sp.dma_start(w_ff2[:], A["w_ff2"]).then_inc(ld["w_ff2"], 16)
            sp.dma_start(rows[:, 3:], A["rows"][3:].rearrange("(a r) n -> a r n", a=1)
                         .to_broadcast([128, len(ROWS) - 3, DIM])).then_inc(ld["rows"], 16)
            sp.dma_start(br[:], A["br"].to_broadcast([128, 1])).then_inc(ld["rows"], 16)
            sp.dma_start(w_ffn[:], A["w_ffn"]).then_inc(ld["w_ffn"], 16)
            sp.dma_start(W1[:], A["W1"]).then_inc(ld["W1"], 16)
            sp.dma_start(W2[:], A["W2"]).then_inc(ld["W2"], 16)
            for t in range(TILES):
                sp.wait_ge(mk["y"], t + 1)
                sp.dma_start(out[tokens(t), :], y[:, t]).then_inc(stored, 16)
            sp.wait_ge(stored, 16 * TILES)

        @block.tensor
        def _(te):
            mm = nc.tensor.matmul

            def turn(dst, src, parts):
                return nc.tensor.transpose(dst, src, ident[0:parts, 0:parts])

            def turn_tile(src, t, where):
                for c in range(2):
                    last = turn(bank(where)[0:HALF, c * TILE:(c + 1) * TILE],
                                src[:, t, c * HALF:(c + 1) * HALF], 128)
                return last

            def keep_warm(products, where):
                for _ in range(products):
                    mm(bank(where)[:, 0:128], zeros[:], zeros[:], start=True, stop=True)

            def turn_spread(nth, where):
                te.wait_ge(mk["spread"], nth + 1)
                for k in range(MAX_WIDTH[nth]):
                    last = turn(bank(where)[:, k * 128:(k + 1) * 128], spread[:, k, :], 128)
                last.then_inc(pe["wide"], 1)

            def turn_h(t):
                if t == 0:
                    te.wait_ge(ld["ident"], 16)
                te.wait_ge(mk["xhat"], t + 1)
                turn_tile(xhat, t, 4 + t).then_inc(pe["xhatT"], 1)

            te.wait_ge(mk["zeros"], 1)
            keep_warm(7, 7)
            for t in range(TILES):
                if t == TILES - 1:
                    turn_h(0)
                    turn_h(1)
                if t > 0:
                    te.wait_ge(ld_x[t], 16)
                for c in range(PATCH_CHUNKS):
                    if t == 0 and c % 2 == 0:
                        te.wait_ge(ld_wp[c // 2], 16)
                        te.wait_ge(ld_x0[c // 2], 16)
                    last = mm(bank(t)[:, 0:DIM], xT[:, t, c, :], w_patch[:, c, :],
                              start=(c == 0), stop=(c == PATCH_CHUNKS - 1))
                last.then_inc(pe["patch"], 1)

            def split_product(dst, a, b):
                passes = [(x, y, c) for x, y in ((0, 0), (0, 1), (1, 0)) for c in range(2)]
                for k, (x, y, c) in enumerate(passes):
                    last = mm(dst, a[x][:, c, :], b[y][:, c, :], start=(k == 0), stop=(k == len(passes) - 1))
                return last

            def project_qk(half):
                te.wait_ge(mk["hT"], 2 * half + 2)
                for m in range(2 * INNER_CHUNKS):
                    n = half * 2 * INNER_CHUNKS + m
                    if n == 3:
                        te.wait_ge(mk["t1"], 4)
                    if n == INNER_CHUNKS:
                        turn_h(2)
                        turn_h(3)
                        te.wait_ge(mk["h_parts"], 1)
                        te.wait_ge(mk["w_parts"], 1)
                    if n == INNER_CHUNKS * 3 // 2:
                        te.wait_ge(mk["w_parts"], 2)
                    if n == 2 * INNER_CHUNKS:
                        te.wait_ge(mk["w_parts"], 4)
                        te.wait_ge(mk["h_parts"], 2)
                    if n >= 4:
                        te.wait_ge(mk["qk"], n - 3)
                    dst, chunk, own = bank(n % 4)[:, 0:256], slice(m * 128, (m + 1) * 128), slice(half * 256, (half + 1) * 256)
                    if n < INNER_CHUNKS:
                        for c in range(2):
                            last = mm(dst, w_qkv[:, c, chunk], hT[:, c, own], start=(c == 0), stop=(c == 1))
                    else:
                        last = split_product(dst, [w[:, :, chunk] for w in w_qkv_parts], [h[:, :, own] for h in hT_parts])
                    last.then_inc(pe["qk"], 1)

            def scores(t):
                te.wait_ge(mk["qk"], 2 * INNER_CHUNKS * (t // 2 + 1))
                if t >= 2:
                    te.wait_ge(mk["sub"], t - 1)
                for h2 in range(INNER_CHUNKS):
                    for i in range(PER_TILE):
                        for r in range(2):
                            where, half, slot = place1(2 * h2 + r)
                            rr = slice(64 * r, 64 * r + 64)
                            last = mm(pairs[2 + t % 2][64 * half:64 * half + 64, where,
                                                       slot * 128 + 64 * i:slot * 128 + 64 * i + 64],
                                      qkT[rr, h2, image(t, i)], qkT[rr, INNER_CHUNKS + h2, image(t, i)],
                                      start=True, stop=True)
                last.then_inc(pe["scores"], 1)

            def project_v(t):
                te.wait_ge(mk["qk"], 2 * INNER_CHUNKS * (t // 2 + 1) - 2 * (1 - t % 2))
                for g in range(2):
                    columns = slice(2 * INNER + g * 384, 2 * INNER + (g + 1) * 384)
                    last = split_product(pairs[V_PAIR[t]][:, g, 0:384], [h[:, :, tokens(t)] for h in hT_parts],
                                         [w[:, :, columns] for w in w_qkv_parts])
                last.then_inc(pe["v"], 1)

            te.wait_ge(ld["w_q"], 16)
            te.wait_ge(mk["t1"], 3)
            project_qk(0)
            te.wait_ge(mk["w_parts"], 3)
            te.wait_ge(mk["hT"], 4)
            project_v(0)
            project_v(1)
            scores(0)
            scores(1)
            te.wait_ge(mk["v"], 2)
            project_qk(1)

            def turn_p(t):
                te.wait_ge(mk["p"], t + 1)
                if t < 2:
                    te.wait_ge(mk["v"], t + 3)
                if t >= 2:
                    te.wait_ge(mk["oT"], t - 1)
                for r in range(2):
                    for m in range(3):
                        last = turn(pairs[t % 2][:, r, m * 128:(m + 1) * 128],
                                    p1[:, t, r, 2 * m:2 * m + 2, :].rearrange("p a j -> p (a j)"), 128)
                last.then_inc(pe["pT"], 1)

            def attend(t):
                te.wait_ge(mk["v"], t + 1)
                te.wait_ge(mk["pT"], t + 1)
                for h2 in range(INNER_CHUNKS):
                    for r in range(2):
                        where, half, slot = place1(2 * h2 + r)
                        for i in range(PER_TILE):
                            ii = slice(64 * i, 64 * i + 64)
                            h = 2 * h2 + r
                            last = mm(pairs[t % 2][64 * r:64 * r + 64, i, h2 * 64:(h2 + 1) * 64],
                                      v1[ii, t, h * 64:(h + 1) * 64],
                                      pT1[ii, t, where, slot, 64 * half:64 * half + 64], start=True, stop=True)
                last.then_inc(pe["o"], 1)

            def turn_half(half, normed, turned):
                for t in (2 * half, 2 * half + 1):
                    te.wait_ge(mk["xhat"], normed + t + 1)
                    turn_tile(xhat, t, t).then_inc(turned, 1)

            def project_out(t):
                te.wait_ge(mk["oT"], t + 1)
                for c in range(INNER_CHUNKS):
                    last = mm(bank(OUT_BANK[t])[:, 0:DIM], oT1[:, c, t].rearrange("p i n -> p (i n)"), w_out[:, c, :],
                              start=(c == 0), stop=(c == INNER_CHUNKS - 1))
                last.then_inc(pe["out"], 1)

            project_v(2)
            te.wait_ge(mk["sub"], 1)
            turn_spread(MAX_W, 4)
            project_v(3)
            te.wait_ge(mk["wscale"], 1)
            scores(2)
            turn_p(0)
            scores(3)
            turn_p(1)
            attend(0)
            attend(1)
            te.wait_ge(ld["w_out"], 16)
            te.wait_ge(mk["sub"], 4)
            turn_p(2)
            project_out(0)
            turn_p(3)
            attend(2)
            project_out(1)
            attend(3)
            project_out(2)
            te.wait_ge(mk["oT"], 4)
            turn_half(0, 4, pe["x2T"])
            project_out(3)

            def up(half, w, src, done, freed, ahead, normed, turned):
                for m in range(MLP_CHUNKS):
                    n = half * MLP_CHUNKS + m
                    if half == 0 and m == ahead:
                        turn_half(1, normed, turned)
                    if n >= 4:
                        te.wait_ge(freed, n - 3)
                    split_product(bank(4 + n % 4)[:, 0:256], [part[:, :, m * 128:(m + 1) * 128] for part in w],
                                  [part[:, :, half * 256:(half + 1) * 256] for part in src]).then_inc(done, 1)

            def down(t, w, src, done):
                for c in range(MLP_CHUNKS):
                    last = mm(bank(t)[:, 0:DIM], src[:, c, tokens(t)], w[:, c, :],
                              start=(c == 0), stop=(c == MLP_CHUNKS - 1))
                last.then_inc(done, 1)

            te.wait_ge(mk["w_ff1_parts"], 1)
            te.wait_ge(ld["w_ff2"], 16)
            te.wait_ge(mk["t2"], 4)
            for half in range(2):
                te.wait_ge(mk["h2T_parts"], 2 * half + 2)
                up(half, w_ff1_parts, h2T_parts, pe["ff1"], mk["gelu"], AHEAD1, 4, pe["x2T"])
            for t in range(TILES):
                te.wait_ge(mk["gelu"], MLP_CHUNKS * (t // 2 + 1))
                down(t, w_ff2, ff, pe["ff2"])

            te.wait_ge(mk["gelu"], 2 * MLP_CHUNKS)
            keep_warm(7, 5)
            turn_spread(MAX_H, 4)
            keep_warm(6, 5)
            for t in range(TILES):
                te.wait_ge(mk["hr"], t + 1)
                turn_tile(hr, t, t).then_inc(pe["hT"], 1)
            te.wait_ge(mk["wq"], 2)
            keep_warm(5, 5)
            te.wait_ge(mk["hq"], 4)
            te.wait_ge(mk["scale"], 2)
            for t in range(TILES):
                for c in range(2):
                    last = mm(bank(t)[:, 0:DIM], hq[:, c, tokens(t)], wqkv_q[:, c, 2 * DIM:3 * DIM],
                              start=(c == 0), stop=(c == 1))
                last.then_inc(pe["v2"], 1)
            for m in range(4):
                for c in range(2):
                    last = mm(bank(4 + m)[0:HALF, :], wqkv_q[:, c, m * HALF:(m + 1) * HALF], hq[:, c, :],
                              start=(c == 0), stop=(c == 1))
                last.then_inc(pe["qk2"], 1)
            te.wait_ge(mk["v2"], 4)
            turn_spread(MAX_QKV, 0)
            te.wait_ge(mk["scale"], 3)
            te.wait_ge(mk["qk2"], 4)
            te.wait_ge(mk["qq"], 1)
            te.wait_ge(mk["kd"], 4)
            te.wait_ge(mk["ka"], 2)
            for t in range(TILES):
                for i in range(PER_TILE):
                    for c in range(2):
                        last = mm(pairs[t][64 * c:64 * c + 64, i, 0:CHUNK_HEADS * TOKENS], q_q[:, c, image(t, i)],
                                  k_heads[:, :, c, image(t, i)], start=True, stop=True)
                last.then_inc(pe["scores2"], 1)
            te.wait_ge(mk["sub2"], TILES - 1)
            te.wait_ge(mk["copied2"], 1)
            keep_warm(6, 1)
            turn_spread(MAX_P, 0)
            te.wait_ge(mk["identb"], 1)
            te.wait_ge(mk["vq"], 1)

            def turn_p2(t):
                te.wait_ge(mk["p2"], t + 1)
                dst = bank(t).bitcast(bf16)
                for h in range(CHUNK_HEADS):
                    last = nc.tensor.transpose(dst[:, h * 128:(h + 1) * 128], p2q[:, t, h, :], ident_b[:, :])
                last.then_inc(pe["pT2"], 1)

            def attend2(t):
                te.wait_ge(mk["pT2"], t + 1)
                for h in range(HEADS):
                    for i in range(PER_TILE):
                        ii = slice(64 * i, 64 * i + 64)
                        half, slot = h // CHUNK_HEADS, h % CHUNK_HEADS
                        r = h % 4
                        at = (t % 2) * 192 + (h // 4) * 64
                        last = mm(pairs[2 + i][32 * r:32 * r + 32, t // 2, at:at + 64],
                                  v_q[ii, t, h, :], pT2[ii, t, slot, 64 * half:64 * half + 64],
                                  start=True, stop=True)
                last.then_inc(pe["o2"], 1)

            keep_warm(7, 7)
            turn_p2(0)
            keep_warm(2, 7)
            turn_p2(1)
            attend2(0)
            turn_p2(2)
            attend2(1)
            turn_p2(3)
            attend2(2)
            attend2(3)
            te.wait_ge(mk["pT2"], 4)
            turn_spread(MAX_O, 0)
            for t in range(TILES):
                te.wait_ge(mk["oq"], t // 2 + 1)
                for c in range(3):
                    last = mm(bank(t)[:, 0:DIM], o_q[:, c, t].rearrange("p i n -> p (i n)"), wproj_q[:, c, :],
                              start=(c == 0), stop=(c == 2))
                last.then_inc(pe["proj"], 1)

            WQ, WK, WV, WO, WM = range(5)
            te.wait_ge(mk["oq"], 2)
            keep_warm(8, 7)
            for t in range(TILES):
                te.wait_ge(mk["nh"], t + 1)
                turn_tile(nh, t, NT_BANK[t]).then_inc(pe["nT"], 1)
            keep_warm(8, 7)
            te.wait_ge(mk["score_b"], 1)
            for t in range(TILES):
                last = turn(bank(2)[:, tokens(t)], score_b[:, t, :], 128)
            last.then_inc(pe["scoreT"], 1)
            keep_warm(3, 7)
            te.wait_ge(ld["w_ffn"], 16)
            te.wait_ge(mk["nT"], 4)

            def project_k3(m):
                for c in range(2):
                    last = mm(bank(m)[0:HALF, :], w_ffn[:, WK, c, m * HALF:(m + 1) * HALF], nT[:, c, :],
                              start=(c == 0), stop=(c == 1))
                last.then_inc(pe["k3"], 1)

            def project_v3(t):
                for c in range(2):
                    last = mm(bank(4 + t)[:, 0:DIM], nT[:, c, tokens(t)], w_ffn[:, WV, c, :],
                              start=(c == 0), stop=(c == 1))
                last.then_inc(pe["v3"], 1)

            project_k3(0)
            te.wait_ge(mk["n3"], 4)
            for t in range(TILES):
                te.wait_ge(mk["picked"], t + 1)
                for c in range(2):
                    last = mm(own_picks(bank(3)[0:HALF, c * ALL_PICKED:(c + 1) * ALL_PICKED], t),
                              n3[:, t, c * HALF:(c + 1) * HALF], own_picks(picked[:, t, :], t), start=True, stop=True)
            last.then_inc(pe["nsel"], 1)
            project_k3(1)
            te.wait_ge(mk["nselT"], 1)
            for m in range(2):
                for c in range(2):
                    last = mm(bank(3)[0:HALF, m * ALL_PICKED:(m + 1) * ALL_PICKED],
                              w_ffn[:, WQ, c, m * HALF:(m + 1) * HALF], nselT[:, c, :],
                              start=(c == 0), stop=(c == 1))
            last.then_inc(pe["q3"], 1)
            te.wait_ge(mk["k3"], 2)
            for t in range(TILES):
                last = turn(bank(0)[0:ALL_PICKED, tokens(t)], picked[:, t, :], 128)
            last.then_inc(pe["pickT"], 1)
            project_v3(0)
            project_v3(1)

            def mix(t):
                te.wait_ge(mk["v3"], t + 1)
                te.wait_ge(mk["mixer"], t + 1)
                for c in range(2):
                    last = mm(bank(4 + t)[0:HALF, c * TILE:(c + 1) * TILE], n3[:, t, c * HALF:(c + 1) * HALF],
                              mixer[:, t, :], start=True, stop=True)
                last.then_inc(pe["mixT"], 1)

            te.wait_ge(mk["q3h"], 2)
            for n in range(IMAGES):
                t, i = n % TILES, n // TILES
                for c in range(2):
                    last = mm(bank(3)[64 * c:64 * c + 64, image(t, i)], q3h[:, c, n, :],
                              k3[:, c, image(t, i)], start=True, stop=True)
            last.then_inc(pe["scores3"], 1)
            project_v3(2)
            project_v3(3)
            for t in range(TILES):
                mix(t)

            def project_mix(t):
                te.wait_ge(mk["mixT"], t + 1)
                for c in range(2):
                    last = mm(bank(4 + t)[:, 0:DIM], mixT[:, c, tokens(t)], w_ffn[:, WM, c, :],
                              start=(c == 0), stop=(c == 1))
                last.then_inc(pe["mix"], 1)

            for g in range(2):
                te.wait_ge(mk["p3"], g + 1)
                for t in (2 * g, 2 * g + 1):
                    last = turn(bank(PT3_BANK[g])[:, (t % 2) * TILE:(t % 2 + 1) * TILE],
                                p3[:, 2 * t:2 * t + 2, :].rearrange("p i j -> p (i j)"), 128)
                last.then_inc(pe["pT3"], 1)
                project_mix(g)
            te.wait_ge(mk["pickT"], 1)
            for g in range(2):
                te.wait_ge(mk["pT3"], g + 1)
                for t in (2 * g, 2 * g + 1):
                    for c in range(2):
                        for i in range(PER_TILE):
                            ii = slice(64 * i, 64 * i + 64)
                            at = (2 * c + t % 2) * HEAD_ROWS
                            last = mm(bank(O3_BANK[g][i])[0:HALF, at:at + CHUNK_HEADS * PICKED],
                                      v3[ii, t, c * HALF:(c + 1) * HALF],
                                      pT3[ii, t, HEAD_ROWS * c:HEAD_ROWS * c + CHUNK_HEADS * PICKED],
                                      start=True, stop=True)
                last.then_inc(pe["o3"], 1)
                project_mix(2 + g)
            te.wait_ge(mk["o3T"], 2)
            keep_warm(3, 3)
            te.wait_ge(mk["o3T"], 4)
            for c in range(2):
                last = mm(bank(3)[0:ALL_PICKED, 0:DIM], o3T[:, c].rearrange("p i t q -> p (i t q)"),
                          w_ffn[:, WO, c, :], start=(c == 0), stop=(c == 1))
            last.then_inc(pe["a3"], 1)
            te.wait_ge(mk["a3"], 1)
            for t in range(TILES):
                te.wait_ge(mk["mixz"], t + 1)
                mm(bank(4 + t)[:, 0:DIM], pickedT[:, tokens(t)], a3[:, :], start=True, stop=True).then_inc(pe["spread"], 1)
            te.wait_ge(mk["W1_parts"], 1)
            te.wait_ge(ld["W2"], 16)
            keep_warm(4, 3)
            turn_half(0, 8, pe["x4T"])
            te.wait_ge(mk["h4"], 4)
            keep_warm(6, 7)
            for half in range(2):
                te.wait_ge(mk["h5T_parts"], 2 * half + 2)
                up(half, W1_parts, h5T_parts, pe["W1"], mk["gelu3"], AHEAD3, 8, pe["x4T"])
            for t in range(TILES):
                te.wait_ge(mk["gelu3"], MLP_CHUNKS * (t // 2 + 1))
                down(t, W2, ff3, pe["W2"])

        @block.gpsimd
        def _(pool):
            steps = [0]

            def step(ins):
                steps[0] += 1
                ins.then_inc(pool_step, 1)
                pool.wait_ge(pool_step, steps[0])

            def inverse_deviation(group):
                tt = GROUPS[group]
                pool.wait_ge(mk["var"], group + 1)
                nc.gpsimd.tensor_tensor(rstd[:, tt[0]:tt[-1] + 1], var_eps[:, tt[0]:tt[-1] + 1],
                                        power[:, 0:len(tt)], ALU.pow).then_inc(mk["rstd"], 1)

            nc.gpsimd.memset(w_proj[:], 0.0).then_inc(mk["zero"], 1)
            nc.gpsimd.memset(wmax[:], 0.0).then_inc(mk["zero"], 1)
            nc.gpsimd.memset(qmax[:], 0.0).then_inc(mk["zero"], 1)
            nc.gpsimd.memset(round_bias[:], ROUND).then_inc(mk["zero"], 1)
            step(nc.gpsimd.memset(power[:], -0.5))
            pool.wait_ge(ld["ident"], 16)
            nc.gpsimd.tensor_copy(ident_b[:], ident[:]).then_inc(mk["identb"], 1)
            for t in range(TILES):
                inverse_deviation(LN1 + t)
            pool.wait_ge(ld["rows_tok"], 16)
            for t in range(TILES):
                nc.gpsimd.tensor_tensor(t1b[:, t], t1[:, t], row("b_out"), ALU.add).then_inc(mk["t1b"], 1)
            pool.wait_ge(mk["wscale"], 1)
            step(nc.gpsimd.tensor_scalar(wqkv_r[:], w_qkv2[:], winv[0:HALF, 0:1], ROUND, ALU.mult, ALU.add))
            nc.gpsimd.tensor_scalar(wqkv_q[:], wqkv_r[:], -ROUND, None, ALU.add).then_inc(mk["wq"], 1)
            step(nc.gpsimd.tensor_scalar(wproj_r[:], w_proj[:], winv[:, 1:2], ROUND, ALU.mult, ALU.add))
            nc.gpsimd.tensor_scalar(wproj_q[:], wproj_r[:], -ROUND, None, ALU.add).then_inc(mk["wq"], 1)
            pool.wait_ge(ld["rows"], 32)
            for g in range(2):
                inverse_deviation(LN2 + g)
                for t in (2 * g, 2 * g + 1):
                    nc.gpsimd.tensor_tensor(t2b[:, t], t2[:, t], row("b_ff2"), ALU.add).then_inc(mk["t2b"], 1)
            for t in range(TILES):
                pool.wait_ge(mk["h1"], t + 1)
                nc.gpsimd.tensor_tensor(h1b[:, t], h1[:, t], row("b_proj"), ALU.add).then_inc(mk["h1b"], 1)
            step(nc.gpsimd.memset(v_q[:], 0.0))
            step(nc.gpsimd.memset(q3h[:], 0.0))
            pool.wait_ge(mk["scale"], 3)
            step(nc.gpsimd.tensor_scalar(v_r[:], v2[:], qinv[:, 2:3], ROUND, ALU.mult, ALU.add))
            nc.gpsimd.tensor_scalar(v_q[:, :, :, 0:HEAD], v_r[:].rearrange("p t (h d) -> p t h d", d=HEAD), -ROUND, None,
                                    ALU.add).then_inc(mk["vq"], 1)
            pool.wait_ge(mk["max2"], 1)
            e = e2[:, COPIED].rearrange("p h i j -> p (h i) j")
            nc.gpsimd.tensor_tensor(e, e, mx2[:, COPIED].unsqueeze(2).to_broadcast([128, HEADS, TOKENS]),
                                    ALU.subtract).then_inc(mk["pool_sub2"], 1)
            for t in range(TILES - 1):
                pool.wait_ge(mk["exp2"], t + 1)
                e = e2[:, t].rearrange("p h i j -> p (h i) j")
                nc.gpsimd.tensor_tensor(folded[:, t], e[:, :, 0:TOKENS // 2], e[:, :, TOKENS // 2:TOKENS],
                                        ALU.add).then_inc(mk["folded"], 1)
            pool.wait_ge(mk["f2"], 1)
            nc.gpsimd.tensor_tensor(p2[:, TILES - 1].rearrange("p h (i j) -> p (h i) j", j=TOKENS),
                                    e2[:, TILES - 1].rearrange("p h i j -> p (h i) j"),
                                    f2[:, TILES - 1].unsqueeze(2).to_broadcast([128, HEADS, TOKENS]),
                                    ALU.mult).then_inc(mk["p2_last"], 1)
            for g in range(2):
                pool.wait_ge(mk["var"], LNZ + g + 1)
                nc.gpsimd.tensor_tensor(rstd_n[:, 2 * g:2 * g + 2], var_n[:, 2 * g:2 * g + 2], power[:, 0:2],
                                        ALU.pow).then_inc(mk["rstd_n"], 1)
                inverse_deviation(LNZ + g)
            for t in range(TILES):
                pool.wait_ge(mk["nh"], t + 1)
                step(nc.gpsimd.tensor_tensor(ng[:, t], nh[:, t], row("g1"), ALU.mult))
                nc.gpsimd.tensor_tensor(n3[:, t], ng[:, t], row("b1"), ALU.add).then_inc(mk["n3"], 1)
            for t in range(TILES):
                pool.wait_ge(mk["z"], t + 1)
                nc.gpsimd.tensor_tensor(zb[:, t], z[:, t], row("bf2"), ALU.add).then_inc(mk["zb"], 1)
            for g in range(2):
                inverse_deviation(LN4 + g)
                for t in (2 * g, 2 * g + 1):
                    pool.wait_ge(mk["zb"], t + 1)
                    nc.gpsimd.tensor_tensor(h4z[:, t], h4[:, t], zb[:, t], ALU.add).then_inc(mk["h4z"], 1)
            for t in range(TILES):
                inverse_deviation(LNY + t)

        @block.scalar
        def _(act):
            act.dma_start(rows[:, 0:1], A["rows"][0:1].rearrange("(a r) n -> a r n", a=1)
                          .to_broadcast([128, 1, DIM])).then_inc(ld["row0"], 16)
            act.dma_start(cols[:], A["cols"]).then_inc(ld["cols"], 16)

            def from_chunks(t, where, dst, scale, bias, done):
                for c in range(2):
                    last = nc.scalar.activation(dst[:, c, tokens(t)], split_chunks(bank(where))[:, c, :], ACT.Identity,
                                                scale=col(scale, c), bias=col(bias, c))
                last.then_inc(done, 1)

            def keep_h(t):
                act.wait_ge(pe["xhatT"], t + 1)
                from_chunks(t, 4 + t, hT, "g1", "beta1", mk["hT"])

            act.wait_ge(mk["zeros"], 1)
            nc.scalar.activation(one[:], zeros[:, 0:1], ACT.Exp)
            act.wait_ge(ld["cols"], 16)
            keep_h(0)
            keep_h(1)

            def exp1(t):
                act.wait_ge(mk["sub"], t + 1)
                nc.scalar.activation(p1[:, t], p1[:, t], ACT.Exp, scale=HEAD1 ** -0.5).then_inc(mk["exp"], 1)

            def keep_qk(half):
                for m in range(2 * INNER_CHUNKS):
                    n = half * 2 * INNER_CHUNKS + m
                    if n == INNER_CHUNKS:
                        keep_h(2)
                        keep_h(3)
                    if n == 2 * INNER_CHUNKS + 3:
                        exp1(1)
                    act.wait_ge(pe["qk"], n + 1)
                    nc.scalar.activation(qkT[:, m, half * 256:(half + 1) * 256], bank(n % 4)[:, 0:256],
                                         ACT.Copy).then_inc(mk["qk"], 1)

            def keep_pT(t):
                act.wait_ge(pe["pT"], t + 1)
                nc.scalar.activation(pT1[:, t].rearrange("p r m n -> p r (m n)"), pairs[t % 2][:, :, 0:384],
                                     ACT.Copy).then_inc(mk["pT"], 1)

            def keep_o(t):
                act.wait_ge(pe["o"], t + 1)
                nc.scalar.activation(oT1[:, :, t].rearrange("p c i n -> p i c n"),
                                     pairs[t % 2][:, :, 0:384].rearrange("p i (c n) -> p i c n", n=TOKENS),
                                     ACT.Copy).then_inc(mk["oT"], 1)

            keep_qk(0)
            exp1(0)
            keep_qk(1)
            keep_pT(0)
            exp1(2)
            keep_pT(1)
            exp1(3)
            keep_o(0)
            keep_o(1)
            keep_pT(2)
            keep_pT(3)
            keep_o(2)
            keep_o(3)

            def keep_half(half, turned, dst, scale, bias, done):
                for t in (2 * half, 2 * half + 1):
                    act.wait_ge(turned, t + 1)
                    from_chunks(t, t, dst, scale, bias, done)

            def gelus(half, src, dst, which, done, ahead, *second_half):
                for m in range(MLP_CHUNKS):
                    n = half * MLP_CHUNKS + m
                    if half == 0 and m == ahead:
                        keep_half(1, *second_half)
                    act.wait_ge(src, n + 1)
                    nc.scalar.activation(dst[:, m, half * 256:(half + 1) * 256], bank(4 + n % 4)[:, 0:256], ACT.Gelu,
                                         bias=cols_ff[:, which, m:m + 1]).then_inc(done, 1)

            act.wait_ge(ld["cols_ff"], 16)
            turned = (pe["x2T"], h2T, "g2", "beta2", mk["h2T"])
            keep_half(0, *turned)
            for half in range(2):
                gelus(half, pe["ff1"], ff, 0, mk["gelu"], AHEAD1, *turned)

            for t in range(TILES):
                act.wait_ge(pe["hT"], t + 1)
                nc.scalar.activation(hq[:, :, tokens(t)], split_chunks(bank(t)), ACT.Copy,
                                     bias=-ROUND).then_inc(mk["hq"], 1)
            act.wait_ge(mk["scale"], 2)
            for m in range(4):
                act.wait_ge(pe["qk2"], m + 1)
                nc.scalar.activation(qk2[:, m, :], bank(4 + m)[0:HALF, :], ACT.Identity, scale=hs[0:HALF, 2:3],
                                     bias=col("bq2" if m < 2 else "bk2", m % 2)).then_inc(mk["qk2"], 1)
            act.wait_ge(mk["scale"], 3)
            nc.scalar.activation(qk_r[:, 0:2], qk2[:, 0:2], ACT.Identity, scale=qinv[0:HALF, 0:1],
                                 bias=round_bias[0:HALF, 0:1]).then_inc(mk["qkr"], 1)
            act.wait_ge(mk["kq"], 1)
            for h in range(4, CHUNK_HEADS):
                nc.scalar.activation(k_heads[:, h], k_q[:], ACT.Copy, scale=head_mask[:, h:h + 1]).then_inc(mk["ka"], 1)
            act.wait_ge(pe["scores2"], COPIED + 1)
            nc.scalar.activation(e2[:, COPIED].rearrange("p h i j -> p i h j"),
                                 pairs[COPIED][:, :, 0:384].rearrange("p i (h j) -> p i h j", j=TOKENS),
                                 ACT.Copy).then_inc(mk["copied2"], 1)
            for t in range(TILES):
                if t == COPIED:
                    act.wait_ge(mk["pool_sub2"], 1)
                else:
                    act.wait_ge(mk["sub2"], t + 1 if t < COPIED else t)
                nc.scalar.activation(e2[:, t], e2[:, t], ACT.Exp, scale=slog[:, 0:1]).then_inc(mk["exp2"], 1)
            for t in range(TILES):
                act.wait_ge(pe["pT2"], t + 1)
                nc.scalar.activation(pT2[:, t].rearrange("p h n -> p (h n)"), bank(t).bitcast(bf16)[:, 0:768],
                                     ACT.Copy).then_inc(mk["pT2"], 1)
            act.wait_ge(mk["scale"], 4)
            for g in range(2):
                nc.scalar.activation(o_r[:, :, 2 * g:2 * g + 2, 1, :].rearrange("p c t n -> p t c n"),
                                     pairs[3][:, g, 0:384].rearrange("p (t c n) -> p t c n", t=2, c=3),
                                     ACT.Identity, scale=os_[:, 4:5], bias=round_bias[:, 0:1]).then_inc(mk["or"], 1)

            for t in range(TILES):
                if t == 2:
                    act.wait_ge(mk["router"], 2)
                    act.wait_ge(mk["logit"], TILES)
                    nc.scalar.activation(eneg[:], logit[:], ACT.Exp, scale=-1.0,
                                         bias=router_bias[:]).then_inc(mk["eneg"], 1)
                act.wait_ge(pe["nT"], t + 1)
                from_chunks(t, NT_BANK[t], nT, "ffn_g1", "ffn_b1", mk["nT"])

            def keep_k3(m):
                act.wait_ge(pe["k3"], m + 1)
                nc.scalar.activation(k3[:, m, :], bank(m)[0:HALF, :], ACT.Identity, bias=col("bk3", m)).then_inc(mk["k3"], 1)

            keep_k3(0)
            act.wait_ge(pe["nsel"], 1)
            nc.scalar.activation(nselT[:].rearrange("p c n -> p (c n)"), bank(3)[0:HALF, 0:2 * ALL_PICKED],
                                 ACT.Copy).then_inc(mk["nselT"], 1)
            keep_k3(1)
            act.wait_ge(pe["q3"], 1)
            for c in range(2):
                nc.scalar.activation(q3[:, c].rearrange("p n q -> p (n q)"),
                                     bank(3)[0:HALF, c * ALL_PICKED:(c + 1) * ALL_PICKED], ACT.Identity,
                                     bias=col("bq3", c)).then_inc(mk["q3"], 1)
            act.wait_ge(pe["pickT"], 1)
            nc.scalar.activation(pickedT[:], bank(0)[0:ALL_PICKED, :], ACT.Copy).then_inc(mk["pickT"], 1)
            for g in range(2):
                act.wait_ge(mk["sub3"], g + 1)
                nc.scalar.activation(p3[:, 4 * g:4 * g + 4], p3[:, 4 * g:4 * g + 4], ACT.Exp,
                                     scale=HEAD ** -0.5).then_inc(mk["exp3"], 1)
            for t in range(TILES):
                act.wait_ge(pe["mixT"], t + 1)
                nc.scalar.activation(mixT[:, :, tokens(t)], split_chunks(bank(4 + t)), ACT.Copy).then_inc(mk["mixT"], 1)
            for g in range(2):
                act.wait_ge(pe["pT3"], g + 1)
                nc.scalar.activation(pT3[:, 2 * g:2 * g + 2].rearrange("p t n -> p (t n)"),
                                     bank(PT3_BANK[g])[:, 0:2 * TILE], ACT.Copy).then_inc(mk["pT3"], 1)
            turned = (pe["x4T"], h5T, "ffn_g2", "ffn_b2", mk["h5T"])
            keep_half(0, *turned)
            for half in range(2):
                gelus(half, pe["W1"], ff3, 1, mk["gelu3"], AHEAD3, *turned)

        @block.vector
        def _(dve):
            v = nc.vector
            steps = [0]

            def step(ins):
                steps[0] += 1
                ins.then_inc(dve_step, 1)
                dve.wait_ge(dve_step, steps[0])

            def wide(ap, n):
                return ap.unsqueeze(len(ap.shape)).to_broadcast(list(ap.shape) + [n])

            def statistics(group, src):
                tt = GROUPS[group]
                for t in tt:
                    last = v.bn_stats(stats[:, t], src[:, t])
                step(last)
                for t in tt:
                    last = v.bn_aggr(mv[:, t], stats[:, t])
                step(last)
                g = slice(tt[0], tt[-1] + 1)
                return v.tensor_scalar(var_eps[:, g], mv[:, g, 1], EPS, None, ALU.add)

            def centre(t, src, dst, factor):
                return v.tensor_scalar(dst[:, t], src[:, t], mv[:, t, 0:1], factor[:, t:t + 1], ALU.subtract, ALU.mult)

            def layernorm(group, src, dst, done):
                statistics(group, src).then_inc(mk["var"], 1)
                dve.wait_ge(mk["rstd"], group + 1)
                for t in GROUPS[group]:
                    centre(t, src, dst, rstd).then_inc(done, 1)

            def global_max(nth, maxima, dst, where):
                width = MAX_WIDTH[nth]
                if nth > 0:
                    dve.wait_ge(pe["wide"], nth)
                v.tensor_copy(spread[:, 0:width, :], wide(maxima, 128)).then_inc(mk["spread"], 1)
                dve.wait_ge(pe["wide"], nth + 1)
                step(v.tensor_reduce(dst, bank(where)[:, 0:width * 128].rearrange("p (k n) -> p k n", k=width), X, ALU.max))

            def scale_of(dst, maxima):
                return v.tensor_scalar(dst, maxima, 1.0 / QMAX, 1e-8, ALU.mult, ALU.max)

            v.memset(zeros[:], 0.0).then_inc(mk["zeros"], 1)
            dve.wait_ge(ld["row0"], 16)
            for t in range(TILES):
                dve.wait_ge(pe["patch"], t + 1)
                v.tensor_tensor(t1[:, t], bank(t)[:, 0:DIM], row("b_patch"), ALU.add).then_inc(mk["t1"], 1)
                dve.wait_ge(mk["t1"], t + 1)
                layernorm(LN1 + t, t1, xhat, mk["xhat"])

            def split(whole, parts, done):
                step(v.tensor_copy(parts[0], whole))
                v.tensor_tensor(parts[1], whole, parts[0].bitcast(f32), ALU.subtract).then_inc(done, 1)

            def split_h(half):
                hh = slice(half * 256, (half + 1) * 256)
                dve.wait_ge(mk["hT"], 2 * half + 2)
                split(hT[:, :, hh], [h[:, :, hh] for h in hT_parts], mk["h_parts"])

            def split_w(start, end):
                part = slice(start, end)
                split(w_qkv[:, :, part], [w[:, :, part] for w in w_qkv_parts], mk["w_parts"])

            split_h(0)
            dve.wait_ge(ld["w_k"], 16)
            split_w(INNER, 3 * INNER // 2)
            split_w(3 * INNER // 2, 2 * INNER)
            dve.wait_ge(ld["w_v"], 16)
            split_w(2 * INNER, 3 * INNER)
            split_h(1)
            dve.wait_ge(ld["w_q"], 16)
            split_w(0, INNER)
            def soft_scores(t):
                src = pairs[2 + t % 2][:, :, 0:384].rearrange("p r (s j) -> p r s j", j=TOKENS)
                m = mx1[:, t].rearrange("p (r s) -> p r s", r=2)
                dve.wait_ge(pe["scores"], t + 1)
                step(v.tensor_reduce(m, src, X, ALU.max))
                v.tensor_tensor(p1[:, t], src, wide(m, TOKENS), ALU.subtract).then_inc(mk["sub"], 1)

            def keep_v(t):
                dve.wait_ge(pe["v"], t + 1)
                v.tensor_copy(v1[:, t].rearrange("p (g n) -> p g n", g=2), pairs[V_PAIR[t]][:, :, 0:384]).then_inc(mk["v"], 1)

            def normalise(t):
                e = p1[:, t].rearrange("p r s j -> p (r s) j")
                dve.wait_ge(mk["exp"], t + 1)
                step(v.tensor_reduce(sum1[:, t], e, X, ALU.add))
                step(v.reciprocal(inv1[:, t], sum1[:, t]))
                v.tensor_tensor(e, e, wide(inv1[:, t], TOKENS), ALU.mult).then_inc(mk["p"], 1)

            keep_v(0)
            keep_v(1)
            soft_scores(0)
            soft_scores(1)
            normalise(0)
            normalise(1)
            dve.wait_ge(mk["zero"], 4)
            dve.wait_ge(ld["w_qkv2"], 16)
            dve.wait_ge(ld["w_proj"], 64)
            dve.wait_ge(ld["const"], 16)
            step(v.tensor_reduce(wmax[0:HALF, 0:1], w_qkv2[:].rearrange("p c n -> p (c n)"), X, ALU.max,
                                 apply_absolute_value=True))
            step(v.tensor_reduce(wmax[:, 1:2], w_proj[:].rearrange("p c n -> p (c n)"), X, ALU.max,
                                 apply_absolute_value=True))
            global_max(MAX_W, wmax[:], gm[:, 0:2], 4)
            step(scale_of(wscale[:], gm[:, 0:2]))
            v.reciprocal(winv[:], wscale[:]).then_inc(mk["wscale"], 1)
            keep_v(2)
            keep_v(3)
            soft_scores(2)
            soft_scores(3)
            normalise(2)
            normalise(3)

            dve.wait_ge(ld["w_ff1"], 16)
            split(w_ff1[:], [part[:] for part in w_ff1_parts], mk["w_ff1_parts"])

            def split_half(half, turned, whole, parts, done):
                for t in (2 * half, 2 * half + 1):
                    dve.wait_ge(turned, t + 1)
                    split(whole[:, :, tokens(t)], [part[:, :, tokens(t)] for part in parts], done)

            for g in range(2):
                if g == 1:
                    split_half(0, mk["h2T"], h2T, h2T_parts, mk["h2T_parts"])
                for t in (2 * g, 2 * g + 1):
                    dve.wait_ge(pe["out"], t + 1)
                    dve.wait_ge(mk["t1b"], t + 1)
                    v.tensor_tensor(t2[:, t], bank(OUT_BANK[t])[:, 0:DIM], t1b[:, t], ALU.add).then_inc(mk["t2"], 1)
                dve.wait_ge(mk["t2"], 2 * g + 2)
                layernorm(LN2 + g, t2, xhat, mk["xhat"])
            split_half(1, mk["h2T"], h2T, h2T_parts, mk["h2T_parts"])
            dve.wait_ge(ld["W1"], 16)
            split(W1[:], [part[:] for part in W1_parts], mk["W1_parts"])
            dve.wait_ge(ld["rows"], 32)
            v.tensor_tensor(router_g[:], row("g1"), row("Wr"), ALU.mult).then_inc(mk["router"], 1)
            step(v.scalar_tensor_tensor(out=weighed_b[:], in0=row("b1"), scalar=1.0, in1=row("Wr"),
                                        op0=ALU.mult, op1=ALU.mult, accum_out=router_c[:]))
            v.tensor_scalar(router_bias[:], router_c[:], br[:, 0:1], -1.0, ALU.add, ALU.mult).then_inc(mk["router"], 1)
            for t in range(TILES):
                dve.wait_ge(pe["ff2"], t + 1)
                dve.wait_ge(mk["t2b"], t + 1)
                v.tensor_tensor(h1[:, t], bank(t)[:, 0:DIM], t2b[:, t], ALU.add).then_inc(mk["h1"], 1)
                dve.wait_ge(mk["h1"], t + 1)
                last = v.tensor_reduce(hmax[:, t:t + 1], h1[:, t], X, ALU.max, apply_absolute_value=True)
            step(last)
            step(v.tensor_reduce(hmax[:, TILES:TILES + 1], hmax[:, 0:TILES], X, ALU.max))

            global_max(MAX_H, hmax[:, TILES:TILES + 1], gm[:, 0:1], 4)
            step(scale_of(hs[:, 0:1], gm[:, 0:1]))
            step(v.reciprocal(hs[:, 1:2], hs[:, 0:1]))
            for t in range(TILES):
                v.tensor_scalar(hr[:, t], h1[:, t], hs[:, 1:2], ROUND, ALU.mult, ALU.add).then_inc(mk["hr"], 1)
            v.tensor_tensor(hs[:, 2:3], hs[:, 0:1], wscale[:, 0:1], ALU.mult).then_inc(mk["scale"], 2)
            dve.wait_ge(mk["scale"], 2)
            for t in range(TILES):
                dve.wait_ge(pe["v2"], t + 1)
                v.scalar_tensor_tensor(out=v2[:, t], in0=bank(t)[:, 0:DIM], scalar=hs[:, 2:3], in1=row("bv2"),
                                       op0=ALU.mult, op1=ALU.add).then_inc(mk["v2"], 1)
            dve.wait_ge(mk["v2"], 4)
            v.tensor_reduce(qmax[:, 2:3], v2[:].rearrange("p t n -> p (t n)"), X, ALU.max, apply_absolute_value=True)
            for m in range(4):
                dve.wait_ge(mk["qk2"], m + 1)
                last = v.tensor_reduce(qmax_parts[0:HALF, m:m + 1], qk2[:, m, :], X, ALU.max, apply_absolute_value=True)
            step(last)
            step(v.tensor_reduce(qmax[0:HALF, 0:2], qmax_parts[0:HALF, :].rearrange("p (a b) -> p a b", a=2), X, ALU.max))
            global_max(MAX_QKV, qmax[:], gm[:, 0:3], 0)
            step(scale_of(qs[:], gm[:, 0:3]))
            v.reciprocal(qinv[:], qs[:]).then_inc(mk["scale"], 1)
            dve.wait_ge(mk["scale"], 3)
            step(v.tensor_scalar(qk_r[:, 2:4], qk2[:, 2:4], qinv[0:HALF, 1:2], ROUND, ALU.mult, ALU.add))
            v.tensor_scalar(k_q[:], qk_r[:, 2:4], -ROUND, None, ALU.add).then_inc(mk["kq"], 1)
            v.tensor_scalar(slog[:], qs[:, 0:1], qs[:, 1:2], HEAD ** -0.5, ALU.mult, ALU.mult)
            dve.wait_ge(mk["kq"], 1)
            for h in range(4):
                v.tensor_scalar(k_heads[:, h], k_q[:], head_mask[:, h:h + 1], None, ALU.mult).then_inc(mk["kd"], 1)
            dve.wait_ge(mk["qkr"], 1)
            v.tensor_scalar(q_q[:], qk_r[:, 0:2], -ROUND, None, ALU.add).then_inc(mk["qq"], 1)
            for t in range(TILES):
                if t == COPIED:
                    dve.wait_ge(mk["copied2"], 1)
                    v.tensor_reduce(mx2[:, t], e2[:, t].rearrange("p h i j -> p (h i) j"), X,
                                    ALU.max).then_inc(mk["max2"], 1)
                else:
                    src = pairs[t][:, :, 0:384].rearrange("p i (h j) -> p i h j", j=TOKENS)
                    m = mx2[:, t].rearrange("p (h i) -> p i h", i=2)
                    dve.wait_ge(pe["scores2"], t + 1)
                    step(v.tensor_reduce(m, src, X, ALU.max))
                    v.tensor_tensor(e2[:, t].rearrange("p h i j -> p i h j"), src, wide(m, TOKENS),
                                    ALU.subtract).then_inc(mk["sub2"], 1)
            for t in range(TILES - 1):
                dve.wait_ge(mk["folded"], t + 1)
                v.tensor_reduce(sum2[:, t], folded[:, t], X, ALU.add)
            dve.wait_ge(mk["exp2"], TILES)
            step(v.tensor_reduce(sum2[:, TILES - 1], e2[:, TILES - 1].rearrange("p h i j -> p (h i) j"), X, ALU.add))
            step(v.reciprocal(inv2[:], sum2[:]))
            step(v.tensor_reduce(pmax[:], inv2[:].rearrange("p t n -> p (t n)"), X, ALU.max))
            global_max(MAX_P, pmax[:], gm[:, 0:1], 0)
            step(scale_of(ps_[:, 0:1], gm[:, 0:1]))
            step(v.reciprocal(ps_[:, 1:2], ps_[:, 0:1]))
            v.tensor_scalar(f2[:], inv2[:], ps_[:, 1:2], None, ALU.mult).then_inc(mk["f2"], 1)
            dve.wait_ge(mk["f2"], 1)
            for t in range(TILES):
                if t < TILES - 1:
                    step(v.tensor_tensor(p2[:, t].rearrange("p h (i j) -> p (h i) j", j=TOKENS),
                                         e2[:, t].rearrange("p h i j -> p (h i) j"), wide(f2[:, t], TOKENS), ALU.mult))
                else:
                    dve.wait_ge(mk["p2_last"], 1)
                v.tensor_scalar(p2q[:, t], p2[:, t], ROUND, ROUND, ALU.add, ALU.subtract).then_inc(mk["p2"], 1)
            step(v.tensor_tensor(os_[:, 0:1], qs[:, 2:3], ps_[:, 0:1], ALU.mult))
            step(v.tensor_scalar(os_[:, 1:2], os_[:, 0:1], 1.0 / QMAX, None, ALU.mult))
            for g in range(2):
                for i in range(PER_TILE):
                    dve.wait_ge(pe["o2"], 2 * g + 2)
                    last = v.tensor_reduce(omax_parts[:, 2 * g + i:2 * g + i + 1], pairs[2 + i][:, g, 0:384],
                                           X, ALU.max, apply_absolute_value=True)
            step(last)
            step(v.tensor_reduce(omax[:], omax_parts[:], X, ALU.max))
            global_max(MAX_O, omax[:], gm[:, 0:1], 0)
            step(v.tensor_scalar(os_[:, 2:3], gm[:, 0:1], os_[:, 1:2], 1e-8, ALU.mult, ALU.max))
            step(v.reciprocal(os_[:, 3:4], os_[:, 2:3]))
            v.tensor_tensor(os_[:, 4:5], os_[:, 3:4], os_[:, 0:1], ALU.mult).then_inc(mk["scale"], 1)
            dve.wait_ge(mk["scale"], 4)
            for g in range(2):
                step(v.tensor_scalar(o_r[:, :, 2 * g:2 * g + 2, 0, :].rearrange("p c t n -> p t c n"),
                                     pairs[2][:, g, 0:384].rearrange("p (t c n) -> p t c n", t=2, c=3),
                                     os_[:, 4:5], ROUND, ALU.mult, ALU.add))
                dve.wait_ge(mk["or"], g + 1)
                v.tensor_scalar(o_q[:, :, 2 * g:2 * g + 2], o_r[:, :, 2 * g:2 * g + 2], -ROUND, None,
                                ALU.add).then_inc(mk["oq"], 1)
            step(v.tensor_tensor(hs[:, 2:3], os_[:, 2:3], wscale[:, 1:2], ALU.mult))
            for g in range(2):
                gg = slice(2 * g, 2 * g + 2)
                for t in (2 * g, 2 * g + 1):
                    dve.wait_ge(pe["proj"], t + 1)
                    dve.wait_ge(mk["h1b"], t + 1)
                    v.scalar_tensor_tensor(out=zpre[:, t], in0=bank(t)[:, 0:DIM], scalar=hs[:, 2:3], in1=h1b[:, t],
                                           op0=ALU.mult, op1=ALU.add).then_inc(mk["zpre"], 1)
                dve.wait_ge(mk["zpre"], 2 * g + 2)
                step(statistics(LNZ + g, zpre))
                v.scalar_tensor_tensor(out=var_n[:, gg], in0=var_eps[:, gg], scalar=EPS, in1=mv[:, gg, 1],
                                       op0=ALU.mult, op1=ALU.add).then_inc(mk["var"], 1)
            for g in range(2):
                dve.wait_ge(mk["rstd_n"], g + 1)
                for t in (2 * g, 2 * g + 1):
                    centre(t, zpre, nh, rstd_n).then_inc(mk["nh"], 1)
            dve.wait_ge(mk["router"], 2)
            for t in range(TILES):
                dve.wait_ge(mk["nh"], t + 1)
                v.scalar_tensor_tensor(out=weighed[:, t], in0=nh[:, t], scalar=1.0, in1=router_g[:],
                                       op0=ALU.mult, op1=ALU.mult, accum_out=logit[:, t:t + 1]).then_inc(mk["logit"], 1)
            dve.wait_ge(mk["rstd"], LNZ + 2)
            for t in range(2):
                centre(t, zpre, z, rstd).then_inc(mk["z"], 1)
            dve.wait_ge(mk["eneg"], 1)
            step(v.tensor_scalar(eneg1[:], eneg[:], 1.0, None, ALU.add))
            step(v.reciprocal(score[:], eneg1[:]))
            v.tensor_copy(score_b[:], wide(score[:], 128)).then_inc(mk["score_b"], 1)
            for t in range(2, TILES):
                centre(t, zpre, z, rstd).then_inc(mk["z"], 1)
            dve.wait_ge(pe["scoreT"], 1)
            for t in range(TILES):
                s = bank(2)[:, tokens(t)]
                v.scalar_tensor_tensor(out=below[:, t], in0=s, scalar=score[:, t:t + 1], in1=same,
                                       op0=ALU.is_lt, op1=ALU.mult, accum_out=less[:, t:t + 1])
                last = v.scalar_tensor_tensor(out=equal[:, t], in0=s, scalar=score[:, t:t + 1], in1=before,
                                              op0=ALU.is_equal, op1=ALU.mult, accum_out=tie[:, t:t + 1])
            step(last)
            step(v.tensor_tensor(rank[:], less[:], tie[:], ALU.add))
            for t in range(TILES):
                v.tensor_scalar(picked[:, t, :], pick_at[:, t, :], rank[:, t:t + 1], None,
                                ALU.is_equal).then_inc(mk["picked"], 1)

            def keep_v3(t):
                dve.wait_ge(pe["v3"], t + 1)
                v.tensor_tensor(v3[:, t], bank(4 + t)[:, 0:DIM], row("bv3"), ALU.add).then_inc(mk["v3"], 1)

            for t in range(TILES):
                last = v.scalar_tensor_tensor(out=sTm[:, t], in0=bank(2)[:, tokens(t)], scalar=1.0, in1=same,
                                              op0=ALU.mult, op1=ALU.mult, accum_out=total[:, t:t + 1])
            step(last)
            v.tensor_scalar(rest[:], rank[:], float(PICKED), None, ALU.is_ge)
            step(v.tensor_scalar(total_e[:], total[:], 1e-6, None, ALU.add))
            step(v.reciprocal(total_i[:], total_e[:]))
            step(v.tensor_tensor(weight[:], score[:], total_i[:], ALU.mult))
            for t in range(TILES):
                v.scalar_tensor_tensor(out=mixer[:, t], in0=sTm[:, t], scalar=weight[:, t:t + 1], in1=ident[:],
                                       op0=ALU.mult, op1=ALU.add).then_inc(mk["mixer"], 1)
            dve.wait_ge(mk["z"], 4)
            for t in range(TILES):
                v.scalar_tensor_tensor(out=zm[:, t], in0=row("bm"), scalar=rest[:, t:t + 1], in1=z[:, t],
                                       op0=ALU.mult, op1=ALU.add).then_inc(mk["zm"], 1)
            for c in range(2):
                dve.wait_ge(mk["q3"], c + 1)
                v.tensor_tensor(q3h[:, c, :, 0:CHUNK_HEADS * PICKED].rearrange("p n (h q) -> p n h q", q=PICKED),
                                q3[:, c].unsqueeze(2).to_broadcast([HALF, IMAGES, CHUNK_HEADS, PICKED]),
                                head_mask.unsqueeze(1).unsqueeze(3).to_broadcast([HALF, IMAGES, CHUNK_HEADS, PICKED]),
                                ALU.mult).then_inc(mk["q3h"], 1)
            keep_v3(0)
            keep_v3(1)
            dve.wait_ge(pe["scores3"], 1)
            src = bank(3).rearrange("p (n j) -> p n j", j=TOKENS)
            step(v.tensor_reduce(mx3[:], src, X, ALU.max))
            fours = (slice(0, IMAGES // 2), slice(IMAGES // 2, IMAGES))
            for n in fours:
                v.tensor_tensor(p3[:, n], src[:, n], wide(mx3[:, n], TOKENS), ALU.subtract).then_inc(mk["sub3"], 1)
            keep_v3(2)
            keep_v3(3)
            for g, n in enumerate(fours):
                dve.wait_ge(mk["exp3"], g + 1)
                step(v.tensor_reduce(sum3[:, n], p3[:, n], X, ALU.add))
                step(v.reciprocal(inv3[:, n], sum3[:, n]))
                v.tensor_tensor(p3[:, n], p3[:, n], wide(inv3[:, n], TOKENS), ALU.mult).then_inc(mk["p3"], 1)

            def keep_mix(t):
                dve.wait_ge(pe["mix"], t + 1)
                v.scalar_tensor_tensor(out=mixz[:, t], in0=bank(4 + t)[:, 0:DIM], scalar=rest[:, t:t + 1], in1=zm[:, t],
                                       op0=ALU.mult, op1=ALU.add).then_inc(mk["mixz"], 1)

            dve.wait_ge(mk["zm"], 4)
            for t in range(2):
                keep_mix(t)
            for g in range(2):
                dve.wait_ge(pe["o3"], g + 1)
                for i in range(PER_TILE):
                    src = bank(O3_BANK[g][i])[0:HALF, 0:4 * HEAD_ROWS].rearrange("p (a b) -> p a b", b=HEAD_ROWS)
                    src = src[:, :, 0:CHUNK_HEADS * PICKED].rearrange("p a (h q) -> p a h q", q=PICKED)
                    last = v.tensor_tensor(o3m[:, g, i].rearrange("p a (h q) -> p a h q", q=PICKED), src,
                                           head_mask.unsqueeze(1).unsqueeze(3).to_broadcast([HALF, 4, CHUNK_HEADS, PICKED]),
                                           ALU.mult)
                step(last)
                for i in range(PER_TILE):
                    v.tensor_reduce(o3T[:, :, i, 2 * g:2 * g + 2],
                                    o3m[:, g, i].rearrange("p (c t) (h q) -> p c t q h", c=2, q=PICKED),
                                    X, ALU.add).then_inc(mk["o3T"], 1)
            for t in range(2, TILES):
                keep_mix(t)
            dve.wait_ge(pe["a3"], 1)
            v.tensor_tensor(a3[:], bank(3)[0:ALL_PICKED, 0:DIM], row("bo")[0:ALL_PICKED, :], ALU.add).then_inc(mk["a3"], 1)
            for g in range(2):
                for t in (2 * g, 2 * g + 1):
                    dve.wait_ge(pe["spread"], t + 1)
                    v.tensor_tensor(h4[:, t], bank(4 + t)[:, 0:DIM], mixz[:, t], ALU.add).then_inc(mk["h4"], 1)
                dve.wait_ge(mk["h4"], 2 * g + 2)
                if g == 0:
                    layernorm(LN4, h4, xhat, mk["xhat"])
                else:
                    statistics(LN4 + 1, h4).then_inc(mk["var"], 1)
                    split_half(0, mk["h5T"], h5T, h5T_parts, mk["h5T_parts"])
                    dve.wait_ge(mk["rstd"], LN4 + 2)
                    for t in GROUPS[LN4 + 1]:
                        centre(t, h4, xhat, rstd).then_inc(mk["xhat"], 1)
            split_half(1, mk["h5T"], h5T, h5T_parts, mk["h5T_parts"])
            for t in range(TILES):
                dve.wait_ge(pe["W2"], t + 1)
                dve.wait_ge(mk["h4z"], t + 1)
                v.tensor_tensor(ypre[:, t], bank(t)[:, 0:DIM], h4z[:, t], ALU.add).then_inc(mk["ypre"], 1)
                dve.wait_ge(mk["ypre"], t + 1)
                layernorm(LNY + t, ypre, y, mk["y"])


def kernel(**inputs):
    import concourse.bacc as bacc
    from concourse.bass_utils import run_bass_kernel_spmd

    a = {k: np.asarray(x) for k, x in inputs.items()}
    tok = lambda n: a["L0_tok_" + n]
    att = lambda n: a["L0_attn_" + n]
    ffn = lambda n: a["L0_ffn_" + n]

    def chunks(w, rows):
        return w.reshape(-1, rows, w.shape[1]).transpose(1, 0, 2)

    def column(x, rows):
        return x.reshape(-1, rows).T

    x = a["x"].reshape(IMAGES, CHANNELS, GRID, PATCH, GRID, PATCH).transpose(3, 5, 1, 0, 2, 4)
    x = x.reshape(PATCH_CHUNKS, 128, TILES, TILE).transpose(1, 2, 0, 3)

    token = np.arange(128)
    mine = token[:, None] // TOKENS == token[None, :] // TOKENS
    pick = np.full((128, TILES, PER_TILE, TILES, PICKED), -1.0)
    for t in range(TILES):
        for i in range(PER_TILE):
            pick[i * TOKENS:(i + 1) * TOKENS, t, i, t, :] = np.arange(PICKED)
    head = np.zeros((128, CHUNK_HEADS))
    head[np.arange(HALF), np.arange(HALF) // HEAD] = 1.0
    table = {"same": mine, "before": mine & (token[None, :] < token[:, None]),
             "pick": pick.reshape(128, -1), "head": head}

    qkv_b, qkv_w = att("b_qkv"), att("w_qkv")
    arrays = {
        "xT": x,
        "w_patch": chunks(tok("w_patch"), 128),
        "w_qkv": chunks(tok("w_qkv"), HALF),
        "w_out": chunks(tok("w_out"), 128),
        "w_ff1": chunks(tok("w_ff1"), HALF),
        "w_ff2": chunks(tok("w_ff2"), 128),
        "w_qkv2": chunks(qkv_w, HALF),
        "w_proj": att("w_proj").reshape(3, 4, HEAD, DIM).transpose(1, 2, 0, 3),
        "w_ffn": np.stack([chunks(ffn(n), HALF) for n in ("Wq", "Wk", "Wv", "Wo", "Wm")], axis=1),
        "br": ffn("br").reshape(1, 1),
        "W1": chunks(ffn("W1"), HALF),
        "W2": chunks(ffn("W2"), 128),
        "rows": np.stack([tok("b_patch"), tok("b_out"), tok("b_ff2"), qkv_b[2 * DIM:], att("b_proj"), ffn("g1"),
                          ffn("b1"), ffn("bo"), ffn("bm"), ffn("bf2"), ffn("bv"), ffn("Wr")]),
        "cols": np.stack([column(v, HALF) for v in (tok("g1"), tok("beta1"), tok("g2"), tok("beta2"), qkv_b[:DIM],
                                                    qkv_b[DIM:2 * DIM], ffn("bq"), ffn("bk"), ffn("g1"), ffn("b1"), ffn("g2"),
                                                    ffn("b2"))], axis=1),
        "cols_ff": np.stack([column(tok("b_ff1"), 128), column(ffn("bf1"), 128)], axis=1),
        "ident": np.eye(128, dtype=np.float32),
        "consts": np.concatenate([table[n] for n in CONSTS], axis=1).astype(np.float32),
    }
    arrays = {k: np.ascontiguousarray(v) for k, v in arrays.items()}

    nc = bacc.Bacc("TRN2", target_bir_lowering=False, num_devices=1)
    f32 = mybir.dt.float32
    A = {k: nc.dram_tensor("in_" + k, v.shape, f32, kind="ExternalInput").ap() for k, v in arrays.items()}
    out = nc.dram_tensor("out", (ALL, DIM), f32, kind="ExternalOutput").ap()
    vit_kernel(nc, A, out)
    r = run_bass_kernel_spmd(nc, [{"in_" + k: v for k, v in arrays.items()}], core_ids=[0])
    return r.results[0]["out"].reshape(IMAGES, TOKENS, DIM)
```
